# Optimizing a Trainium2 kernel written in Bass

```python
import numpy as np
import jax
import jax.numpy as jnp

def _softmax(x, axis=-1):
    return jax.nn.softmax(x, axis=axis)

def _gelu(x):
    return jax.nn.gelu(x, approximate=True)

def _silu(x):
    return jax.nn.silu(x)

def _sigmoid(x):
    return jax.nn.sigmoid(x)

def _layernorm(x, axis=-1, eps=1e-05):
    m = jnp.mean(x, axis=axis, keepdims=True)
    v = jnp.var(x, axis=axis, keepdims=True)
    return (x - m) / jnp.sqrt(v + eps)

def _scatter_add(tgt, idx, src, axis=0):
    return tgt.at[idx].add(src)

def _segment_sum(src, seg, n):
    return jax.ops.segment_sum(src, seg, n)
kernel_name = 'mk_gnn_resnorm_d4_gnn_r64_650d6b'

def setup_inputs(seed: int=0):
    np.random.seed(seed)
    _w = jnp.asarray

    def _rec_inputs():
        import jax
        import jax.numpy as jnp
        _gk = jax.random.key(seed)
        x = -0.0007083 + 1.001 * jax.random.normal(jax.random.fold_in(_gk, 1), (100000, 48), jnp.float32)
        src = jax.random.randint(jax.random.fold_in(_gk, 2), (25000,), 0, 100000, jnp.int32)
        dst = jnp.minimum((100000 * jax.random.uniform(jax.random.fold_in(_gk, 3), (25000,)) ** 2.0).astype(jnp.int32), 99999)
        _o = jnp.argsort(dst, stable=True)
        src = src[_o]
        dst = dst[_o]
        edge_attr_40 = jax.random.uniform(jax.random.fold_in(_gk, 13), (25000, 40), jnp.float32, 0.0, 1)
        edge_type_8 = jax.random.randint(jax.random.fold_in(_gk, 15), (25000,), 0, 8, jnp.int32)
        edge_weight = jax.random.uniform(jax.random.fold_in(_gk, 16), (25000,), jnp.float32, 0.0, 6.99999)
        edge_weight1 = jax.random.uniform(jax.random.fold_in(_gk, 17), (25000, 1), jnp.float32, 0.0, 1)
        node_type_119 = jax.random.randint(jax.random.fold_in(_gk, 18), (100000,), 0, 119, jnp.int32)
        node_vec = jax.random.uniform(jax.random.fold_in(_gk, 19), (100000,), jnp.float32, 0.0, 1.49999)
        return (x, src, dst, edge_attr_40, edge_type_8, edge_weight, edge_weight1, node_type_119, node_vec)
    x, src, dst, edge_attr_40, edge_type_8, edge_weight, edge_weight1, node_type_119, node_vec = _rec_inputs()

    def _L0_gnn_setup():
        import jax, jax.numpy as jnp
        import numpy as np
        CUTOFF = 6.0
        LN_EPS = 1e-05
        key = jax.random.key(seed)
        ks = jax.random.split(key, 16)
        N, E, H, R, NEL, G = (50000, 12500, 48, 40, 119, 32)
        inp = {'h': jax.random.normal(ks[0], (N, H), jnp.float32), 'edge_index': jax.random.randint(ks[1], (2, E), 0, N, jnp.int64), 'edge_attr': jax.random.uniform(ks[2], (E, R), jnp.float32), 'distances': jax.random.uniform(ks[3], (E,), jnp.float32) * 7.0, 'atom_z': jax.random.randint(ks[4], (N,), 0, NEL, jnp.int64), 'node_mult': jax.random.uniform(ks[5], (N,), jnp.float32) + 0.5, 'batch': jnp.zeros((N,), jnp.int64), 'W1': jax.random.normal(ks[6], (H, R), jnp.float32) / np.sqrt(R), 'b1': jax.random.normal(ks[7], (H,), jnp.float32) * 0.01, 'W2': jax.random.normal(ks[8], (H, H), jnp.float32) / np.sqrt(H), 'b2': jax.random.normal(ks[9], (H,), jnp.float32) * 0.01, 'emb': jax.random.normal(ks[10], (NEL, G), jnp.float32) * 0.01, 'adaptW': jax.random.normal(ks[11], (G, G), jnp.float32) * 0.01, 'gamma': jnp.ones((H,), jnp.float32), 'beta': jnp.zeros((H,), jnp.float32)}
        return inp
    _L0_gnn_all = _L0_gnn_setup()
    _L0_gnn_in = {k: v for k, v in _L0_gnn_all.items() if k in ('W1', 'b1', 'W2', 'b2', 'emb', 'adaptW', 'gamma', 'beta')}
    del _L0_gnn_all

    def _L1_gnn_setup():
        import jax, jax.numpy as jnp
        import numpy as np
        import math
        K = 10
        A = 1.0
        B = 1.0
        ALPHA = 1.0

        def _An(n, a, b):
            nab = 2 * n + a + b
            return nab * (nab - 1) * (nab - 2) / (2 * n * (nab - n) * (nab - 2))

        def _Bn(n, a, b):
            nab = 2 * n + a + b
            return (nab - 1) * (a * a - b * b) / (2 * n * (nab - n) * (nab - 2))

        def _Cn(n, a, b):
            nab = 2 * n + a + b
            return -(2 * (n + a - 1) * (n + b - 1) * nab) / (2 * n * (nab - n) * (nab - 2))

        def _norm_weights(a, b):
            ws = []
            for i in range(K + 1):
                t1 = math.pow(2.0, a + b + 1) / (2 * i + a + b + 1)
                t2 = math.exp(math.lgamma(i + a + 1) - math.lgamma(i + a + b + 1))
                t3 = math.exp(math.lgamma(i + b + 1) - math.lgamma(i + 1))
                ws.append(math.sqrt(t1 * t2 * t3))
            return ws
        key = jax.random.key(seed)
        k1, k2 = jax.random.split(key)
        N, E, D = (100000, 25000, 48)
        x = jax.random.normal(k1, (N, D), dtype=jnp.float32)
        edge_index = jax.random.randint(k2, (2, E), 0, N, dtype=jnp.int64)
        lap_coefs = jnp.ones((K + 1,), dtype=jnp.float32)
        mf_weights = jnp.ones((1, K + 1, 1), dtype=jnp.float32)
        return {'x': x, 'edge_index': edge_index, 'lap_coefs': lap_coefs, 'mf_weights': mf_weights}
    _L1_gnn_all = _L1_gnn_setup()
    _L1_gnn_in = {k: v for k, v in _L1_gnn_all.items() if k in ('lap_coefs', 'mf_weights')}
    del _L1_gnn_all

    def _L2_gnn_setup():
        import jax, jax.numpy as jnp
        import numpy as np
        N_NODES = 50000
        N_EDGES = 25000
        D_IN = 48
        D_OUT = 48
        key = jax.random.key(seed)
        k1, k2, k3, k4 = jax.random.split(key, 4)
        features = jax.random.normal(k1, (N_NODES, D_IN), dtype=jnp.float32)
        src = jax.random.randint(k2, (N_EDGES,), 0, N_NODES, dtype=jnp.int64)
        dst = jax.random.randint(k3, (N_EDGES,), 0, N_NODES, dtype=jnp.int64)
        std = np.sqrt(2.0 / (D_IN + D_OUT))
        W = jax.random.normal(k4, (D_OUT, D_IN), dtype=jnp.float32) * std
        b = jnp.zeros((D_OUT,), dtype=jnp.float32)
        return {'features': features, 'src': src, 'dst': dst, 'W': W, 'b': b}
    _L2_gnn_all = _L2_gnn_setup()
    _L2_gnn_in = {k: v for k, v in _L2_gnn_all.items() if k in ('W', 'b')}
    del _L2_gnn_all

    def _L3_gnn_setup():
        import jax, jax.numpy as jnp
        import numpy as np
        N_NODES = 50000
        N_EDGES = 25000
        IN_FEAT = 48
        OUT_FEAT = 48
        NUM_RELS = 8
        key = jax.random.key(seed)
        ks = jax.random.split(key, 9)
        s1 = float(np.sqrt(2.0) * np.sqrt(6.0 / (IN_FEAT + IN_FEAT)))
        s2 = float(np.sqrt(2.0) * np.sqrt(6.0 / (IN_FEAT + OUT_FEAT)))
        return {'inputs': jax.random.normal(ks[0], (N_NODES, IN_FEAT), dtype=jnp.float32), 'norm': jax.random.uniform(ks[1], (N_EDGES, 1), dtype=jnp.float32), 'weight1': jax.random.uniform(ks[2], (NUM_RELS, IN_FEAT, IN_FEAT), jnp.float32, -s1, s1), 'weight2': jax.random.uniform(ks[3], (NUM_RELS, IN_FEAT, OUT_FEAT), jnp.float32, -s2, s2), 'bias1': jax.random.normal(ks[4], (IN_FEAT,), dtype=jnp.float32) * 0.1, 'bias2': jax.random.normal(ks[5], (OUT_FEAT,), dtype=jnp.float32) * 0.1, 'src': jax.random.randint(ks[6], (N_EDGES,), 0, N_NODES, dtype=jnp.int64) if jax.config.jax_enable_x64 else jax.random.randint(ks[6], (N_EDGES,), 0, N_NODES).astype(jnp.int32), 'dst': jax.random.randint(ks[7], (N_EDGES,), 0, N_NODES).astype(jnp.int32), 'rel_type': jax.random.randint(ks[8], (N_EDGES,), 0, NUM_RELS).astype(jnp.int32)}
    _L3_gnn_all = _L3_gnn_setup()
    _L3_gnn_in = {k: v for k, v in _L3_gnn_all.items() if k in ('weight1', 'weight2', 'bias1', 'bias2')}
    del _L3_gnn_all
    return {'x': x, 'src': src, 'dst': dst, 'edge_attr_40': edge_attr_40, 'edge_type_8': edge_type_8, 'edge_weight': edge_weight, 'edge_weight1': edge_weight1, 'node_type_119': node_type_119, 'node_vec': node_vec, 'L0_gnn_W1': _L0_gnn_in['W1'], 'L0_gnn_b1': _L0_gnn_in['b1'], 'L0_gnn_W2': _L0_gnn_in['W2'], 'L0_gnn_b2': _L0_gnn_in['b2'], 'L0_gnn_emb': _L0_gnn_in['emb'], 'L0_gnn_adaptW': _L0_gnn_in['adaptW'], 'L0_gnn_gamma': _L0_gnn_in['gamma'], 'L0_gnn_beta': _L0_gnn_in['beta'], 'L1_gnn_lap_coefs': _L1_gnn_in['lap_coefs'], 'L1_gnn_mf_weights': _L1_gnn_in['mf_weights'], 'L2_gnn_W': _L2_gnn_in['W'], 'L2_gnn_b': _L2_gnn_in['b'], 'L3_gnn_weight1': _L3_gnn_in['weight1'], 'L3_gnn_weight2': _L3_gnn_in['weight2'], 'L3_gnn_bias1': _L3_gnn_in['bias1'], 'L3_gnn_bias2': _L3_gnn_in['bias2']}

def reference(x, src, dst, edge_attr_40, edge_type_8, edge_weight, edge_weight1, node_type_119, node_vec, L0_gnn_W1, L0_gnn_b1, L0_gnn_W2, L0_gnn_b2, L0_gnn_emb, L0_gnn_adaptW, L0_gnn_gamma, L0_gnn_beta, L1_gnn_lap_coefs, L1_gnn_mf_weights, L2_gnn_W, L2_gnn_b, L3_gnn_weight1, L3_gnn_weight2, L3_gnn_bias1, L3_gnn_bias2):
    import jax
    import jax.numpy as jnp

    def _L0_gnn_ref(h, edge_index, edge_attr, distances, atom_z, node_mult, batch, W1, b1, W2, b2, emb, adaptW, gamma, beta):
        import jax, jax.numpy as jnp
        import numpy as np
        CUTOFF = 6.0
        LN_EPS = 1e-05
        src, dst = (edge_index[0], edge_index[1])
        N = h.shape[0]
        gate = jax.nn.silu(edge_attr @ W1.T + b1) @ W2.T + b2
        ei = emb[atom_z[src]]
        ej = emb[atom_z[dst]]
        adapt_logit = jnp.sum(ei * (ej @ adaptW.T), axis=-1, keepdims=True)
        gate = gate + adapt_logit
        cw = jnp.where(distances < CUTOFF, 0.5 * (jnp.cos(jnp.pi * distances / CUTOFF) + 1.0), 0.0)
        mj = node_mult[dst]
        msg = gate * h[dst] * (cw * mj)[:, None]
        agg = jax.ops.segment_sum(msg, src, num_segments=N)
        tot = jax.ops.segment_sum(mj, src, num_segments=N)
        agg = agg / jnp.clip(tot, 1e-08, None)[:, None]
        x = h + agg
        mu = jnp.mean(x, axis=-1, keepdims=True)
        var = jnp.mean(jnp.square(x - mu), axis=-1, keepdims=True)
        return (x - mu) / jnp.sqrt(var + LN_EPS) * gamma + beta

    def _L1_gnn_ref(x, edge_index, lap_coefs, mf_weights):
        import jax, jax.numpy as jnp
        import numpy as np
        import math
        K = 10
        A = 1.0
        B = 1.0
        ALPHA = 1.0

        def _An(n, a, b):
            nab = 2 * n + a + b
            return nab * (nab - 1) * (nab - 2) / (2 * n * (nab - n) * (nab - 2))

        def _Bn(n, a, b):
            nab = 2 * n + a + b
            return (nab - 1) * (a * a - b * b) / (2 * n * (nab - n) * (nab - 2))

        def _Cn(n, a, b):
            nab = 2 * n + a + b
            return -(2 * (n + a - 1) * (n + b - 1) * nab) / (2 * n * (nab - n) * (nab - 2))

        def _norm_weights(a, b):
            ws = []
            for i in range(K + 1):
                t1 = math.pow(2.0, a + b + 1) / (2 * i + a + b + 1)
                t2 = math.exp(math.lgamma(i + a + 1) - math.lgamma(i + a + b + 1))
                t3 = math.exp(math.lgamma(i + b + 1) - math.lgamma(i + 1))
                ws.append(math.sqrt(t1 * t2 * t3))
            return ws
        N = x.shape[0]
        src = edge_index[0]
        dst = edge_index[1]
        deg = jax.ops.segment_sum(jnp.ones(src.shape, dtype=x.dtype), dst, num_segments=N)
        dinv = jnp.where(deg > 0, jax.lax.rsqrt(jnp.where(deg > 0, deg, 1.0)), 0.0)
        enorm = dinv[src] * dinv[dst]

        def prop(h):
            return jax.ops.segment_sum(enorm[:, None] * h[src], dst, num_segments=N)
        nw = _norm_weights(A, B)
        c0 = (A - B) / 2.0
        c1 = (A + B + 2.0) / 2.0
        P0 = x
        P1 = c0 * x + c1 * prop(x)
        outs = [P0, P1]
        for n in range(2, K + 1):
            an, bn, cn = (_An(n, A, B), _Bn(n, A, B), _Cn(n, A, B))
            outs.append(bn * outs[-1] + cn * outs[-2] + an * prop(outs[-1]))
        lap = jnp.cumprod(ALPHA * jnp.tanh(lap_coefs))
        coef_outs = [outs[0] / nw[0]]
        for i in range(1, K + 1):
            coef_outs.append(lap[i - 1] / nw[i] * outs[i])
        stacked = jnp.stack(coef_outs, axis=1)
        return jnp.sum(stacked * mf_weights, axis=1)

    def _L2_gnn_ref(features, src, dst, W, b):
        import jax, jax.numpy as jnp
        import numpy as np
        N_NODES = 50000
        N_EDGES = 25000
        D_IN = 48
        D_OUT = 48
        n = features.shape[0]
        ones = jnp.ones(src.shape[0], dtype=features.dtype)
        out_deg = jax.ops.segment_sum(ones, src, num_segments=n)
        in_deg = jax.ops.segment_sum(ones, dst, num_segments=n)
        ci = jax.lax.rsqrt(jnp.maximum(out_deg, 1.0))
        cj = jax.lax.rsqrt(jnp.maximum(in_deg, 1.0))
        msg = features[src] * ci[src][:, None]
        agg = jax.ops.segment_sum(msg, dst, num_segments=n) * cj[:, None]
        h = jnp.where(in_deg[:, None] > 0, agg, features)
        out = jax.nn.relu(h @ W.T + b)
        return out

    def _L3_gnn_ref(inputs, norm, weight1, weight2, bias1, bias2, src, dst, rel_type):
        import jax, jax.numpy as jnp
        import numpy as np
        N_NODES = 50000
        N_EDGES = 25000
        IN_FEAT = 48
        OUT_FEAT = 48
        NUM_RELS = 8
        h1 = jax.nn.relu(jnp.einsum('ni,rij->nrj', inputs, weight1) + bias1)
        h2 = jnp.einsum('nrj,rjo->nro', h1, weight2)
        msg = h2[src, rel_type] * norm
        agg = jax.ops.segment_sum(msg, dst, num_segments=inputs.shape[0])
        return jax.nn.relu(agg + bias2)
    edge_index = jnp.stack([src, dst])
    batch0 = jnp.zeros((100000,), jnp.int32)
    x = _layernorm(x + _L0_gnn_ref(x, edge_index, edge_attr_40, edge_weight, node_type_119, node_vec, batch0, L0_gnn_W1, L0_gnn_b1, L0_gnn_W2, L0_gnn_b2, L0_gnn_emb, L0_gnn_adaptW, L0_gnn_gamma, L0_gnn_beta), axis=-1)
    x = _layernorm(x + _L1_gnn_ref(x, edge_index, L1_gnn_lap_coefs, L1_gnn_mf_weights), axis=-1)
    x = _layernorm(x + _L2_gnn_ref(x, src, dst, L2_gnn_W, L2_gnn_b), axis=-1)
    x = _layernorm(x + _L3_gnn_ref(x, edge_weight1, L3_gnn_weight1, L3_gnn_weight2, L3_gnn_bias1, L3_gnn_bias2, src, dst, edge_type_8), axis=-1)
    return x

_drawn_inputs = setup_inputs


def setup_inputs(seed=0):
    import zlib

    import numpy as np

    out = dict(_drawn_inputs(seed))
    spreads = {'L0_gnn_gamma': (1.0, 0.2),
     'L0_gnn_beta': (0.0, 0.1),
     'L1_gnn_lap_coefs': (1.0, 0.6),
     'L1_gnn_mf_weights': (1.0, 0.2),
     'L2_gnn_b': (0.0, 0.1)}
    factors = {'node_vec': 64.0,
     'L0_gnn_b1': 54.078,
     'L0_gnn_b2': 36.477,
     'L0_gnn_emb': 64.0,
     'L0_gnn_adaptW': 64.0,
     'L3_gnn_bias1': 3.804,
     'edge_attr_40': 4.26}
    for name, (base, spread) in spreads.items():
        noise = np.random.default_rng([zlib.crc32(name.encode()), seed]).standard_normal(out[name].shape)
        drawn = base * np.exp(spread * noise) if base else spread * noise
        out[name] = jnp.asarray(drawn.astype(out[name].dtype))
    for name, factor in factors.items():
        out[name] = (out[name] * factor).astype(out[name].dtype)
    return out
```

```python
from contextlib import ExitStack

import numpy as np

import concourse.bass as bass
from concourse import mybir
from concourse.alu_op_type import AluOpType as ALU

ACT = mybir.ActivationFunctionType
AX = mybir.AxisListType
F32 = mybir.dt.float32
I32 = mybir.dt.int32
I16 = mybir.dt.int16
BF16 = mybir.dt.bfloat16
RMAX = bass.bass_isa.ReduceOp.max

P = 128
N = 100000
E = 25000
D = 48
R = 40
NEL = 119
G = 32
NREL = 8
K = 10
CUTOFF = 6.0
EPS = 1e-5

LO = 1024
HI = -(-N // LO)
NP = HI * LO
NF = NP // P
T = 4 * (-(-E // (4 * P)))
EP = T * P
TB = 4
NB = T // TB
GE = 2 * P
SPARE_SRC, SPARE_DST = N, N + 1
SINK = N + 8
XW = D + 2
AW = D + 1
CH = 56
NC = NF // CH
PI = float(np.pi)
assert NP == P * NF and NF % (2 * CH) == 0 and SINK + GE <= NP
assert T % 7 == 0


def jacobi_basis():
    import math
    a = b = 1.0
    rows = np.zeros((K + 1, K + 1))
    rows[0, 0] = 1.0
    rows[1, 0], rows[1, 1] = (a - b) / 2.0, (a + b + 2.0) / 2.0
    for n in range(2, K + 1):
        nab = 2 * n + a + b
        an = nab * (nab - 1) * (nab - 2) / (2 * n * (nab - n) * (nab - 2))
        bn = (nab - 1) * (a * a - b * b) / (2 * n * (nab - n) * (nab - 2))
        cn = -(2 * (n + a - 1) * (n + b - 1) * nab) / (2 * n * (nab - n) * (nab - 2))
        rows[n] = bn * rows[n - 1] + cn * rows[n - 2]
        rows[n, 1:] += an * rows[n - 1, :-1]
    for i in range(K + 1):
        t1 = math.pow(2.0, a + b + 1) / (2 * i + a + b + 1)
        t2 = math.exp(math.lgamma(i + a + 1) - math.lgamma(i + a + b + 1))
        t3 = math.exp(math.lgamma(i + b + 1) - math.lgamma(i + 1))
        rows[i] /= math.sqrt(t1 * t2 * t3)
    return rows.astype(np.float32)


def program(nc, a, out):
    with ExitStack() as ctx:
        def sb(name, shape, dt=F32):
            return ctx.enter_context(nc.sbuf_tensor(name, shape, dt))

        def psum(name, shape, dt=F32):
            return ctx.enter_context(nc.psum_tensor(name, shape, dt))

        def sem(name):
            return ctx.enter_context(nc.semaphore(name))

        def table(name, rows, width):
            return nc.dram_tensor(name, [rows, width], F32, kind="Internal").ap()

        xz_t = a["xz"]
        srow_t = table("srow_t", NP, 4)
        indeg_t = table("indeg_t", NP, 1)
        agg0_t = table("agg0_t", NP, AW)
        pow_t = table("pow_t", 3 * NP, D)
        y_t = table("y_t", NP, D)
        agg2_t = table("agg2_t", NP, D)
        agg3_t = table("agg3_t", NP, D)
        x2_t = table("x2_t", NP, D)
        x3_t = table("x3_t", NP, D)
        edge_t = table("edge_t", EP + 1, 4)
        x1_t = pow_t[0:NP, :]

        ident = sb("ident", [P, P])
        iota_lo = sb("iota_lo", [P, LO], I16)
        earlier = sb("earlier", [P, 2, GE])
        zeros = sb("zeros", [P, 2048])
        sink = sb("sink", [P, TB])
        src_i = sb("src_i", [P, T + TB], I32)
        dst_i = sb("dst_i", [P, T + TB], I32)
        src_f = sb("src_f", [P, T])
        dst_f = sb("dst_f", [P, T])
        srows = sb("srows", [P, T, 4])
        dist = sb("dist", [P, T])
        cutw = sb("cutw", [P, T])
        norm = sb("norm", [P, T])
        w1t = sb("w1t", [R, D])
        b1c = sb("b1c", [D, 1])
        w2b = sb("w2b", [D + 1, D])
        embt = sb("embt", [G, NEL])
        adwt = sb("adwt", [G, G])
        vmat = sb("vmat", [G, NEL])
        kindm = sb("kindm", [NEL, NEL])
        gammab = sb("gammab", [P, D])
        betab = sb("betab", [P, D])
        halfpi = sb("halfpi", [P, 1])
        jac = sb("jac", [P, (K + 1) * (K + 1)])
        coef = sb("coef", [P, 6, K + 1])
        qk = sb("qk", [P, K + 2])
        wl2 = sb("wl2", [2 * D, 2 * D])
        bl2 = sb("bl2", [1, 10 * D])
        onesrow = sb("onesrow", [1, P])
        wr1 = sb("wr1", [D, NREL * D])
        br1 = sb("br1", [P, 3])
        wr2 = sb("wr2", [P, 3 * D])
        relc = sb("relc", [P, 3])
        b3b = sb("b3b", [P, D])

        s_ix = sem("indices_loaded")
        s_w = sem("weights_loaded")
        s_c = sem("constants_made")
        s_z = sem("zeros_made")
        s_agg0 = sem("agg0_cleared")
        s_pow = sem("power_tables_cleared")
        s_y = sem("filter_table_cleared")
        s_agg3 = sem("agg3_cleared")

        TBL_BYTES_COLS = 2048

        def clear(eng, tbl, done):
            total = tbl.shape[0] * tbl.shape[1]
            flat = tbl.rearrange("a b -> (a b)").rearrange("(p c) -> p c", p=P)
            cols = total // P
            n = 0
            for c0 in range(0, cols, TBL_BYTES_COLS):
                w = min(TBL_BYTES_COLS, cols - c0)
                eng.dma_start(flat[:, c0:c0 + w], zeros[:, 0:w]).then_inc(done, 16)
                n += 16
            return n

        def cleared(tbl):
            return 16 * (-(-(tbl.shape[0] * tbl.shape[1] // P) // TBL_BYTES_COLS))

        WEIGHTS = [(w1t, "w1t"), (b1c, "b1"), (w2b, "w2b"), (embt, "embt"), (adwt, "adwt"),
                   (gammab, "gamma"), (betab, "beta"), (jac, "jacobi"), (coef[:, 0, :], "lap"),
                   (coef[:, 1, :], "mf"), (wl2, "wl2"), (bl2, "bl2"), (wr1, "wr1"), (br1, "br1"),
                   (wr2, "wr2"), (relc, "relc"), (b3b, "b3"), (dist, "dist"), (norm, "norm")]
        BROADCAST = ("gamma", "beta", "jacobi", "lap", "mf", "b3")

        with ExitStack() as ph, nc.Block() as block:
            def tmp(name, shape, dt=F32):
                return ph.enter_context(nc.sbuf_tensor(name, shape, dt))

            digit = tmp("digit", [P, 4, T], I32)
            digit_f = tmp("digit_f", [P, 4, T])
            hot_hi = tmp("hot_hi", [P, TB, 2, HI], BF16)
            hot_lo = tmp("hot_lo", [P, TB, 2, LO], BF16)
            kind_i = tmp("kind_i", [HI, LO], I32)
            srow = tmp("srow", [HI, LO, 4])
            indeg = tmp("indeg", [HI, LO])
            outdeg = tmp("outdeg", [HI, LO])
            deg_p = ph.enter_context(nc.psum_tensor("deg_p", [P, 2, LO], F32))
            mat_p = ph.enter_context(nc.psum_tensor("mat_p", [P, 512], F32))
            mat2_p = ph.enter_context(nc.psum_tensor("mat2_p", [P, 512], F32))
            s_dig = sem("digits_chain")
            s_hot = sem("onehots_made")
            s_hotu = sem("onehots_used")
            s_degz = sem("degrees_started")
            s_m = sem("kind_matrix")
            s_mc = sem("kind_matrix_copied")
            s_srow = sem("source_rows_made")
            s_sq = sem("outdegree_root")
            s_coef = sem("coefficients")
            s_st = sem("source_rows_stored")
            s_cut = sem("cutoff_weights")

            @block.sync
            def _(sp):
                sp.dma_start(src_i[:, :], a["src"]).then_inc(s_ix, 16)
                sp.dma_start(dst_i[:, :], a["dst"]).then_inc(s_ix, 16)
                sp.dma_start(kind_i[:, :], a["kind"]).then_inc(s_ix, 16)
                for tile, name in WEIGHTS:
                    src = a[name].partition_broadcast(P) if name in BROADCAST else a[name]
                    dst = tile if isinstance(tile, bass.AP) else tile[:, :]
                    sp.dma_start(dst, src).then_inc(s_w, 16)
                sp.wait_ge(s_z, 1)
                clear(sp, agg0_t, s_agg0)
                sp.wait_ge(s_srow, 2)
                sp.dma_start(srow_t.rearrange("(h l) c -> h (l c)", h=HI),
                             srow[:, :, :].rearrange("h l c -> h (l c)")).then_inc(s_st, 16)
                sp.dma_start(indeg_t.rearrange("(h l) c -> h (l c)", h=HI), indeg[:, :]).then_inc(s_st, 16)
                sp.wait_ge(s_st, 32)

            @block.gpsimd
            def _(pool):
                pool.iota(iota_lo[:, :], pattern=[[1, LO]], base=0, channel_multiplier=0).then_inc(s_c, 1)
                pool.memset(ident[:, :], 0.0).then_inc(s_c, 1)
                pool.memset(earlier[:, :, :], 1.0).then_inc(s_c, 1)
                pool.iota(sink[:, :], pattern=[[0, TB // 2], [P, 2]], base=SINK, channel_multiplier=1,
                          allow_small_or_imprecise_dtypes=True).then_inc(s_c, 1)
                pool.wait_ge(s_c, 4)
                pool.affine_select(out=ident[:, :], in_=ident[:, :], compare_op=ALU.not_equal, fill=1.0,
                                   base=0, pattern=[[-1, P]], channel_multiplier=1).then_inc(s_c, 1)
                for u in range(2):
                    pool.affine_select(out=earlier[:, u, :], in_=earlier[:, u, :], compare_op=ALU.is_gt,
                                       fill=0.0, base=u * P, pattern=[[-1, GE]],
                                       channel_multiplier=1).then_inc(s_c, 1)

            @block.vector
            def _(dve):
                n = [0]

                def link(ins):
                    n[0] += 1
                    ins.then_inc(s_dig, 1)
                    dve.wait_ge(s_dig, n[0])

                dve.memset(zeros[:, :], 0.0).then_inc(s_z, 1)
                dve.memset(onesrow[:, :], 1.0).then_inc(s_z, 1)
                dve.memset(halfpi[:, :], PI / 2).then_inc(s_z, 1)
                dve.wait_ge(s_ix, 48)
                for j, ids in ((0, src_i), (2, dst_i)):
                    link(dve.tensor_scalar(digit[:, j, :], ids[:, 0:T], 10, None, ALU.logical_shift_right))
                    link(dve.tensor_scalar(digit[:, j + 1, :], ids[:, 0:T], LO - 1, None, ALU.bitwise_and))
                link(dve.tensor_copy(digit_f[:, :, :], digit[:, :, :]))
                link(dve.tensor_copy(src_f[:, :], src_i[:, 0:T]))
                link(dve.tensor_copy(dst_f[:, :], dst_i[:, 0:T]))
                dve.wait_ge(s_c, 7)
                with dve.Fori(0, NB) as i:
                    for u in range(TB):
                        for j in range(2):
                            if j == 0:
                                dve.wait_ge(s_hotu, i * TB + u)
                            dve.tensor_scalar(hot_hi[:, u, j, :], iota_lo[:, 0:HI],
                                              digit_f[:, 2 * j, bass.ds(i * TB + u, 1)], None, ALU.is_equal)
                            ins = dve.tensor_scalar(hot_lo[:, u, j, :], iota_lo[:, :],
                                                    digit_f[:, 2 * j + 1, bass.ds(i * TB + u, 1)], None,
                                                    ALU.is_equal)
                        ins.then_inc(s_hot, 1)
                dve.wait_ge(s_w, 16 * len(WEIGHTS))
                link(dve.tensor_scalar(cutw[:, :], dist[:, :], CUTOFF, None, ALU.min))
                dve.sem_inc(s_cut, 1)
                dve.wait_ge(s_cut, 2)
                link(dve.tensor_scalar(cutw[:, :], cutw[:, :], 1.0, 0.5, ALU.add, ALU.mult))
                link(dve.tensor_scalar(dist[:, :], dist[:, :], CUTOFF, None, ALU.is_lt))
                link(dve.tensor_tensor(cutw[:, :], cutw[:, :], dist[:, :], ALU.mult))
                dve.wait_ge(s_m, 1)
                dve.tensor_copy(vmat[:, :], mat_p[0:G, 0:NEL]).then_inc(s_mc, 1)
                dve.wait_ge(s_m, 2)
                link(dve.tensor_copy(kindm[:, :], mat2_p[0:NEL, 0:NEL]))
                dve.wait_ge(s_coef, 1)
                link(dve.tensor_copy(coef[:, 3, 0:1], coef[:, 2, 0:1]))
                for i in range(1, K):
                    link(dve.tensor_tensor(coef[:, 3, i:i + 1], coef[:, 3, i - 1:i], coef[:, 2, i:i + 1],
                                           ALU.mult))
                link(dve.tensor_copy(coef[:, 4, 0:1], coef[:, 1, 0:1]))
                link(dve.tensor_tensor(coef[:, 4, 1:K + 1], coef[:, 1, 1:K + 1], coef[:, 3, 0:K], ALU.mult))
                jv = jac[:, :].rearrange("p (k i) -> p k i", i=K + 1)
                link(dve.tensor_tensor(jv, jv, coef[:, 4:5, :].to_broadcast([P, K + 1, K + 1]), ALU.mult))
                link(dve.tensor_reduce(qk[:, 0:K + 1], jv, AX.X, ALU.add))
                link(dve.tensor_scalar(qk[:, K + 1:K + 2], qk[:, 0:1], 1.0, None, ALU.add))
                dve.wait_ge(s_hotu, T)
                dve.memset(srow[:, :, 3:4], 0.0)
                dve.tensor_copy(srow[:, :, 0:1].rearrange("h l c -> h (l c)"), kind_i[:, :])
                link(dve.tensor_copy(srow[:, :, 1:2].rearrange("h l c -> h (l c)"), deg_p[0:HI, 1, :]))
                link(dve.tensor_scalar(outdeg[:, :], deg_p[0:HI, 0, :], 1.0, None, ALU.max))
                link(dve.reciprocal(outdeg[:, :], outdeg[:, :]))
                dve.sem_inc(s_sq, 1)
                dve.tensor_copy(indeg[:, :], deg_p[0:HI, 1, :]).then_inc(s_srow, 1)
                dve.wait_ge(s_sq, 2)

            @block.scalar
            def _(act):
                act.wait_ge(s_w, 16 * len(WEIGHTS))
                act.wait_ge(s_z, 3)
                act.wait_ge(s_cut, 1)
                act.activation(cutw[:, :], cutw[:, :], ACT.Sin, bias=halfpi[:, 0:1],
                               scale=-PI / CUTOFF).then_inc(s_cut, 1)
                act.activation(coef[:, 2, :], coef[:, 0, :], ACT.Tanh).then_inc(s_coef, 1)
                act.wait_ge(s_sq, 1)
                act.activation(srow[:, :, 2:3].rearrange("h l c -> h (l c)"), outdeg[:, :],
                               ACT.Sqrt).then_inc(s_sq, 1)
                act.wait_ge(s_sq, 2)
                act.sem_inc(s_srow, 1)

            @block.tensor
            def _(pe):
                pe.wait_ge(s_z, 1)
                for j in range(2):
                    for h in range(2):
                        pe.matmul(deg_p[0:HI, j, 512 * h:512 * h + 512], zeros[:, 0:HI],
                                  zeros[:, 0:512], start=True, stop=False, skip_group_check=True)
                with pe.Fori(0, NB) as i:
                    for u in range(TB):
                        pe.wait_ge(s_hot, i * TB + u + 1)
                        pe.nop(nofuse=True)
                        for j in range(2):
                            for h in range(2):
                                ins = pe.matmul(deg_p[0:HI, j, 512 * h:512 * h + 512], hot_hi[:, u, j, :],
                                                hot_lo[:, u, j, 512 * h:512 * h + 512], start=False,
                                                stop=False, skip_group_check=True)
                        ins.then_inc(s_hotu, 1)
                pe.wait_ge(s_w, 16 * len(WEIGHTS))
                pe.matmul(mat_p[0:G, 0:NEL], adwt[:, :], embt[:, :], start=True, stop=True).then_inc(s_m, 1)
                pe.wait_ge(s_mc, 1)
                pe.matmul(mat2_p[0:NEL, 0:NEL], embt[:, :], vmat[:, :], start=True, stop=True).then_inc(s_m, 1)

        H7 = 7
        with ExitStack() as ph, nc.Block() as block:
            stage = ph.enter_context(nc.sbuf_tensor("sr_stage", [P, 2, H7], I32))
            ring = ph.enter_context(nc.sbuf_tensor("sr_ring", [P, 2, H7, 4], F32))
            s_stage = sem("source_index_staged")
            s_free = sem("source_ring_free")
            s_got = [sem(f"source_rows_got{h}") for h in range(2)]

            @block.scalar
            def _(act):
                clear(act, pow_t[NP:, :], s_pow)
                clear(act, y_t, s_y)
                clear(act, agg3_t, s_agg3)
                with act.Fori(0, T // (2 * H7)) as i:
                    for h in range(2):
                        act.wait_ge(s_got[h], i * (16 * H7))
                        act.nop(nofuse=True)
                        act.copy(stage[:, h, :], src_i[:, bass.ds((i * 2 + h) * H7, H7)]).then_inc(s_stage, 1)

            @block.gpsimd
            def _(pool):
                with pool.Fori(0, T // (2 * H7)) as i:
                    for h in range(2):
                        pool.wait_ge(s_stage, i * 2 + h + 1)
                        pool.wait_ge(s_free, i * 2 + h + 1)
                        pool.nop(nofuse=True)
                        for u in range(H7):
                            pool.indirect_dma_start(
                                out=ring[:, h, u, :], out_offset=None, in_=srow_t,
                                in_offset=bass.IndirectOffsetOnAxis(ap=stage[:, h, u:u + 1], axis=0),
                            ).then_inc(s_got[h], 16)

            @block.vector
            def _(dve):
                dve.sem_inc(s_free, 2)
                with dve.Fori(0, T // (2 * H7)) as i:
                    for h in range(2):
                        dve.wait_ge(s_got[h], i * (16 * H7) + 16 * H7)
                        dve.nop(nofuse=True)
                        dve.tensor_copy(
                            srows[:, :, :].rearrange("p t c -> p (t c)")[:, bass.ds((i * 2 + h) * (4 * H7), 4 * H7)],
                            ring[:, h, :, :].rearrange("p t c -> p (t c)")).then_inc(s_free, 1)

        def edge_dmas(pool, xt, aggt, xg, gidx, rows, sidx, s_gi, s_gx, s_xc, s_rows, s_si, s_add):
            def gather(u):
                pool.indirect_dma_start(
                    out=xg[:, u, :], out_offset=None, in_=xt,
                    in_offset=bass.IndirectOffsetOnAxis(ap=gidx[:, u:u + 1], axis=0)).then_inc(s_gx, 16)

            def add(u):
                pool.indirect_dma_start(
                    out=aggt, out_offset=bass.IndirectOffsetOnAxis(ap=sidx[:, u:u + 1], axis=0),
                    in_=rows[:, u, :], in_offset=None, compute_op=ALU.add).then_inc(s_add, 16)

            pool.wait_ge(s_gi, 1)
            for u in range(TB):
                gather(u)
            with pool.Fori(0, NB) as i:
                pool.wait_ge(s_xc, i + 1)
                pool.wait_ge(s_gi, i + 2)
                pool.nop(nofuse=True)
                gather(0)
                gather(1)
                pool.wait_ge(s_rows, i + 1)
                pool.wait_ge(s_si, i + 1)
                pool.wait_ge(s_add, i * 64)
                pool.nop(nofuse=True)
                add(0)
                add(1)
                gather(2)
                gather(3)
                pool.wait_ge(s_add, i * 64 + 32)
                pool.nop(nofuse=True)
                add(2)
                add(3)

        def group_sums(pe, sum_p, same, msg):
            width = msg.shape[2]
            for g in range(TB // 2):
                for c in range(2):
                    for r in range(2):
                        ins = pe.matmul(sum_p[:, 2 * g + c, 0:width],
                                        same[:, 2 * g + r, c * P:(c + 1) * P], msg[:, 2 * g + r, :],
                                        start=(r == 0), stop=(r == 1))
            return ins

        with ExitStack() as ph, nc.Block() as block:
            def tmp(name, shape, dt=F32):
                return ph.enter_context(nc.sbuf_tensor(name, shape, dt))

            def ptmp(name, shape, dt=F32):
                return ph.enter_context(nc.psum_tensor(name, shape, dt))

            iota_f = tmp("iota_f", [P, NEL])
            keys = tmp("keys", [P, TB // 2, GE], I32)
            same = tmp("same", [P, TB, GE])
            junk = tmp("junk", [P, TB, GE])
            junk2 = tmp("junk2", [P, TB, NEL])
            rank = tmp("rank", [P, TB])
            sidx = tmp("sidx", [P, TB], I32)
            gidx = tmp("gidx", [P, TB], I32)
            xg = tmp("xg", [P, TB, XW])
            xc = tmp("xc", [P, TB, XW])
            kind_d = tmp("kind_d", [P, TB])
            hot = tmp("hot", [P, TB, NEL])
            hot_t = tmp("hot_t", [NEL, TB, P])
            logit = tmp("logit", [P, TB])
            wgt = tmp("wgt", [P, TB])
            gated = tmp("gated", [P, TB, D])
            msg = tmp("msg", [P, TB, AW])
            rows = tmp("rows", [P, TB, AW])
            ea = tmp("ea", [R, TB * P])
            hid = tmp("hid", [D + 1, TB * P])
            hid_p = ptmp("hid_p", [P, 512])
            gate_p = ptmp("gate_p", [P, TB, 128])
            hott_p = ptmp("hott_p", [P, TB, P])
            logit_p = ptmp("logit_p", [P, TB, 128])
            sum_p = ptmp("sum_p", [P, TB, 128])
            s_ea = sem("l0_edge_features")
            s_key = sem("l0_keys")
            s_gx = sem("l0_target_rows_got")
            s_xc = sem("l0_target_rows_copied")
            s_gi = sem("l0_gather_index")
            s_hp = sem("l0_hidden_product")
            s_hid = sem("l0_hidden")
            s_gate = sem("l0_gate")
            s_hot = sem("l0_onehots")
            s_hott = sem("l0_onehots_turned")
            s_hotc = sem("l0_turned_copied")
            s_lg = sem("l0_logit_rows")
            s_same = sem("l0_same")
            s_si = sem("l0_scatter_index")
            s_msg = sem("l0_messages")
            s_sum = sem("l0_sums")
            s_rows = sem("l0_rows")
            s_add = sem("l0_added")
            s_v = sem("l0_vector_chain")
            s_one = sem("l0_ones")

            @block.sync
            def _(sp):
                with sp.Fori(0, NB) as i:
                    sp.wait_ge(s_hp, i)
                    sp.dma_start(ea[:, :], a["ea"][:, bass.ds(i * (TB * P), TB * P)]).then_inc(s_ea, 16)
                    sp.wait_ge(s_same, i)
                    sp.dma_start(keys[:, :, :].rearrange("p a b -> p (a b)"),
                                 a["src_rows"][bass.ds(i, 1), :].partition_broadcast(P)).then_inc(s_key, 16)

            @block.gpsimd
            def _(pool):
                pool.iota(iota_f[:, :], pattern=[[1, NEL]], base=0, channel_multiplier=0,
                          allow_small_or_imprecise_dtypes=True).then_inc(s_one, 1)
                pool.wait_ge(s_agg0, cleared(agg0_t))

                edge_dmas(pool, xz_t.bitcast(F32), agg0_t, xg, gidx, rows, sidx, s_gi, s_gx, s_xc, s_rows, s_si, s_add)

            @block.scalar
            def _(act):
                act.copy(gidx[:, :], dst_i[:, 0:TB]).then_inc(s_gi, 1)
                act.wait_ge(s_one, 2)
                with act.Fori(0, NB) as i:
                    act.wait_ge(s_gx, i * 64 + 64)
                    act.wait_ge(s_msg, i)
                    act.nop(nofuse=True)
                    act.copy(xc[:, :, :].bitcast(I32), xg[:, :, :].bitcast(I32)).then_inc(s_xc, 1)
                    act.copy(gidx[:, :], dst_i[:, bass.ds(i * TB + TB, TB)]).then_inc(s_gi, 1)
                    act.wait_ge(s_hp, i + 1)
                    act.wait_ge(s_gate, i)
                    act.activation(hid[0:D, :], hid_p[0:D, :], ACT.Silu, bias=b1c[:, 0:1]).then_inc(s_hid, 1)
                    act.wait_ge(s_hott, i + 1)
                    act.wait_ge(s_lg, i)
                    act.activation(hot_t[:, :, :], hott_p[0:NEL, :, :], ACT.Copy).then_inc(s_hotc, 1)
                    act.wait_ge(s_sum, i + 1)
                    act.wait_ge(s_add, i * 64)
                    act.activation(rows[:, :, :], sum_p[:, :, 0:AW], ACT.Copy).then_inc(s_rows, 1)

            @block.tensor
            def _(pe):
                with pe.Fori(0, NB) as i:
                    pe.wait_ge(s_ea, i * 16 + 16)
                    pe.nop(nofuse=True)
                    pe.matmul(hid_p[0:D, :], w1t[:, :], ea[:, :], start=True, stop=True).then_inc(s_hp, 1)
                    pe.wait_ge(s_hid, i + 1)
                    pe.wait_ge(s_msg, i)
                    pe.nop(nofuse=True)
                    for u in range(TB):
                        ins = pe.matmul(gate_p[:, u, 0:D], hid[:, u * P:(u + 1) * P], w2b[:, :],
                                        start=True, stop=True)
                    ins.then_inc(s_gate, 1)
                    pe.wait_ge(s_hot, i + 1)
                    pe.nop(nofuse=True)
                    for u in range(TB):
                        ins = pe.transpose(hott_p[0:NEL, u, :], hot[:, u, :], ident[:, :])
                    ins.then_inc(s_hott, 1)
                    pe.wait_ge(s_hotc, i + 1)
                    pe.nop(nofuse=True)
                    for u in range(TB):
                        ins = pe.matmul(logit_p[:, u, 0:NEL], hot_t[:, u, :], kindm[:, :], start=True, stop=True)
                    ins.then_inc(s_lg, 1)
                    pe.wait_ge(s_msg, i + 1)
                    pe.wait_ge(s_rows, i)
                    pe.nop(nofuse=True)
                    group_sums(pe, sum_p, same, msg).then_inc(s_sum, 1)

            @block.vector
            def _(dve):
                STEPS = 5
                dve.memset(hid[:, :], 1.0).then_inc(s_one, 1)
                dve.wait_ge(s_one, 2)
                with dve.Fori(0, NB) as i:
                    n = [0]

                    def chain(ins):
                        n[0] += 1
                        ins.then_inc(s_v, 1)
                        dve.wait_ge(s_v, i * STEPS + n[0])

                    dve.wait_ge(s_key, i * 16 + 16)
                    dve.wait_ge(s_sum, i)
                    for u in range(TB):
                        dve.tensor_scalar(same[:, u, :], keys[:, u // 2, :], src_f[:, bass.ds(i * TB + u, 1)],
                                          None, ALU.is_equal)
                    for u in range(TB):
                        ins = dve.scalar_tensor_tensor(out=junk[:, u, :], in0=keys[:, u // 2, :],
                                                       scalar=src_f[:, bass.ds(i * TB + u, 1)],
                                                       in1=earlier[:, u % 2, :], op0=ALU.is_equal, op1=ALU.mult,
                                                       accum_out=rank[:, u:u + 1])
                    ins.then_inc(s_same, 1)
                    dve.wait_ge(s_same, i + 1)
                    chain(dve.scalar_tensor_tensor(out=rank[:, :], in0=rank[:, :], scalar=1.0, in1=sink[:, :],
                                                   op0=ALU.min, op1=ALU.mult))
                    dve.wait_ge(s_add, i * 64)
                    dve.tensor_tensor(sidx[:, :], rank[:, :], src_f[:, bass.ds(i * TB, TB)],
                                      ALU.max).then_inc(s_si, 1)
                    dve.wait_ge(s_hott, i)
                    for u in range(TB):
                        ins = dve.tensor_scalar(hot[:, u, :], iota_f[:, :],
                                                srows[:, bass.ds(i * TB + u, 1), 0:1].rearrange("p a b -> p (a b)"),
                                                None, ALU.is_equal)
                    ins.then_inc(s_hot, 1)
                    dve.wait_ge(s_xc, i + 1)
                    chain(dve.tensor_copy(kind_d[:, :], xc[:, :, D + 1].bitcast(I32)))
                    dve.tensor_tensor(wgt[:, :], cutw[:, bass.ds(i * TB, TB)], xc[:, :, D], ALU.mult)
                    dve.wait_ge(s_lg, i + 1)
                    for u in range(TB):
                        ins = dve.scalar_tensor_tensor(out=junk2[:, u, :], in0=iota_f[:, :],
                                                       scalar=kind_d[:, u:u + 1], in1=logit_p[:, u, 0:NEL],
                                                       op0=ALU.is_equal, op1=ALU.mult,
                                                       accum_out=logit[:, u:u + 1])
                    chain(ins)
                    dve.wait_ge(s_gate, i + 1)
                    for u in range(TB):
                        ins = dve.scalar_tensor_tensor(out=gated[:, u, :], in0=gate_p[:, u, 0:D],
                                                       scalar=logit[:, u:u + 1], in1=xc[:, u, 0:D],
                                                       op0=ALU.add, op1=ALU.mult)
                    chain(ins)
                    for u in range(TB):
                        dve.tensor_scalar(msg[:, u, 0:D], gated[:, u, :], wgt[:, u:u + 1], None, ALU.mult)
                    chain(dve.tensor_copy(msg[:, :, D], xc[:, :, D]))
                    dve.sem_inc(s_msg, 1)
                    assert n[0] == STEPS
                dve.wait_ge(s_add, NB * 64)

        indeg_n = sb("indeg_n", [P, NF])
        cj_n = sb("cj_n", [P, NF])
        dinv_n = sb("dinv_n", [P, NF])
        none_n = sb("none_n", [P, NF])

        def nodes(tbl, c, width):
            return tbl.rearrange("(p f) d -> p (f d)", p=P)[:, bass.ds(c * (CH * width), CH * width)]

        def stream(sp, loads, stores, s_ld, s_res, s_st):
            def load(c, s):
                for tbl, width, tile in loads:
                    sp.dma_start(tile[:, s, :, :].rearrange("p f d -> p (f d)"),
                                 nodes(tbl, c, width)).then_inc(s_ld[s], 16)

            def store(c, s):
                sp.wait_ge(s_res, c + 1)
                for tbl, width, tile in stores:
                    sp.dma_start(nodes(tbl, c, width),
                                 tile[:, s, :, :].rearrange("p f d -> p (f d)")).then_inc(s_st[s], 16)

            load(0, 0)
            load(1, 1)
            with sp.Fori(0, NC // 2 - 1) as i:
                for s in range(2):
                    store(i * 2 + s, s)
                    load(i * 2 + s + 2, s)
            for s in range(2):
                store(NC - 2 + s, s)
            for s in range(2):
                sp.wait_ge(s_st[s], 16 * len(stores) * (NC // 2))

        class Norm:

            def __init__(self, name, x, sq, stat, per_step):
                self.x, self.sq, self.stat, self.per = x, sq, stat, per_step
                self.s_cent = sem(name + "_centred")
                self.s_sq = sem(name + "_squared")
                self.s_var = sem(name + "_variance")
                self.s_root = sem(name + "_root")

            def count(self, i, k, s):
                return i * (2 * self.per) + 2 * k + s + 1

            def centre(self, dve, i, did, need, k):
                at = [did(dve.tensor_reduce(self.stat[:, s, 0, :], self.x[:, s, :, :], AX.X, ALU.add))
                      for s in range(2)]
                for s in range(2):
                    need(at[s])
                    at[s] = did(dve.tensor_scalar(self.stat[:, s, 0, :], self.stat[:, s, 0, :], -1.0 / D, None,
                                                  ALU.mult))
                for s in range(2):
                    need(at[s])
                    mean = self.stat[:, s, 0, :].unsqueeze(2).to_broadcast([P, CH, D])
                    dve.tensor_tensor(self.x[:, s, :, :], self.x[:, s, :, :], mean,
                                      ALU.add).then_inc(self.s_cent, 1)

            def scale(self, dve, i, did, need, k):
                at = [0, 0]
                for s in range(2):
                    dve.wait_ge(self.s_sq, self.count(i, k, s))
                    at[s] = did(dve.tensor_reduce(self.stat[:, s, 1, :], self.sq[:, s, :, :], AX.X, ALU.add))
                for s in range(2):
                    need(at[s])
                    dve.tensor_scalar(self.stat[:, s, 1, :], self.stat[:, s, 1, :], 1.0 / D, EPS, ALU.mult,
                                      ALU.add).then_inc(self.s_var, 1)
                for s in range(2):
                    dve.wait_ge(self.s_root, self.count(i, k, s))
                    at[s] = did(dve.reciprocal(self.stat[:, s, 2, :], self.stat[:, s, 2, :]))
                for s in range(2):
                    need(at[s])
                    inv = self.stat[:, s, 2, :].unsqueeze(2).to_broadcast([P, CH, D])
                    at[s] = did(dve.tensor_tensor(self.x[:, s, :, :], self.x[:, s, :, :], inv, ALU.mult))
                return at

            def square(self, act, i, k):
                for s in range(2):
                    act.wait_ge(self.s_cent, self.count(i, k, s))
                    act.activation(self.sq[:, s, :, :], self.x[:, s, :, :], ACT.Square).then_inc(self.s_sq, 1)
                for s in range(2):
                    act.wait_ge(self.s_var, self.count(i, k, s))
                    act.activation(self.stat[:, s, 2, :], self.stat[:, s, 1, :], ACT.Sqrt).then_inc(self.s_root, 1)

        def chain_of(dve, s_v, i, steps):
            n = [0]

            def did(ins):
                n[0] += 1
                ins.then_inc(s_v, 1)
                return n[0]

            def need(k):
                dve.wait_ge(s_v, i * steps + k)
            return did, need, n

        with ExitStack() as ph, nc.Block() as block:
            def tmp(name, shape, dt=F32):
                return ph.enter_context(nc.sbuf_tensor(name, shape, dt))

            xin = tmp("d0_x", [P, 2, CH, XW])
            agg = tmp("d0_agg", [P, 2, CH, AW])
            x = tmp("d0_out", [P, 2, CH, D])
            sq = tmp("d0_sq", [P, 2, CH, D])
            stat = tmp("d0_stat", [P, 2, 3, CH])
            ln = Norm("d0", x, sq, stat, 2)
            s_ld = [sem(f"d0_loaded{s}") for s in range(2)]
            s_st = [sem(f"d0_stored{s}") for s in range(2)]
            s_res = sem("d0_result")
            s_v = sem("d0_chain")
            s_n = sem("node_degrees")
            s_nr = sem("node_roots")

            @block.sync
            def _(sp):
                sp.dma_start(indeg_n[:, :], indeg_t.rearrange("(p f) c -> p (f c)", p=P)).then_inc(s_n, 16)
                stream(sp, [(xz_t.bitcast(F32), XW, xin), (agg0_t, AW, agg)], [(x1_t, D, x)], s_ld, s_res, s_st)

            @block.scalar
            def _(act):
                act.wait_ge(s_nr, 1)
                act.activation(cj_n[:, :], cj_n[:, :], ACT.Sqrt).then_inc(s_nr, 1)
                with act.Fori(0, NC // 2) as i:
                    for k in range(2):
                        ln.square(act, i, k)

            @block.vector
            def _(dve):
                m = [0]

                def link(ins):
                    m[0] += 1
                    ins.then_inc(s_v, 1)
                    dve.wait_ge(s_v, m[0])

                FIRST = 5
                dve.wait_ge(s_n, 16)
                link(dve.tensor_scalar(cj_n[:, :], indeg_n[:, :], 1.0, None, ALU.max))
                dve.reciprocal(cj_n[:, :], cj_n[:, :]).then_inc(s_nr, 1)
                link(dve.tensor_scalar(indeg_n[:, :], indeg_n[:, :], 1.0, None, ALU.min))
                link(dve.tensor_scalar(none_n[:, :], indeg_n[:, :], -1.0, 1.0, ALU.mult, ALU.add))
                dve.wait_ge(s_nr, 2)
                link(dve.tensor_tensor(dinv_n[:, :], cj_n[:, :], indeg_n[:, :], ALU.mult))
                link(dve.memset(sq[:, 0, 0:1, 0:1], 0.0))
                assert m[0] == FIRST
                STEPS = 34
                with dve.Fori(0, NC // 2) as i:
                    did, need, n = chain_of(dve, s_v, i, STEPS)

                    def need(k):
                        dve.wait_ge(s_v, i * STEPS + (FIRST + k))
                    at = [0, 0]
                    for s in range(2):
                        dve.wait_ge(s_ld[s], i * 32 + 32)
                        at[s] = did(dve.tensor_scalar(stat[:, s, 0, :], agg[:, s, :, D], 1e-8, None, ALU.max))
                    for s in range(2):
                        need(at[s])
                        at[s] = did(dve.reciprocal(stat[:, s, 1, :], stat[:, s, 0, :]))
                    for s in range(2):
                        need(at[s])
                        dve.wait_ge(s_st[s], i * 16)
                        at[s] = did(dve.tensor_tensor(x[:, s, :, :], agg[:, s, :, 0:D],
                                                      stat[:, s, 1, :].unsqueeze(2).to_broadcast([P, CH, D]),
                                                      ALU.mult))
                    for s in range(2):
                        need(at[s])
                        at[s] = did(dve.tensor_tensor(x[:, s, :, :], x[:, s, :, :], xin[:, s, :, 0:D], ALU.add))
                    need(at[1])
                    ln.centre(dve, i, did, need, 0)
                    at = ln.scale(dve, i, did, need, 0)
                    for vec, op in ((gammab, ALU.mult), (betab, ALU.add)):
                        for s in range(2):
                            need(at[s])
                            at[s] = did(dve.tensor_tensor(x[:, s, :, :], x[:, s, :, :],
                                                          vec[:, :].unsqueeze(1).to_broadcast([P, CH, D]), op))
                    for s in range(2):
                        need(at[s])
                        at[s] = did(dve.tensor_tensor(x[:, s, :, :], x[:, s, :, :], xin[:, s, :, 0:D], ALU.add))
                    need(at[1])
                    ln.centre(dve, i, did, need, 1)
                    at = ln.scale(dve, i, did, need, 1)
                    need(at[1])
                    dve.sem_inc(s_res, 2)
                    assert n[0] == STEPS, n[0]

        with ExitStack() as ph, nc.Block() as block:
            def tmp(name, shape, dt=F32):
                return ph.enter_context(nc.sbuf_tensor(name, shape, dt))

            def ptmp(name, shape, dt=F32):
                return ph.enter_context(nc.psum_tensor(name, shape, dt))

            TL = T + TB
            TOP = 256
            edge = tmp("edge", [P, T, 4])
            filler = tmp("filler", [1, 4])
            lst = tmp("list", [P, TL, 4])
            prev_dst = tmp("prev_dst", [P, TL])
            own_dst = tmp("own_dst", [P, TL])
            w_k = tmp("w_k", [P, TL])
            zero_in = tmp("zero_in", [P, TL])
            key = tmp("key", [P, T])
            ttop = tmp("ttop", [P, TL])
            best = tmp("best", [P, 8])
            order = tmp("order", [P, T + 8])
            live = tmp("live", [P, T + 8])
            eid_f = tmp("eid_f", [P, T + 8])
            eid = tmp("eid", [P, T + 8], I32)
            ebase = tmp("ebase", [P, 1])
            count = tmp("count", [P, 1])
            sizes_f = tmp("sizes_f", [1, 4])
            sizes = tmp("sizes", [1, 4], I32)
            gi = tmp("gi", [P, TL], I32)
            ri = tmp("ri", [P, TL], I32)
            ci = tmp("ci", [P, TL], I32)
            level = tmp("level", [P, 2 * K])
            off = tmp("off", [P, 2])
            qcur = tmp("qcur", [P, 1])
            gidx = tmp("p_gidx", [P, TB], I32)
            sidx_r = tmp("p_sidx_r", [P, TB], I32)
            sidx_y = tmp("p_sidx_y", [P, TB], I32)
            cidx = tmp("p_cidx", [P, TB], I32)
            lidx = tmp("p_lidx", [P, 2, 2], I32)
            lring = tmp("p_lring", [P, 2, 2, 4])
            fidx = tmp("p_fidx", [P, 2, 2], I32)
            fring = tmp("p_fring", [P, 2, 2, D])
            fjunk = tmp("p_fjunk", [P, 2, 2, D])
            fcount = tmp("p_fcount", [P, 2, 2])
            xg = tmp("p_xg", [P, TB, D])
            xc = tmp("p_xc", [P, TB, D])
            dkey = tmp("p_dkey", [P, TB])
            keys = tmp("p_keys", [P, TB, P])
            same = tmp("p_same", [P, TB, GE])
            junk = tmp("p_junk", [P, TB, GE])
            rank = tmp("p_rank", [P, TB])
            msg = tmp("p_msg", [P, TB, D])
            rows_r = tmp("p_rows_r", [P, TB, D])
            rows_y = tmp("p_rows_y", [P, TB, D])
            keys_p = ptmp("keys_p", [P, TB, P])
            sum_p = ptmp("psum_p", [P, TB, 128])
            cnt_p = ptmp("cnt_p", [P, 512])
            s_lv = sem("p_level_constants")
            s_edge = sem("p_edge_table")
            s_cnt = sem("p_count")
            s_cntt = sem("p_count_turned")
            s_nx = sem("p_list_size")
            s_ei = sem("p_edge_ids")
            s_li = sem("p_list_index")
            s_lg = [sem(f"p_list_rows{h}") for h in range(2)]
            s_lf = sem("p_list_ring_free")
            s_go = sem("p_level_ready")
            s_q = sem("p_coefficient")
            s_gi = sem("p_gather_index")
            s_gx = sem("p_rows_got")
            s_xc = sem("p_rows_copied")
            s_dk = sem("p_target_keys")
            s_kt = sem("p_keys_turned")
            s_kc = sem("p_keys_copied")
            s_si = sem("p_scatter_index")
            s_msg = sem("p_messages")
            s_sum = sem("p_sums")
            s_rows = sem("p_rows_ready")
            s_addr = sem("p_added_powers")
            s_addy = sem("p_added_filter")
            s_ci = sem("p_clear_index")
            s_cl = sem("p_cleared")
            s_fi = sem("p_flag_index")
            s_fg = [sem(f"p_flag_rows{h}") for h in range(2)]
            s_ff = sem("p_flag_ring_free")
            s_v = sem("p_chain")
            s_root = sem("p_first_weights")
            H2 = 2

            class Levels:

                def __init__(self, eng, tag):
                    self.eng = eng
                    self.reg = {x: eng.alloc_register(f"{tag}_{x}") for x in ("n", "c", "m", "b")}
                    eng.wait_ge(s_nx, 1)
                    first = self.size(0)
                    eng.reg_mov(self.reg["n"], first)
                    for x, v in (("c", 0), ("m", 1), ("b", 0)):
                        eng.reg_mov(self.reg[x], v)
                    self.first = first

                def size(self, j):
                    self.eng.nop(nofuse=True)
                    return self.eng.value_load(sizes[0:1, j:j + 1], min_val=1, max_val=NB)

                def here(self):
                    return [self.eng.snap(self.reg[x]) for x in ("n", "c", "m", "b")]

                def next(self, n, c, m, b, new):
                    self.eng.reg_mov(self.reg["b"], b + m)
                    self.eng.reg_mov(self.reg["m"], n)
                    self.eng.reg_mov(self.reg["c"], c + n)
                    self.eng.reg_mov(self.reg["n"], new)

            @block.sync
            def _(sp):
                sp.dma_start(level[:, :], a["level"].partition_broadcast(P)).then_inc(s_lv, 16)
                sp.wait_ge(s_edge, 1)
                sp.dma_start(edge_t[0:EP, :].rearrange("(p t) c -> p (t c)", p=P),
                             edge[:, :, :].rearrange("p t c -> p (t c)")).then_inc(s_edge, 16)
                sp.dma_start(edge_t[EP:EP + 1, :], filler[:, :]).then_inc(s_edge, 16)
                sp.wait_ge(s_edge, 33)

            @block.gpsimd
            def _(pool):
                pool.iota(ebase[:, :], pattern=[[0, 1]], base=TOP - EP, channel_multiplier=T,
                          allow_small_or_imprecise_dtypes=True).then_inc(s_lv, 1)
                pool.iota(edge[:, :, 3:4].rearrange("p t c -> p (t c)"), pattern=[[1, T]], base=0,
                          channel_multiplier=0, allow_small_or_imprecise_dtypes=True).then_inc(s_lv, 1)

                def build(n, c):
                    with pool.Fori(0, n) as i:
                        for h in range(2):
                            pool.wait_ge(s_li, (c + i) * 2 + (h + 1))
                            pool.wait_ge(s_lf, (c + i) * 2 + (h + 1))
                            pool.nop(nofuse=True)
                            for u in range(H2):
                                pool.indirect_dma_start(
                                    out=lring[:, h, u, :], out_offset=None, in_=edge_t,
                                    in_offset=bass.IndirectOffsetOnAxis(ap=lidx[:, h, u:u + 1], axis=0),
                                ).then_inc(s_lg[h], 16)

                def gather(u):
                    pool.indirect_dma_start(
                        out=xg[:, u, :], out_offset=None, in_=pow_t,
                        in_offset=bass.IndirectOffsetOnAxis(ap=gidx[:, u:u + 1], axis=0)).then_inc(s_gx, 16)

                def add(tbl, idx, rows, done, u):
                    pool.indirect_dma_start(
                        out=tbl, out_offset=bass.IndirectOffsetOnAxis(ap=idx[:, u:u + 1], axis=0),
                        in_=rows[:, u, :], in_offset=None, compute_op=ALU.add).then_inc(done, 16)

                lv = Levels(pool, "pool")
                pool.wait_ge(s_edge, 33)
                build(lv.first, 0)
                pool.wait_ge(s_pow, cleared(pow_t[NP:, :]))
                pool.wait_ge(s_y, cleared(y_t))
                with pool.Fori(0, K) as k:
                    n, c, m, b = lv.here()
                    pool.wait_ge(s_gi, c + k + 1)
                    pool.nop(nofuse=True)
                    for u in range(TB):
                        gather(u)
                    pool.wait_ge(s_cl, b * 64)
                    pool.nop(nofuse=True)
                    with pool.Fori(0, n) as i:
                        pool.wait_ge(s_xc, c + i + 1)
                        pool.wait_ge(s_gi, c + k + i + 2)
                        pool.nop(nofuse=True)
                        gather(0)
                        gather(1)
                        pool.wait_ge(s_rows, c + i + 1)
                        pool.wait_ge(s_si, c + i + 1)
                        pool.wait_ge(s_addr, (c + i) * 64)
                        pool.wait_ge(s_addy, (c + i) * 64)
                        pool.nop(nofuse=True)
                        for g in range(2):
                            if g == 1:
                                gather(2)
                                gather(3)
                                pool.wait_ge(s_addr, (c + i) * 64 + 32)
                                pool.wait_ge(s_addy, (c + i) * 64 + 32)
                                pool.nop(nofuse=True)
                            for u in (2 * g, 2 * g + 1):
                                add(pow_t, sidx_r, rows_r, s_addr, u)
                            for u in (2 * g, 2 * g + 1):
                                add(y_t, sidx_y, rows_y, s_addy, u)
                    pool.wait_ge(s_gx, (c + k + n + 1) * 64)
                    pool.nop(nofuse=True)
                    with pool.Fori(0, m) as i:
                        pool.wait_ge(s_ci, b + i + 1)
                        pool.nop(nofuse=True)
                        for u in range(TB):
                            if u == GE // P:
                                pool.wait_ge(s_cl, (b + i) * 64 + 32)
                                pool.nop(nofuse=True)
                            pool.indirect_dma_start(
                                out=pow_t, out_offset=bass.IndirectOffsetOnAxis(ap=cidx[:, u:u + 1], axis=0),
                                in_=zeros[:, 0:D], in_offset=None).then_inc(s_cl, 16)
                    pool.wait_ge(s_addr, (c + n) * 64)
                    pool.nop(nofuse=True)
                    with pool.Fori(0, n) as i:
                        for h in range(2):
                            pool.wait_ge(s_fi, (c + i) * 2 + (h + 1))
                            pool.wait_ge(s_ff, (c + i) * 2 + (h + 1))
                            pool.nop(nofuse=True)
                            for u in range(H2):
                                pool.indirect_dma_start(
                                    out=fring[:, h, u, :], out_offset=None, in_=pow_t,
                                    in_offset=bass.IndirectOffsetOnAxis(ap=fidx[:, h, u:u + 1], axis=0),
                                ).then_inc(s_fg[h], 16)
                    pool.wait_ge(s_nx, k + 2)
                    new = lv.size(0)
                    build(new, c + n)
                    lv.next(n, c, m, b, new)

            @block.scalar
            def _(act):
                def build(n, c):
                    with act.Fori(0, n) as i:
                        for h in range(2):
                            act.wait_ge(s_lg[h], (c + i) * (16 * H2))
                            act.nop(nofuse=True)
                            act.copy(lidx[:, h, :], eid[:, bass.ds(i * TB + h * H2, H2)]).then_inc(s_li, 1)

                lv = Levels(act, "act")
                act.wait_ge(s_ei, 1)
                build(lv.first, 0)
                act.wait_ge(s_root, 1)
                act.activation(w_k[:, :], w_k[:, :], ACT.Sqrt).then_inc(s_root, 1)
                with act.Fori(0, K) as k:
                    n, c, m, b = lv.here()
                    act.wait_ge(s_go, k + 1)
                    act.nop(nofuse=True)
                    act.copy(qcur[:, :], qk[:, bass.ds(k + 1, 1)]).then_inc(s_q, 1)
                    act.copy(gidx[:, :], gi[:, 0:TB]).then_inc(s_gi, 1)
                    act.wait_ge(s_q, k + 1)
                    with act.Fori(0, n) as i:
                        act.wait_ge(s_gx, (c + k + i) * 64 + 64)
                        act.wait_ge(s_msg, c + i)
                        act.nop(nofuse=True)
                        act.copy(xc[:, :, :], xg[:, :, :]).then_inc(s_xc, 1)
                        act.copy(gidx[:, :], gi[:, bass.ds(i * TB + TB, TB)]).then_inc(s_gi, 1)
                        act.wait_ge(s_kt, c + i + 1)
                        act.wait_ge(s_si, c + i)
                        act.activation(keys[:, :, :], keys_p[:, :, :], ACT.Copy).then_inc(s_kc, 1)
                        act.wait_ge(s_sum, c + i + 1)
                        act.wait_ge(s_addr, (c + i) * 64)
                        act.wait_ge(s_addy, (c + i) * 64)
                        act.activation(rows_r[:, :, :], sum_p[:, :, 0:D], ACT.Copy)
                        act.activation(rows_y[:, :, :], sum_p[:, :, 0:D], ACT.Copy,
                                       scale=qcur[:, 0:1]).then_inc(s_rows, 1)
                    with act.Fori(0, m) as i:
                        act.wait_ge(s_cl, (b + i) * 64)
                        act.nop(nofuse=True)
                        act.copy(cidx[:, :], ci[:, bass.ds(i * TB, TB)]).then_inc(s_ci, 1)
                    with act.Fori(0, n) as i:
                        for h in range(2):
                            act.wait_ge(s_fg[h], (c + i) * (16 * H2))
                            act.nop(nofuse=True)
                            act.copy(fidx[:, h, :], ri[:, bass.ds(i * TB + h * H2, H2)]).then_inc(s_fi, 1)
                    act.wait_ge(s_nx, k + 2)
                    new = lv.size(0)
                    act.wait_ge(s_ei, k + 2)
                    build(new, c + n)
                    lv.next(n, c, m, b, new)

            @block.tensor
            def _(pe):
                pe.wait_ge(s_cnt, 1)
                pe.transpose(cnt_p[0:1, 0:P], count[:, 0:1], ident[:, :]).then_inc(s_cntt, 1)
                lv = Levels(pe, "pe")
                with pe.Fori(0, K) as k:
                    n, c, m, b = lv.here()
                    with pe.Fori(0, n) as i:
                        pe.wait_ge(s_dk, c + i + 1)
                        pe.wait_ge(s_kc, c + i)
                        pe.nop(nofuse=True)
                        for u in range(TB):
                            ins = pe.transpose(keys_p[:, u, :], dkey[:, u:u + 1].to_broadcast([P, P]), ident[:, :])
                        ins.then_inc(s_kt, 1)
                        pe.wait_ge(s_msg, c + i + 1)
                        pe.wait_ge(s_rows, c + i)
                        pe.nop(nofuse=True)
                        group_sums(pe, sum_p, same, msg).then_inc(s_sum, 1)
                    pe.wait_ge(s_cnt, k + 2)
                    pe.nop(nofuse=True)
                    pe.transpose(cnt_p[0:1, 0:P], count[:, 0:1], ident[:, :]).then_inc(s_cntt, 1)
                    pe.wait_ge(s_nx, k + 2)
                    lv.next(n, c, m, b, lv.size(0))

            @block.vector
            def _(dve):
                mark = dve.alloc_register("dve_mark")
                dve.reg_mov(mark, 0)
                here = [dve.snap(mark), 0]

                def chain(ins):
                    here[1] += 1
                    ins.then_inc(s_v, 1)
                    dve.wait_ge(s_v, here[0] + here[1])

                def settle(extra=0):
                    dve.reg_mov(mark, here[0] + (here[1] + extra))

                def resume():
                    here[0], here[1] = dve.snap(mark), 0

                def size_and_sort(k):
                    chain(dve.tensor_scalar(live[:, 0:T], key[:, :], 0.5, None, ALU.is_gt))
                    dve.tensor_reduce(count[:, :], live[:, 0:T], AX.X, ALU.add).then_inc(s_cnt, 1)
                    dve.wait_ge(s_cntt, k + 1)
                    dve.nop(nofuse=True)
                    chain(dve.tensor_reduce(sizes_f[:, 0:1], cnt_p[0:1, 0:P], AX.X, ALU.max))
                    chain(dve.tensor_scalar(sizes_f[:, 0:1], sizes_f[:, 0:1], 3.0, None, ALU.add))
                    chain(dve.tensor_copy(sizes[:, 0:1], sizes_f[:, 0:1]))
                    chain(dve.tensor_scalar(sizes[:, 0:1], sizes[:, 0:1], 2, None, ALU.logical_shift_right))
                    chain(dve.tensor_copy(sizes_f[:, 0:1], sizes[:, 0:1]))
                    chain(dve.tensor_scalar(sizes_f[:, 0:1], sizes_f[:, 0:1], 1.0, None, ALU.max))
                    chain(dve.tensor_scalar(sizes_f[:, 1:2], sizes_f[:, 0:1], 1.0, None, ALU.add))
                    chain(dve.tensor_copy(sizes[:, 0:2], sizes_f[:, 0:2]))
                    chain(dve.tensor_scalar(sizes[:, 1:2], sizes[:, 1:2], 1, None, ALU.logical_shift_right))
                    dve.sem_inc(s_nx, 1)
                    rounds = dve.value_load(sizes[0:1, 1:2], min_val=1, max_val=(NB + 1) // 2)
                    settle()
                    with dve.Fori(0, rounds) as r:
                        resume()
                        chain(dve.max(best[:, :], key[:, :]))
                        dve.tensor_copy(order[:, bass.ds(r * 8, 8)], best[:, :])
                        chain(dve.match_replace(key[:, :], best[:, :], key[:, :], 0.0))
                        settle()
                    resume()
                    chain(dve.tensor_scalar(live[:, :], order[:, :], 1.0, None, ALU.min))
                    chain(dve.tensor_scalar(eid_f[:, :], order[:, :], -1.0, ebase[:, 0:1], ALU.mult, ALU.add))
                    chain(dve.tensor_tensor(eid_f[:, :], eid_f[:, :], live[:, :], ALU.mult))
                    chain(dve.tensor_scalar(eid[:, :], eid_f[:, :], float(EP), None, ALU.add))
                    dve.sem_inc(s_ei, 1)

                def build(n, c):
                    flat = lst[:, :, :].rearrange("p t c -> p (t c)")
                    with dve.Fori(0, n) as i:
                        for h in range(2):
                            dve.wait_ge(s_lg[h], (c + i) * (16 * H2) + 16 * H2)
                            dve.nop(nofuse=True)
                            ins = dve.tensor_copy(flat[:, bass.ds(i * (4 * TB) + h * (4 * H2), 4 * H2)],
                                                  lring[:, h, :, :].rearrange("p t c -> p (t c)"))
                            ins.then_inc(s_lf, 1)
                    dve.wait_ge(s_lf, (c + n) * 2 + 2)
                    dve.nop(nofuse=True)

                dve.wait_ge(s_lv, 18)
                dve.sem_inc(s_lf, 2)
                dve.sem_inc(s_ff, 2)
                dve.tensor_copy(edge[:, :, 0], src_f[:, :])
                dve.tensor_copy(edge[:, :, 1], dst_f[:, :])
                dve.tensor_copy(edge[:, :, 2], srows[:, :, 1])
                dve.memset(order[:, :], 0.0)
                chain(dve.memset(filler[:, :], 0.0))
                dve.memset(filler[:, 0:1], float(SPARE_SRC))
                dve.memset(filler[:, 1:2], float(SPARE_DST))
                dve.memset(filler[:, 2:3], 1.0)
                dve.memset(lst[:, :, :], 1.0)
                dve.memset(prev_dst[:, :], 0.0)
                dve.memset(own_dst[:, :], 0.0)
                chain(dve.tensor_scalar(key[:, :], edge[:, :, 3], -1.0, float(TOP), ALU.mult, ALU.add))
                dve.sem_inc(s_edge, 1)
                dve.tensor_copy(prev_dst[:, 0:TB], sink[:, :])
                chain(dve.tensor_scalar(live[:, 0:T], edge[:, :, 2], 1.0, None, ALU.min))
                chain(dve.tensor_tensor(key[:, :], key[:, :], live[:, 0:T], ALU.mult))
                size_and_sort(0)
                settle()
                lv = Levels(dve, "dve")
                build(lv.first, 0)
                resume()
                dve.reciprocal(w_k[:, :], lst[:, :, 2]).then_inc(s_root, 1)
                dve.wait_ge(s_root, 2)
                with dve.Fori(0, K) as k:
                    n, c, m, b = lv.here()
                    resume()
                    chain(dve.tensor_copy(off[:, :], level[:, bass.ds(k * 2, 2)]))
                    dve.tensor_scalar(gi[:, :], lst[:, :, 0], off[:, 0:1], None, ALU.add)
                    dve.tensor_scalar(ri[:, :], lst[:, :, 0], off[:, 1:2], None, ALU.add)
                    dve.tensor_scalar(ci[:, :], prev_dst[:, :], off[:, 0:1], None, ALU.add)
                    dve.tensor_scalar(ttop[:, :], lst[:, :, 3], -1.0, float(TOP), ALU.mult, ALU.add)
                    dve.memset(zero_in[:, :], float(D))
                    chain(dve.tensor_copy(dkey[:, :], lst[:, 0:TB, 1]))
                    dve.sem_inc(s_go, 1)
                    settle()
                    with dve.Fori(0, n) as i:
                        resume()
                        dve.wait_ge(s_kt, c + i)
                        chain(dve.tensor_copy(dkey[:, :], lst[:, bass.ds(i * TB, TB), 1]))
                        dve.sem_inc(s_dk, 1)
                        dve.wait_ge(s_kc, c + i + 1)
                        dve.wait_ge(s_sum, c + i)
                        for u in range(TB):
                            kg = keys[:, 2 * (u // 2):2 * (u // 2) + 2, :].rearrange("p a b -> p (a b)")
                            dve.tensor_scalar(same[:, u, :], kg, dkey[:, u:u + 1], None, ALU.is_equal)
                        for u in range(TB):
                            kg = keys[:, 2 * (u // 2):2 * (u // 2) + 2, :].rearrange("p a b -> p (a b)")
                            ins = dve.scalar_tensor_tensor(out=junk[:, u, :], in0=kg, scalar=dkey[:, u:u + 1],
                                                           in1=earlier[:, u % 2, :], op0=ALU.is_equal,
                                                           op1=ALU.mult, accum_out=rank[:, u:u + 1])
                        chain(ins)
                        chain(dve.scalar_tensor_tensor(out=rank[:, :], in0=rank[:, :], scalar=1.0, in1=sink[:, :],
                                                   op0=ALU.min, op1=ALU.mult))
                        chain(dve.tensor_tensor(rank[:, :], rank[:, :], dkey[:, :], ALU.max))
                        dve.wait_ge(s_addr, (c + i) * 64)
                        dve.wait_ge(s_addy, (c + i) * 64)
                        dve.tensor_copy(sidx_y[:, :], rank[:, :])
                        dve.tensor_copy(own_dst[:, bass.ds(i * TB, TB)], rank[:, :])
                        dve.tensor_scalar(sidx_r[:, :], rank[:, :], off[:, 1:2], None, ALU.add).then_inc(s_si, 1)
                        dve.wait_ge(s_xc, c + i + 1)
                        for u in range(TB):
                            ins = dve.tensor_scalar(msg[:, u, :], xc[:, u, :],
                                                    w_k[:, bass.ds(i * TB + u, 1)], None, ALU.mult)
                        chain(ins)
                        dve.sem_inc(s_msg, 1)
                        settle()
                    with dve.Fori(0, n) as i:
                        resume()
                        for h in range(2):
                            dve.wait_ge(s_fg[h], (c + i) * (16 * H2) + 16 * H2)
                            for u in range(H2):
                                ins = dve.tensor_scalar(fjunk[:, h, u, :], fring[:, h, u, :], 0.0, 0.0,
                                                        ALU.is_equal, ALU.add, accum_out=fcount[:, h, u:u + 1])
                            chain(ins)
                            dve.sem_inc(s_ff, 1)
                            chain(dve.tensor_copy(zero_in[:, bass.ds(i * TB + h * H2, H2)], fcount[:, h, :]))
                        settle()
                    resume()
                    chain(dve.scalar_tensor_tensor(out=key[:, :], in0=zero_in[:, 0:T], scalar=D - 0.5,
                                                   in1=ttop[:, 0:T], op0=ALU.is_lt, op1=ALU.mult))
                    dve.wait_ge(s_cl, (b + m) * 64)
                    dve.nop(nofuse=True)
                    chain(dve.tensor_copy(prev_dst[:, :], own_dst[:, :]))
                    size_and_sort(k + 1)
                    new = lv.size(0)
                    build(new, c + n)
                    chain(dve.reciprocal(w_k[:, :], lst[:, :, 2]))
                    settle()
                    lv.next(n, c, m, b, new)

        with ExitStack() as ph, nc.Block() as block:
            def tmp(name, shape, dt=F32):
                return ph.enter_context(nc.sbuf_tensor(name, shape, dt))

            xin = tmp("d1_x", [P, 2, CH, D])
            yin = tmp("d1_y", [P, 2, CH, D])
            x = tmp("d1_out", [P, 2, CH, D])
            own = tmp("d1_own", [P, 2, CH, D])
            sq = tmp("d1_sq", [P, 2, CH, D])
            stat = tmp("d1_stat", [P, 2, 3, CH])
            ln = Norm("d1", x, sq, stat, 1)
            s_ld = [sem(f"d1_loaded{s}") for s in range(2)]
            s_st = [sem(f"d1_stored{s}") for s in range(2)]
            s_res = sem("d1_result")
            s_v = sem("d1_chain")

            @block.sync
            def _(sp):
                stream(sp, [(x1_t, D, xin), (y_t, D, yin)], [(x2_t, D, x), (agg2_t, D, own)], s_ld, s_res, s_st)

            @block.scalar
            def _(act):
                with act.Fori(0, NC // 2) as i:
                    ln.square(act, i, 0)

            @block.vector
            def _(dve):
                STEPS = 14
                with dve.Fori(0, NC // 2) as i:
                    did, need, n = chain_of(dve, s_v, i, STEPS)
                    at = [0, 0]
                    for s in range(2):
                        dve.wait_ge(s_ld[s], i * 32 + 32)
                        dve.wait_ge(s_st[s], i * 32)
                        at[s] = did(dve.tensor_tensor(
                            yin[:, s, :, :], yin[:, s, :, :],
                            dinv_n[:, bass.ds((i * 2 + s) * CH, CH)].unsqueeze(2).to_broadcast([P, CH, D]),
                            ALU.mult))
                    for s in range(2):
                        need(at[s])
                        at[s] = did(dve.scalar_tensor_tensor(
                            out=x[:, s, :, :].rearrange("p f d -> p (f d)"),
                            in0=xin[:, s, :, :].rearrange("p f d -> p (f d)"), scalar=qk[:, K + 1:K + 2],
                            in1=yin[:, s, :, :].rearrange("p f d -> p (f d)"), op0=ALU.mult, op1=ALU.add))
                    need(at[1])
                    ln.centre(dve, i, did, need, 0)
                    at = ln.scale(dve, i, did, need, 0)
                    for s in range(2):
                        need(at[s])
                        ins = dve.tensor_tensor(
                            own[:, s, :, :], x[:, s, :, :],
                            none_n[:, bass.ds((i * 2 + s) * CH, CH)].unsqueeze(2).to_broadcast([P, CH, D]),
                            ALU.mult).then_inc(s_res, 1)
                    assert n[0] == STEPS, n[0]

        own_rows = sb("own_rows", [P, T], I32)
        with ExitStack() as ph, nc.Block() as block:
            def tmp(name, shape, dt=F32):
                return ph.enter_context(nc.sbuf_tensor(name, shape, dt))

            keys = tmp("e2_keys", [P, TB // 2, GE], I32)
            same = tmp("e2_same", [P, TB, GE])
            junk = tmp("e2_junk", [P, TB, GE])
            rank = tmp("e2_rank", [P, TB])
            sidx = tmp("e2_sidx", [P, TB], I32)
            gidx = tmp("e2_gidx", [P, TB], I32)
            xg = tmp("e2_xg", [P, TB, D])
            xc = tmp("e2_xc", [P, TB, D])
            msg = tmp("e2_msg", [P, TB, D])
            rows = tmp("e2_rows", [P, TB, D])
            sum_p = ph.enter_context(nc.psum_tensor("e2_sum", [P, TB, 128], F32))
            s_key = sem("e2_keys_loaded")
            s_gx = sem("e2_rows_got")
            s_xc = sem("e2_rows_copied")
            s_gi = sem("e2_gather_index")
            s_same = sem("e2_same")
            s_si = sem("e2_scatter_index")
            s_msg = sem("e2_messages")
            s_sum = sem("e2_sums")
            s_rows = sem("e2_rows_ready")
            s_add = sem("e2_added")
            s_v = sem("e2_chain")

            @block.sync
            def _(sp):
                with sp.Fori(0, NB) as i:
                    sp.wait_ge(s_same, i)
                    sp.dma_start(keys[:, :, :].rearrange("p a b -> p (a b)"),
                                 a["dst_rows"][bass.ds(i, 1), :].partition_broadcast(P)).then_inc(s_key, 16)

            @block.gpsimd
            def _(pool):
                edge_dmas(pool, x2_t, agg2_t, xg, gidx, rows, sidx, s_gi, s_gx, s_xc, s_rows, s_si, s_add)

            @block.scalar
            def _(act):
                act.copy(gidx[:, :], src_i[:, 0:TB]).then_inc(s_gi, 1)
                with act.Fori(0, NB) as i:
                    act.wait_ge(s_gx, i * 64 + 64)
                    act.wait_ge(s_msg, i)
                    act.nop(nofuse=True)
                    act.copy(xc[:, :, :], xg[:, :, :]).then_inc(s_xc, 1)
                    act.copy(gidx[:, :], src_i[:, bass.ds(i * TB + TB, TB)]).then_inc(s_gi, 1)
                    act.wait_ge(s_sum, i + 1)
                    act.wait_ge(s_add, i * 64)
                    act.activation(rows[:, :, :], sum_p[:, :, 0:D], ACT.Copy).then_inc(s_rows, 1)

            @block.tensor
            def _(pe):
                with pe.Fori(0, NB) as i:
                    pe.wait_ge(s_msg, i + 1)
                    pe.wait_ge(s_rows, i)
                    pe.nop(nofuse=True)
                    group_sums(pe, sum_p, same, msg).then_inc(s_sum, 1)

            @block.vector
            def _(dve):
                STEPS = 3
                with dve.Fori(0, NB) as i:
                    n = [0]

                    def chain(ins):
                        n[0] += 1
                        ins.then_inc(s_v, 1)
                        dve.wait_ge(s_v, i * STEPS + n[0])

                    dve.wait_ge(s_key, i * 16 + 16)
                    dve.wait_ge(s_sum, i)
                    for u in range(TB):
                        dve.tensor_scalar(same[:, u, :], keys[:, u // 2, :], dst_f[:, bass.ds(i * TB + u, 1)],
                                          None, ALU.is_equal)
                    for u in range(TB):
                        ins = dve.scalar_tensor_tensor(out=junk[:, u, :], in0=keys[:, u // 2, :],
                                                       scalar=dst_f[:, bass.ds(i * TB + u, 1)],
                                                       in1=earlier[:, u % 2, :], op0=ALU.is_equal, op1=ALU.mult,
                                                       accum_out=rank[:, u:u + 1])
                    ins.then_inc(s_same, 1)
                    dve.wait_ge(s_same, i + 1)
                    chain(dve.scalar_tensor_tensor(out=rank[:, :], in0=rank[:, :], scalar=1.0, in1=sink[:, :],
                                                   op0=ALU.min, op1=ALU.mult))
                    chain(dve.tensor_tensor(rank[:, :], rank[:, :], dst_f[:, bass.ds(i * TB, TB)], ALU.max))
                    dve.tensor_copy(own_rows[:, bass.ds(i * TB, TB)], rank[:, :])
                    dve.wait_ge(s_add, i * 64)
                    dve.nop(nofuse=True)
                    dve.tensor_copy(sidx[:, :], rank[:, :]).then_inc(s_si, 1)
                    dve.wait_ge(s_xc, i + 1)
                    for u in range(TB):
                        ins = dve.tensor_scalar(
                            msg[:, u, :], xc[:, u, :],
                            srows[:, bass.ds(i * TB + u, 1), 2:3].rearrange("p a b -> p (a b)"), None, ALU.mult)
                    chain(ins)
                    dve.sem_inc(s_msg, 1)
                    assert n[0] == STEPS
                dve.wait_ge(s_add, NB * 64)

        with ExitStack() as ph, nc.Block() as block:
            def tmp(name, shape, dt=F32):
                return ph.enter_context(nc.sbuf_tensor(name, shape, dt))

            def ptmp(name, shape, dt=F32):
                return ph.enter_context(nc.psum_tensor(name, shape, dt))

            NG = CH // 8
            xin = tmp("d2_x", [P, 2, CH, D])
            agg = tmp("d2_agg", [P, 2, CH, D])
            x = tmp("d2_out", [P, 2, CH, D])
            sq = tmp("d2_sq", [P, 2, CH, D])
            stat = tmp("d2_stat", [P, 2, 3, CH])
            ht = tmp("d2_turned", [2 * D, 2, 4 * P])
            ht_p = ptmp("d2_turned_p", [P, 2, 512])
            hw_p = ptmp("d2_product", [P, 2, 512])
            ln = Norm("d2", x, sq, stat, 1)
            s_ld = [sem(f"d2_loaded{s}") for s in range(2)]
            s_st = [sem(f"d2_stored{s}") for s in range(2)]
            s_res = sem("d2_result")
            s_v = sem("d2_chain")
            s_h = sem("d2_h")
            s_ht = sem("d2_turned")
            s_hc = sem("d2_turned_copied")
            s_hw = sem("d2_product")
            s_hr = sem("d2_product_used")

            @block.sync
            def _(sp):
                stream(sp, [(x2_t, D, xin), (agg2_t, D, agg)], [(x3_t, D, x)], s_ld, s_res, s_st)

            @block.tensor
            def _(pe):
                def turn(i, s, g):
                    q = s * NG + g
                    if g == 0:
                        pe.wait_ge(s_h, i * 2 + s + 1)
                    if q < 2:
                        pe.wait_ge(s_hc, i * (2 * NG) + q)
                    else:
                        pe.wait_ge(s_hc, i * (2 * NG) + (q - 1))
                    pe.nop(nofuse=True)
                    for j in range(4):
                        pair = agg[:, s, 8 * g + 2 * j:8 * g + 2 * j + 2, :].rearrange("p f d -> p (f d)")
                        ins = pe.transpose(ht_p[0:2 * D, q % 2, j * P:(j + 1) * P], pair, ident[:, :])
                    ins.then_inc(s_ht, 1)

                def product(i, s, g):
                    q = s * NG + g
                    pe.wait_ge(s_hc, i * (2 * NG) + (q + 1))
                    pe.wait_ge(s_hr, i * (2 * NG) + (q + 1))
                    pe.nop(nofuse=True)
                    pe.matmul(hw_p[:, q % 2, 0:8 * D], onesrow[:, :], bl2[:, 0:8 * D], start=True, stop=False,
                              skip_group_check=True)
                    for j in range(4):
                        ins = pe.matmul(hw_p[:, q % 2, 2 * D * j:2 * D * (j + 1)], ht[:, q % 2, j * P:(j + 1) * P],
                                        wl2[:, :], start=False, stop=(j == 3), skip_group_check=True)
                    ins.then_inc(s_hw, 1)

                with pe.Fori(0, NC // 2) as i:
                    for s in range(2):
                        for g in range(NG):
                            turn(i, s, g)
                            product(i, s, g)

            @block.scalar
            def _(act):
                with act.Fori(0, NC // 2) as i:
                    for q in range(2 * NG):
                        act.wait_ge(s_ht, i * (2 * NG) + (q + 1))
                        if q >= 2:
                            act.wait_ge(s_hw, i * (2 * NG) + (q - 1))
                        else:
                            act.wait_ge(s_hw, i * (2 * NG))
                        act.activation(ht[:, q % 2, :], ht_p[0:2 * D, q % 2, :], ACT.Copy).then_inc(s_hc, 1)
                    ln.square(act, i, 0)

            @block.vector
            def _(dve):
                STEPS = 10
                dve.sem_inc(s_hr, 2)
                with dve.Fori(0, NC // 2) as i:
                    did, need, n = chain_of(dve, s_v, i, STEPS)
                    for s in range(2):
                        dve.wait_ge(s_ld[s], i * 32 + 32)
                        dve.tensor_tensor(
                            agg[:, s, :, :], agg[:, s, :, :],
                            cj_n[:, bass.ds((i * 2 + s) * CH, CH)].unsqueeze(2).to_broadcast([P, CH, D]),
                            ALU.mult).then_inc(s_h, 1)
                    for s in range(2):
                        dve.wait_ge(s_st[s], i * 16)
                        for g in range(NG):
                            dve.wait_ge(s_hw, i * (2 * NG) + (s * NG + g + 1))
                            grp = slice(8 * g, 8 * g + 8)
                            ins = dve.scalar_tensor_tensor(
                                out=x[:, s, grp, :].rearrange("p f d -> p (f d)"),
                                in0=hw_p[:, (s * NG + g) % 2, 0:8 * D], scalar=0.0,
                                in1=xin[:, s, grp, :].rearrange("p f d -> p (f d)"), op0=ALU.max, op1=ALU.add)
                            ins.then_inc(s_hr, 1)
                    dve.wait_ge(s_hr, i * (2 * NG) + (2 * NG + 2))
                    dve.nop(nofuse=True)
                    ln.centre(dve, i, did, need, 0)
                    at = ln.scale(dve, i, did, need, 0)
                    need(at[1])
                    dve.sem_inc(s_res, 2)
                    assert n[0] == STEPS, n[0]

        with ExitStack() as ph, nc.Block() as block:
            def tmp(name, shape, dt=F32):
                return ph.enter_context(nc.sbuf_tensor(name, shape, dt))

            def ptmp(name, shape, dt=F32):
                return ph.enter_context(nc.psum_tensor(name, shape, dt))

            NJ = NREL * D // P
            keys = tmp("e3_keys", [P, TB // 2, GE], I32)
            rel = tmp("e3_rel", [P, TB * P], I32)
            same = tmp("e3_same", [P, TB, GE])
            sidx = tmp("e3_sidx", [P, TB], I32)
            gidx = tmp("e3_gidx", [P, TB], I32)
            xg = tmp("e3_xg", [P, TB, D])
            xc = tmp("e3_xc", [P, TB, D])
            xt = tmp("e3_turned", [D, TB * P])
            hr = tmp("e3_hidden", [P, NJ, TB * P])
            hm = tmp("e3_masked", [P, NJ, TB * P])
            msg = tmp("e3_msg", [P, TB, D])
            rows = tmp("e3_rows", [P, TB, D])
            xt_p = ptmp("e3_turned_p", [P, TB, P])
            h_p = ptmp("e3_hidden_p", [P, NJ, TB * P])
            m_p = ptmp("e3_message_p", [P, TB, 128])
            sum_p = ptmp("e3_sum", [P, TB, 128])
            s_key = sem("e3_keys_loaded")
            s_gx = sem("e3_rows_got")
            s_xc = sem("e3_rows_copied")
            s_gi = sem("e3_gather_index")
            s_xt = sem("e3_rows_turned")
            s_xtc = sem("e3_turned_copied")
            s_hp = sem("e3_hidden_products")
            s_hr = sem("e3_hidden")
            s_hm = sem("e3_masked")
            s_mp = sem("e3_message_products")
            s_same = sem("e3_same")
            s_msg = sem("e3_messages")
            s_sum = sem("e3_sums")
            s_rows = sem("e3_rows_ready")
            s_si = sem("e3_scatter_index")
            s_add = sem("e3_added")

            @block.sync
            def _(sp):
                with sp.Fori(0, NB) as i:
                    sp.wait_ge(s_same, i)
                    sp.dma_start(keys[:, :, :].rearrange("p a b -> p (a b)"),
                                 a["dst_rows"][bass.ds(i, 1), :].partition_broadcast(P)).then_inc(s_key, 16)
                    sp.wait_ge(s_hm, i)
                    sp.dma_start(rel[:, :], a["rel_rows"][bass.ds(i, 1), :].partition_broadcast(P)
                                 ).then_inc(s_key, 16)

            @block.gpsimd
            def _(pool):
                pool.wait_ge(s_agg3, cleared(agg3_t))
                edge_dmas(pool, x3_t, agg3_t, xg, gidx, rows, sidx, s_gi, s_gx, s_xc, s_rows, s_si, s_add)

            @block.scalar
            def _(act):
                act.copy(gidx[:, :], src_i[:, 0:TB]).then_inc(s_gi, 1)
                with act.Fori(0, NB) as i:
                    act.wait_ge(s_gx, i * 64 + 64)
                    act.wait_ge(s_xt, i)
                    act.nop(nofuse=True)
                    act.copy(xc[:, :, :], xg[:, :, :]).then_inc(s_xc, 1)
                    act.copy(gidx[:, :], src_i[:, bass.ds(i * TB + TB, TB)]).then_inc(s_gi, 1)
                    act.wait_ge(s_xt, i + 1)
                    act.wait_ge(s_hp, i * NJ)
                    act.activation(xt[:, :], xt_p[0:D, :, :].rearrange("p a b -> p (a b)"),
                                   ACT.Copy).then_inc(s_xtc, 1)
                    for j in range(NJ):
                        act.wait_ge(s_hp, i * NJ + (j + 1))
                        act.wait_ge(s_hm, i)
                        act.activation(hr[:, j, :], h_p[:, j, :], ACT.Relu, bias=br1[:, j:j + 1]).then_inc(s_hr, 1)
                    act.wait_ge(s_sum, i + 1)
                    act.wait_ge(s_add, i * 64)
                    act.activation(rows[:, :, :], sum_p[:, :, 0:D], ACT.Copy).then_inc(s_rows, 1)

            @block.tensor
            def _(pe):
                with pe.Fori(0, NB) as i:
                    pe.wait_ge(s_xc, i + 1)
                    pe.wait_ge(s_xtc, i)
                    pe.nop(nofuse=True)
                    for u in range(TB):
                        ins = pe.transpose(xt_p[0:D, u, :], xc[:, u, :], ident[:, :])
                    ins.then_inc(s_xt, 1)
                    pe.wait_ge(s_xtc, i + 1)
                    pe.wait_ge(s_hr, i * NJ)
                    pe.nop(nofuse=True)
                    for j in range(NJ):
                        pe.matmul(h_p[:, j, :], wr1[:, j * P:(j + 1) * P], xt[:, :], start=True,
                                  stop=True).then_inc(s_hp, 1)
                    pe.wait_ge(s_hm, i + 1)
                    pe.wait_ge(s_msg, i)
                    pe.nop(nofuse=True)
                    for u in range(TB):
                        for j in range(NJ):
                            ins = pe.matmul(m_p[:, u, 0:D], hm[:, j, u * P:(u + 1) * P],
                                            wr2[:, j * D:(j + 1) * D], start=(j == 0), stop=(j == NJ - 1))
                    ins.then_inc(s_mp, 1)
                    pe.wait_ge(s_msg, i + 1)
                    pe.wait_ge(s_rows, i)
                    pe.nop(nofuse=True)
                    group_sums(pe, sum_p, same, msg).then_inc(s_sum, 1)

            @block.vector
            def _(dve):
                with dve.Fori(0, NB) as i:
                    dve.wait_ge(s_key, i * 32 + 32)
                    dve.wait_ge(s_sum, i)
                    for u in range(TB):
                        ins = dve.tensor_scalar(same[:, u, :], keys[:, u // 2, :],
                                                dst_f[:, bass.ds(i * TB + u, 1)], None, ALU.is_equal)
                    ins.then_inc(s_same, 1)
                    dve.wait_ge(s_add, i * 64)
                    dve.nop(nofuse=True)
                    dve.tensor_copy(sidx[:, :], own_rows[:, bass.ds(i * TB, TB)]).then_inc(s_si, 1)
                    dve.wait_ge(s_mp, i)
                    for j in range(NJ):
                        dve.wait_ge(s_hr, i * NJ + (j + 1))
                        ins = dve.scalar_tensor_tensor(out=hm[:, j, :], in0=rel[:, :], scalar=relc[:, j:j + 1],
                                                       in1=hr[:, j, :], op0=ALU.is_equal, op1=ALU.mult)
                    ins.then_inc(s_hm, 1)
                    dve.wait_ge(s_mp, i + 1)
                    for u in range(TB):
                        ins = dve.tensor_scalar(msg[:, u, :], m_p[:, u, 0:D], norm[:, bass.ds(i * TB + u, 1)],
                                                None, ALU.mult)
                    ins.then_inc(s_msg, 1)
                dve.wait_ge(s_add, NB * 64)

        with ExitStack() as ph, nc.Block() as block:
            def tmp(name, shape, dt=F32):
                return ph.enter_context(nc.sbuf_tensor(name, shape, dt))

            xin = tmp("d3_x", [P, 2, CH, D])
            agg = tmp("d3_agg", [P, 2, CH, D])
            x = tmp("d3_out", [P, 2, CH, D])
            sq = tmp("d3_sq", [P, 2, CH, D])
            stat = tmp("d3_stat", [P, 2, 3, CH])
            ln = Norm("d3", x, sq, stat, 1)
            s_ld = [sem(f"d3_loaded{s}") for s in range(2)]
            s_st = [sem(f"d3_stored{s}") for s in range(2)]
            s_res = sem("d3_result")
            s_v = sem("d3_chain")

            @block.sync
            def _(sp):
                stream(sp, [(x3_t, D, xin), (agg3_t, D, agg)], [(out, D, x)], s_ld, s_res, s_st)

            @block.scalar
            def _(act):
                with act.Fori(0, NC // 2) as i:
                    ln.square(act, i, 0)

            @block.vector
            def _(dve):
                STEPS = 14
                with dve.Fori(0, NC // 2) as i:
                    did, need, n = chain_of(dve, s_v, i, STEPS)
                    at = [0, 0]
                    for s in range(2):
                        dve.wait_ge(s_ld[s], i * 32 + 32)
                        at[s] = did(dve.tensor_tensor(agg[:, s, :, :], agg[:, s, :, :],
                                                      b3b[:, :].unsqueeze(1).to_broadcast([P, CH, D]), ALU.add))
                    for s in range(2):
                        need(at[s])
                        dve.wait_ge(s_st[s], i * 16)
                        at[s] = did(dve.scalar_tensor_tensor(
                            out=x[:, s, :, :].rearrange("p f d -> p (f d)"),
                            in0=agg[:, s, :, :].rearrange("p f d -> p (f d)"), scalar=0.0,
                            in1=xin[:, s, :, :].rearrange("p f d -> p (f d)"), op0=ALU.max, op1=ALU.add))
                    need(at[1])
                    ln.centre(dve, i, did, need, 0)
                    at = ln.scale(dve, i, did, need, 0)
                    need(at[1])
                    dve.sem_inc(s_res, 2)
                    assert n[0] == STEPS, n[0]




def arrange(inputs):
    get = {k: np.asarray(v) for k, v in inputs.items()}
    f32, i32 = np.float32, np.int32
    xz = np.zeros((NP, XW), i32)
    xz[:N, 0:D] = get["x"].view(i32)
    xz[:N, D] = get["node_vec"].view(i32)
    xz[:N, D + 1] = get["node_type_119"]
    kind = np.zeros(NP, i32)
    kind[:N] = get["node_type_119"]

    def edges(v, fill=0):
        full = np.zeros((EP,) + v.shape[1:], v.dtype)
        full[:E] = v
        if len(v.shape) == 1 and fill:
            full[E:] = fill
        return full.reshape((P, T) + v.shape[1:])

    def columns(v):
        return np.concatenate([v, np.zeros((P, TB), v.dtype)], 1)

    def by_step(v):
        return np.ascontiguousarray(v.T).reshape(NB, TB * P)

    src = edges(get["src"].astype(i32), SPARE_SRC)
    dst = edges(get["dst"].astype(i32), SPARE_DST)
    ea = edges(get["edge_attr_40"])
    rel = edges(get["edge_type_8"].astype(i32))
    w2 = get["L2_gnn_W"]
    wl2 = np.zeros((2 * D, 2 * D), f32)
    wl2[:D, :D] = w2.T
    wl2[D:, D:] = w2.T
    wr1, wr2, br1 = get["L3_gnn_weight1"], get["L3_gnn_weight2"], get["L3_gnn_bias1"]
    return {
        "xz": xz, "kind": kind.reshape(HI, LO),
        "src": columns(src), "dst": columns(dst), "src_rows": by_step(src), "dst_rows": by_step(dst),
        "rel_rows": by_step(rel),
        "ea": np.ascontiguousarray(ea.transpose(2, 1, 0)).reshape(R, T * P),
        "dist": edges(get["edge_weight"]), "norm": edges(get["edge_weight1"][:, 0]),
        "w1t": np.ascontiguousarray(get["L0_gnn_W1"].T), "b1": get["L0_gnn_b1"][:, None],
        "w2b": np.concatenate([get["L0_gnn_W2"].T, get["L0_gnn_b2"][None]], 0),
        "embt": np.ascontiguousarray(get["L0_gnn_emb"].T), "adwt": np.ascontiguousarray(get["L0_gnn_adaptW"].T),
        "gamma": get["L0_gnn_gamma"][None], "beta": get["L0_gnn_beta"][None],
        "jacobi": np.ascontiguousarray(jacobi_basis().T).reshape(1, -1),
        "lap": get["L1_gnn_lap_coefs"][None], "mf": get["L1_gnn_mf_weights"].reshape(1, -1),
        "wl2": wl2, "bl2": np.tile(get["L2_gnn_b"], 10)[None],
        "wr1": np.ascontiguousarray(wr1.transpose(1, 0, 2)).reshape(D, NREL * D),
        "br1": np.ascontiguousarray(np.tile(br1, NREL).reshape(3, P).T),
        "wr2": np.ascontiguousarray(wr2.reshape(3, P, D).transpose(1, 0, 2)).reshape(P, 3 * D),
        "relc": np.ascontiguousarray((np.arange(NREL * D) // D).astype(f32).reshape(3, P).T),
        "level": np.array([[(0 if k == 0 else 1 + (k - 1) % 2, 1 + k % 2) for k in range(K)]],
                          f32).reshape(1, -1) * NP,
        "b3": get["L3_gnn_bias2"][None],
    }


def kernel(**inputs):
    import concourse.bacc as bacc
    from concourse.bass_utils import run_bass_kernel_spmd

    nc = bacc.Bacc("TRN2", target_bir_lowering=False, num_devices=1)
    arrays = {"in_" + k: np.ascontiguousarray(v) for k, v in arrange(inputs).items()}
    a = {k[3:]: nc.dram_tensor(k, v.shape, mybir.dt.from_np(v.dtype), kind="ExternalInput").ap()
         for k, v in arrays.items()}
    out = nc.dram_tensor("out", (NP, D), F32, kind="ExternalOutput").ap()
    program(nc, a, out)
    r = run_bass_kernel_spmd(nc, [arrays], core_ids=[0])
    return r.results[0]["out"][:N]
```

```python
from contextlib import ExitStack

import numpy as np

import concourse.bass as bass
from concourse import mybir
from concourse.alu_op_type import AluOpType as ALU

ACT = mybir.ActivationFunctionType
AX = mybir.AxisListType
F32 = mybir.dt.float32
I32 = mybir.dt.int32
I16 = mybir.dt.int16
BF16 = mybir.dt.bfloat16
RMAX = bass.bass_isa.ReduceOp.max

P = 128
N = 100000
E = 25000
D = 48
R = 40
NEL = 119
G = 32
NREL = 8
K = 10
CUTOFF = 6.0
EPS = 1e-5

LO = 1024
HI = -(-N // LO)
NP = HI * LO
NF = NP // P
T = 8 * (-(-E // (8 * P)))
EP = T * P
TB = 4
NB = T // TB
GE = 2 * P
SPARE_SRC, SPARE_DST = N, N + 1
SINK = N + 8
XW = D + 2
AW = D + 1
FILL = 42 * D
CH = 56
NC = NF // CH
PI = float(np.pi)
assert NP == P * NF and NF % (2 * CH) == 0 and SINK + GE <= NP
assert T % 20 == 0


def jacobi_basis():
    import math
    a = b = 1.0
    rows = np.zeros((K + 1, K + 1))
    rows[0, 0] = 1.0
    rows[1, 0], rows[1, 1] = (a - b) / 2.0, (a + b + 2.0) / 2.0
    for n in range(2, K + 1):
        nab = 2 * n + a + b
        an = nab * (nab - 1) * (nab - 2) / (2 * n * (nab - n) * (nab - 2))
        bn = (nab - 1) * (a * a - b * b) / (2 * n * (nab - n) * (nab - 2))
        cn = -(2 * (n + a - 1) * (n + b - 1) * nab) / (2 * n * (nab - n) * (nab - 2))
        rows[n] = bn * rows[n - 1] + cn * rows[n - 2]
        rows[n, 1:] += an * rows[n - 1, :-1]
    for i in range(K + 1):
        t1 = math.pow(2.0, a + b + 1) / (2 * i + a + b + 1)
        t2 = math.exp(math.lgamma(i + a + 1) - math.lgamma(i + a + b + 1))
        t3 = math.exp(math.lgamma(i + b + 1) - math.lgamma(i + 1))
        rows[i] /= math.sqrt(t1 * t2 * t3)
    return rows.astype(np.float32)


def program(nc, a, out):
    with ExitStack() as ctx:
        def sb(name, shape, dt=F32):
            return ctx.enter_context(nc.sbuf_tensor(name, shape, dt))

        def psum(name, shape, dt=F32):
            return ctx.enter_context(nc.psum_tensor(name, shape, dt))

        def sem(name):
            return ctx.enter_context(nc.semaphore(name))

        def table(name, rows, width):
            return nc.dram_tensor(name, [rows, width], F32, kind="Internal").ap()

        xz_t = a["xz"]
        srow_t = table("srow_t", NP, 2)
        indeg_t = table("indeg_t", NP, 1)
        agg0_t = table("agg0_t", NP, AW)
        pow_t = table("pow_t", 3 * NP, D)
        y_t = table("y_t", NP, D)
        agg2_t = table("agg2_t", NP, D)
        agg3_t = table("agg3_t", NP, D)
        x2_t = table("x2_t", NP, D)
        x3_t = table("x3_t", NP, D)
        edge_t = table("edge_t", EP + 1, 4)
        x1_t = pow_t[0:NP, :]

        ident = sb("ident", [P, P])
        iota_lo = sb("iota_lo", [P, LO], I16)
        earlier = sb("earlier", [P, 2, GE])
        zeros = sb("zeros", [P, FILL])
        bias3 = sb("bias3", [P, FILL])
        sink = sb("sink", [P, TB])
        src_i = sb("src_i", [P, T + TB], I32)
        dst_i = sb("dst_i", [P, T + TB], I32)
        src_f = sb("src_f", [P, T])
        dst_f = sb("dst_f", [P, T])
        kind_s = sb("kind_s", [P, T])
        srows = sb("srows", [P, T, 2])
        dist = sb("dist", [P, T])
        cutw = sb("cutw", [P, T])
        norm = sb("norm", [P, T])
        w1t = sb("w1t", [R, D])
        b1c = sb("b1c", [D, 1])
        w2b = sb("w2b", [D + 1, D])
        embt = sb("embt", [G, NEL])
        adwt = sb("adwt", [G, G])
        vmat = sb("vmat", [G, NEL])
        kindm = sb("kindm", [NEL, NEL])
        gammab = sb("gammab", [P, D])
        betab = sb("betab", [P, D])
        halfpi = sb("halfpi", [P, 1])
        jac = sb("jac", [P, (K + 1) * (K + 1)])
        coef = sb("coef", [P, 6, K + 1])
        qk = sb("qk", [P, K + 2])
        wl2 = sb("wl2", [2 * D + 1, 2 * D])
        wr1 = sb("wr1", [D, NREL * D])
        br1 = sb("br1", [P, 3])
        wr2 = sb("wr2", [P, 3 * D])
        relc = sb("relc", [P, 3])
        b3b = sb("b3b", [P, D])

        s_ix = sem("indices_loaded")
        s_w = sem("weights_loaded")
        s_c = sem("constants_made")
        s_z = sem("zeros_made")
        s_agg0 = sem("agg0_cleared")
        s_pow = sem("power_tables_cleared")
        s_y = sem("filter_table_cleared")
        s_agg3 = sem("agg3_cleared")

        def fill(eng, tbl, tile, done):
            cols = tbl.shape[0] * tbl.shape[1] // P
            flat = tbl.rearrange("a b -> (a b)").rearrange("(p c) -> p c", p=P)
            for c0 in range(0, cols, FILL):
                w = min(FILL, cols - c0)
                eng.dma_start(flat[:, c0:c0 + w], tile[:, 0:w]).then_inc(done, 16)

        def filled(tbl):
            return 16 * (-(-(tbl.shape[0] * tbl.shape[1] // P) // FILL))

        WEIGHTS = [(w1t, "w1t"), (b1c, "b1"), (w2b, "w2b"), (embt, "embt"), (adwt, "adwt"),
                   (gammab, "gamma"), (betab, "beta"), (jac, "jacobi"), (coef[:, 0, :], "lap"),
                   (coef[:, 1, :], "mf"), (wl2, "wl2"), (wr1, "wr1"), (br1, "br1"),
                   (wr2, "wr2"), (relc, "relc"), (b3b, "b3"), (dist, "dist"), (norm, "norm")]
        BROADCAST = ("gamma", "beta", "jacobi", "lap", "mf", "b3")

        SR = 10

        with ExitStack() as ph, nc.Block() as block:
            def tmp(name, shape, dt=F32):
                return ph.enter_context(nc.sbuf_tensor(name, shape, dt))

            digit = tmp("digit", [P, 4, T], I32)
            digit_f = tmp("digit_f", [P, 4, T])
            hot_hi = tmp("hot_hi", [P, TB, 2, HI], BF16)
            hot_lo = tmp("hot_lo", [P, TB, 2, LO], BF16)
            srow = tmp("srow", [HI, LO, 2])
            stage = tmp("kind_stage", [P, 2, SR], I32)
            ring = tmp("kind_ring", [P, 2, SR], I32)
            kinds = tmp("kinds", [P, T], I32)
            indeg = tmp("indeg", [HI, LO])
            outdeg = tmp("outdeg", [HI, LO])
            deg_p = ph.enter_context(nc.psum_tensor("deg_p", [P, 2, LO], F32))
            mat_p = ph.enter_context(nc.psum_tensor("mat_p", [P, 512], F32))
            mat2_p = ph.enter_context(nc.psum_tensor("mat2_p", [P, 512], F32))
            s_dig = sem("digits_chain")
            s_hot = sem("onehots_made")
            s_hotu = sem("onehots_used")
            s_degz = sem("degrees_started")
            s_m = sem("kind_matrix")
            s_mc = sem("kind_matrix_copied")
            s_srow = sem("source_rows_made")
            s_sq = sem("outdegree_root")
            s_coef = sem("coefficients")
            s_st = sem("source_rows_stored")
            s_cut = sem("cutoff_weights")
            s_kst = sem("kind_index_staged")
            s_kg = [sem(f"kinds_got{h}") for h in range(2)]
            s_kd = sem("kinds_done")

            @block.sync
            def _(sp):
                sp.dma_start(src_i[:, :], a["src"]).then_inc(s_ix, 16)
                sp.dma_start(dst_i[:, :], a["dst"]).then_inc(s_ix, 16)
                for tile, name in WEIGHTS:
                    src = a[name].partition_broadcast(P) if name in BROADCAST else a[name]
                    dst = tile if isinstance(tile, bass.AP) else tile[:, :]
                    sp.dma_start(dst, src).then_inc(s_w, 16)
                sp.wait_ge(s_z, 1)
                fill(sp, agg0_t, zeros, s_agg0)
                fill(sp, pow_t[NP:, :], zeros, s_pow)
                sp.wait_ge(s_srow, 2)
                sp.dma_start(srow_t.rearrange("(h l) c -> h (l c)", h=HI),
                             srow[:, :, :].rearrange("h l c -> h (l c)")).then_inc(s_st, 16)
                sp.dma_start(indeg_t.rearrange("(h l) c -> h (l c)", h=HI), indeg[:, :]).then_inc(s_st, 16)
                sp.wait_ge(s_st, 32)

            @block.gpsimd
            def _(pool):
                pool.iota(iota_lo[:, :], pattern=[[1, LO]], base=0, channel_multiplier=0).then_inc(s_c, 1)
                pool.memset(ident[:, :], 0.0).then_inc(s_c, 1)
                pool.memset(earlier[:, :, :], 1.0).then_inc(s_c, 1)
                pool.iota(sink[:, :], pattern=[[0, TB // 2], [P, 2]], base=SINK, channel_multiplier=1,
                          allow_small_or_imprecise_dtypes=True).then_inc(s_c, 1)
                pool.wait_ge(s_c, 4)
                pool.affine_select(out=ident[:, :], in_=ident[:, :], compare_op=ALU.not_equal, fill=1.0,
                                   base=0, pattern=[[-1, P]], channel_multiplier=1).then_inc(s_c, 1)
                for u in range(2):
                    pool.affine_select(out=earlier[:, u, :], in_=earlier[:, u, :], compare_op=ALU.is_gt,
                                       fill=0.0, base=u * P, pattern=[[-1, GE]],
                                       channel_multiplier=1).then_inc(s_c, 1)
                with pool.Fori(0, T // (2 * SR)) as i:
                    for h in range(2):
                        pool.wait_ge(s_kst, i * 2 + h + 1)
                        pool.nop(nofuse=True)
                        for u in range(SR):
                            pool.indirect_dma_start(
                                out=ring[:, h, u:u + 1], out_offset=None, in_=a["kind"],
                                in_offset=bass.IndirectOffsetOnAxis(ap=stage[:, h, u:u + 1], axis=0),
                            ).then_inc(s_kg[h], 16)

            @block.vector
            def _(dve):
                n = [0]

                def link(ins):
                    n[0] += 1
                    ins.then_inc(s_dig, 1)
                    dve.wait_ge(s_dig, n[0])

                dve.memset(zeros[:, :], 0.0).then_inc(s_z, 1)
                dve.memset(halfpi[:, :], PI / 2).then_inc(s_z, 1)
                dve.wait_ge(s_ix, 32)
                for j, ids in ((0, src_i), (2, dst_i)):
                    link(dve.tensor_scalar(digit[:, j, :], ids[:, 0:T], 10, None, ALU.logical_shift_right))
                    link(dve.tensor_scalar(digit[:, j + 1, :], ids[:, 0:T], LO - 1, None, ALU.bitwise_and))
                link(dve.tensor_copy(digit_f[:, :, :], digit[:, :, :]))
                link(dve.tensor_copy(src_f[:, :], src_i[:, 0:T]))
                link(dve.tensor_copy(dst_f[:, :], dst_i[:, 0:T]))
                dve.wait_ge(s_c, 7)
                dve.sem_inc(s_hotu, TB)
                with dve.Fori(0, NB) as i:
                    for u in range(TB):
                        for j in range(2):
                            if j == 0:
                                dve.wait_ge(s_hotu, i * TB + u + 1)
                            dve.tensor_scalar(hot_hi[:, u, j, :], iota_lo[:, 0:HI],
                                              digit_f[:, 2 * j, bass.ds(i * TB + u, 1)], None, ALU.is_equal)
                            ins = dve.tensor_scalar(hot_lo[:, u, j, :], iota_lo[:, :],
                                                    digit_f[:, 2 * j + 1, bass.ds(i * TB + u, 1)], None,
                                                    ALU.is_equal)
                        ins.then_inc(s_hot, 1)
                dve.wait_ge(s_w, 16 * len(WEIGHTS))
                link(dve.tensor_scalar(cutw[:, :], dist[:, :], CUTOFF, None, ALU.min))
                dve.sem_inc(s_cut, 1)
                dve.wait_ge(s_cut, 2)
                link(dve.tensor_scalar(cutw[:, :], cutw[:, :], 1.0, 0.5, ALU.add, ALU.mult))
                link(dve.tensor_scalar(dist[:, :], dist[:, :], CUTOFF, None, ALU.is_lt))
                link(dve.tensor_tensor(cutw[:, :], cutw[:, :], dist[:, :], ALU.mult))
                dve.wait_ge(s_m, 1)
                dve.tensor_copy(vmat[:, :], mat_p[0:G, 0:NEL]).then_inc(s_mc, 1)
                dve.wait_ge(s_m, 2)
                link(dve.tensor_copy(kindm[:, :], mat2_p[0:NEL, 0:NEL]))
                dve.wait_ge(s_coef, 1)
                link(dve.tensor_copy(coef[:, 3, 0:1], coef[:, 2, 0:1]))
                for i in range(1, K):
                    link(dve.tensor_tensor(coef[:, 3, i:i + 1], coef[:, 3, i - 1:i], coef[:, 2, i:i + 1],
                                           ALU.mult))
                link(dve.tensor_copy(coef[:, 4, 0:1], coef[:, 1, 0:1]))
                link(dve.tensor_tensor(coef[:, 4, 1:K + 1], coef[:, 1, 1:K + 1], coef[:, 3, 0:K], ALU.mult))
                jv = jac[:, :].rearrange("p (k i) -> p k i", i=K + 1)
                link(dve.tensor_tensor(jv, jv, coef[:, 4:5, :].to_broadcast([P, K + 1, K + 1]), ALU.mult))
                link(dve.tensor_reduce(qk[:, 0:K + 1], jv, AX.X, ALU.add))
                link(dve.tensor_scalar(qk[:, K + 1:K + 2], qk[:, 0:1], 1.0, None, ALU.add))
                dve.wait_ge(s_hotu, T + TB)
                link(dve.tensor_copy(srow[:, :, 0:1].rearrange("h l c -> h (l c)"), deg_p[0:HI, 1, :]))
                link(dve.tensor_scalar(outdeg[:, :], deg_p[0:HI, 0, :], 1.0, None, ALU.max))
                link(dve.reciprocal(outdeg[:, :], outdeg[:, :]))
                dve.sem_inc(s_sq, 1)
                dve.tensor_copy(indeg[:, :], deg_p[0:HI, 1, :]).then_inc(s_srow, 1)
                link(dve.tensor_copy(bias3[:, :].rearrange("p (n d) -> p n d", d=D),
                                     b3b[:, :].unsqueeze(1).to_broadcast([P, FILL // D, D])))
                dve.wait_ge(s_kd, T // SR)
                link(dve.tensor_copy(kind_s[:, :], kinds[:, :]))
                dve.wait_ge(s_sq, 2)

            @block.scalar
            def _(act):
                act.wait_ge(s_ix, 32)
                for h in range(2):
                    act.copy(stage[:, h, :], src_i[:, h * SR:(h + 1) * SR]).then_inc(s_kst, 1)
                with act.Fori(0, T // (2 * SR) - 1) as i:
                    for h in range(2):
                        act.wait_ge(s_kg[h], i * (16 * SR) + 16 * SR)
                        act.nop(nofuse=True)
                        act.copy(kinds[:, bass.ds((i * 2 + h) * SR, SR)], ring[:, h, :]).then_inc(s_kd, 1)
                        act.wait_ge(s_kd, i * 2 + h + 1)
                        act.nop(nofuse=True)
                        act.copy(stage[:, h, :], src_i[:, bass.ds((i * 2 + h + 2) * SR, SR)]).then_inc(s_kst, 1)
                for h in range(2):
                    act.wait_ge(s_kg[h], T // 2 * 16)
                    act.copy(kinds[:, T - (2 - h) * SR:T - (1 - h) * SR], ring[:, h, :]).then_inc(s_kd, 1)
                act.wait_ge(s_w, 16 * len(WEIGHTS))
                act.wait_ge(s_z, 2)
                act.wait_ge(s_cut, 1)
                act.activation(cutw[:, :], cutw[:, :], ACT.Sin, bias=halfpi[:, 0:1],
                               scale=-PI / CUTOFF).then_inc(s_cut, 1)
                act.activation(coef[:, 2, :], coef[:, 0, :], ACT.Tanh).then_inc(s_coef, 1)
                act.wait_ge(s_sq, 1)
                act.activation(srow[:, :, 1:2].rearrange("h l c -> h (l c)"), outdeg[:, :],
                               ACT.Sqrt).then_inc(s_sq, 1)
                act.wait_ge(s_sq, 2)
                act.sem_inc(s_srow, 1)

            @block.tensor
            def _(pe):
                pe.wait_ge(s_z, 1)
                for j in range(2):
                    for h in range(2):
                        pe.matmul(deg_p[0:HI, j, 512 * h:512 * h + 512], zeros[:, 0:HI],
                                  zeros[:, 0:512], start=True, stop=False, skip_group_check=True)
                with pe.Fori(0, NB) as i:
                    for u in range(TB):
                        pe.wait_ge(s_hot, i * TB + u + 1)
                        pe.nop(nofuse=True)
                        for j in range(2):
                            for h in range(2):
                                ins = pe.matmul(deg_p[0:HI, j, 512 * h:512 * h + 512], hot_hi[:, u, j, :],
                                                hot_lo[:, u, j, 512 * h:512 * h + 512], start=False,
                                                stop=False, skip_group_check=True)
                        ins.then_inc(s_hotu, 1)
                pe.wait_ge(s_w, 16 * len(WEIGHTS))
                pe.matmul(mat_p[0:G, 0:NEL], adwt[:, :], embt[:, :], start=True, stop=True).then_inc(s_m, 1)
                pe.wait_ge(s_mc, 1)
                pe.matmul(mat2_p[0:NEL, 0:NEL], embt[:, :], vmat[:, :], start=True, stop=True).then_inc(s_m, 1)

        def later(i):
            return not isinstance(i, int) or i > 0

        def exists(i):
            return not isinstance(i, int) or i < NB

        def edge_dmas(pool, xt, aggt, xg, gidx, rows, sidx, s_gi, s_gx, s_rows, s_si, s_add, lead=2):
            def gather(s, u):
                pool.indirect_dma_start(
                    out=xg[:, s, u, :], out_offset=None, in_=xt,
                    in_offset=bass.IndirectOffsetOnAxis(ap=gidx[:, s, u:u + 1], axis=0)).then_inc(s_gx[s], 16)

            def add(s, u):
                pool.indirect_dma_start(
                    out=aggt, out_offset=bass.IndirectOffsetOnAxis(ap=sidx[:, s, u:u + 1], axis=0),
                    in_=rows[:, s, u, :], in_offset=None, compute_op=ALU.add).then_inc(s_add[s], 16)

            def step(q, s):
                i = q * 2 + s
                pool.wait_ge(s_si, i + 1)
                pool.wait_ge(s_rows, i + 2)
                if later(i):
                    pool.wait_ge(s_add[1 - s], (q + s) * 64)
                pool.nop(nofuse=True)
                for g in range(2):
                    if g == 1:
                        pool.wait_ge(s_add[s], q * 64 + 32)
                        pool.nop(nofuse=True)
                    add(s, 2 * g)
                    add(s, 2 * g + 1)
                    if exists(i + lead):
                        if g == 0:
                            pool.wait_ge(s_gi, i + (lead + 1))
                            pool.nop(nofuse=True)
                        gather((s + lead) % 2, 2 * g)
                        gather((s + lead) % 2, 2 * g + 1)

            for j in range(lead):
                pool.wait_ge(s_gi, j + 1)
                for u in range(TB):
                    gather(j % 2, u)
            step(0, 0)
            step(0, 1)
            with pool.Fori(1, NB // 2 - 2) as q:
                step(q, 0)
                step(q, 1)
            for i in range(NB - 4, NB):
                step(i // 2, i % 2)

        def group_sums(pe, sum_p, same, msg):
            width = msg.shape[2]
            for g in range(TB // 2):
                for c in range(2):
                    for r in range(2):
                        ins = pe.matmul(sum_p[:, 2 * g + c, 0:width],
                                        same[:, 2 * g + r, c * P:(c + 1) * P], msg[:, 2 * g + r, :],
                                        start=(r == 0), stop=(r == 1))
            return ins

        with ExitStack() as ph, nc.Block() as block:
            def tmp(name, shape, dt=F32):
                return ph.enter_context(nc.sbuf_tensor(name, shape, dt))

            def ptmp(name, shape, dt=F32):
                return ph.enter_context(nc.psum_tensor(name, shape, dt))

            iota_f = tmp("iota_f", [P, NEL])
            keys = tmp("keys", [P, 2, TB // 2, GE], I32)
            same = tmp("same", [P, 2, TB, GE])
            junk = tmp("junk", [P, TB, GE])
            junk2 = tmp("junk2", [P, TB, NEL])
            rank = tmp("rank", [P, TB])
            sidx = tmp("sidx", [P, 2, TB], I32)
            gidx = tmp("gidx", [P, 2, TB], I32)
            xg = tmp("xg", [P, 2, TB, XW])
            kind_d = tmp("kind_d", [P, TB])
            hot = tmp("hot", [P, TB, NEL])
            hot_t = tmp("hot_t", [NEL, TB, P])
            logit = tmp("logit", [P, TB])
            wgt = tmp("wgt", [P, TB])
            gated = tmp("gated", [P, TB, D])
            msg = tmp("msg", [P, TB, AW])
            rows = tmp("rows", [P, 2, TB, AW])
            ea = tmp("ea", [R, 2, TB * P])
            hid = tmp("hid", [D + 1, TB * P])
            hid_p = ptmp("hid_p", [P, 512])
            gate_p = ptmp("gate_p", [P, 2, TB, 128])
            hott_p = ptmp("hott_p", [P, TB, P])
            logit_p = ptmp("logit_p", [P, 2, TB, 128])
            sum_p = ptmp("sum_p", [P, TB, 128])
            s_ea = [sem(f"l0_edge_features{s}") for s in range(2)]
            s_key = [sem(f"l0_keys{s}") for s in range(2)]
            s_gx = [sem(f"l0_target_rows_got{s}") for s in range(2)]
            s_gi = sem("l0_gather_index")
            s_hp = sem("l0_hidden_product")
            s_hid = sem("l0_hidden")
            s_gate = sem("l0_gate")
            s_hot = sem("l0_onehots")
            s_hott = sem("l0_onehots_turned")
            s_hotc = sem("l0_turned_copied")
            s_lg = sem("l0_logit_rows")
            s_same = sem("l0_same")
            s_si = sem("l0_scatter_index")
            s_msg = sem("l0_messages")
            s_sum = sem("l0_sums")
            s_rows = sem("l0_rows")
            s_add = [sem(f"l0_added{s}") for s in range(2)]
            s_v = sem("l0_vector_chain")
            s_one = sem("l0_ones")

            @block.sync
            def _(sp):
                sp.sem_inc(s_hp, 1)
                sp.sem_inc(s_same, 1)
                with sp.Fori(0, NB // 2) as q:
                    for s in range(2):
                        i = q * 2 + s
                        sp.wait_ge(s_hp, i)
                        sp.dma_start(ea[:, s, :], a["ea"][:, bass.ds(i * (TB * P), TB * P)]).then_inc(s_ea[s], 16)
                        sp.wait_ge(s_same, i)
                        sp.dma_start(keys[:, s, :, :].rearrange("p a b -> p (a b)"),
                                     a["src_rows"][bass.ds(i, 1), :].partition_broadcast(P)).then_inc(s_key[s], 16)

            @block.gpsimd
            def _(pool):
                pool.iota(iota_f[:, :], pattern=[[1, NEL]], base=0, channel_multiplier=0,
                          allow_small_or_imprecise_dtypes=True).then_inc(s_one, 1)
                pool.wait_ge(s_agg0, filled(agg0_t))
                edge_dmas(pool, xz_t.bitcast(F32), agg0_t, xg, gidx, rows, sidx, s_gi, s_gx, s_rows, s_si, s_add)

            @block.scalar
            def _(act):
                def front(j):
                    act.wait_ge(s_hp, j + 2)
                    if later(j):
                        act.wait_ge(s_gate, j)
                    act.activation(hid[0:D, :], hid_p[0:D, :], ACT.Silu, bias=b1c[:, 0:1]).then_inc(s_hid, 1)
                    act.wait_ge(s_hott, j + 1)
                    if later(j):
                        act.wait_ge(s_lg, j)
                    act.activation(hot_t[:, :, :], hott_p[0:NEL, :, :], ACT.Copy).then_inc(s_hotc, 1)

                def step(q, s):
                    i = q * 2 + s
                    if exists(i + 1):
                        front(i + 1)
                    if exists(i + 2):
                        act.wait_ge(s_gx[s], q * 64 + 64)
                        act.nop(nofuse=True)
                        act.copy(gidx[:, s, :], dst_i[:, bass.ds((i + 2) * TB, TB)]).then_inc(s_gi, 1)
                    act.wait_ge(s_sum, i + 2)
                    if later(q):
                        act.wait_ge(s_add[s], q * 64)
                    act.activation(rows[:, s, :, :], sum_p[:, :, 0:AW], ACT.Copy).then_inc(s_rows, 1)

                act.sem_inc(s_rows, 1)
                for s in range(2):
                    act.copy(gidx[:, s, :], dst_i[:, s * TB:(s + 1) * TB]).then_inc(s_gi, 1)
                act.wait_ge(s_one, 2)
                front(0)
                step(0, 0)
                step(0, 1)
                with act.Fori(1, NB // 2 - 2) as q:
                    step(q, 0)
                    step(q, 1)
                for i in range(NB - 4, NB):
                    step(i // 2, i % 2)

            @block.tensor
            def _(pe):
                def front(qj, s):
                    j = qj * 2 + s
                    pe.wait_ge(s_ea[s], qj * 16 + 16)
                    if later(j):
                        pe.wait_ge(s_hid, j)
                        pe.wait_ge(s_hotc, j)
                    pe.nop(nofuse=True)
                    pe.matmul(hid_p[0:D, :], w1t[:, :], ea[:, s, :], start=True, stop=True).then_inc(s_hp, 1)
                    pe.wait_ge(s_hot, j + 1)
                    pe.nop(nofuse=True)
                    for u in range(TB):
                        ins = pe.transpose(hott_p[0:NEL, u, :], hot[:, u, :], ident[:, :])
                    ins.then_inc(s_hott, 1)
                    pe.wait_ge(s_hid, j + 1)
                    if later(j):
                        pe.wait_ge(s_msg, j)
                    pe.nop(nofuse=True)
                    for u in range(TB):
                        ins = pe.matmul(gate_p[:, s, u, 0:D], hid[:, u * P:(u + 1) * P], w2b[:, :],
                                        start=True, stop=True)
                    ins.then_inc(s_gate, 1)
                    pe.wait_ge(s_hotc, j + 1)
                    pe.nop(nofuse=True)
                    for u in range(TB):
                        ins = pe.matmul(logit_p[:, s, u, 0:NEL], hot_t[:, u, :], kindm[:, :], start=True, stop=True)
                    ins.then_inc(s_lg, 1)

                def step(q, s):
                    i = q * 2 + s
                    if exists(i + 1):
                        front(q + s, 1 - s)
                    pe.wait_ge(s_msg, i + 2)
                    pe.wait_ge(s_rows, i + 1)
                    pe.nop(nofuse=True)
                    group_sums(pe, sum_p, same[:, s, :, :], msg).then_inc(s_sum, 1)

                pe.sem_inc(s_sum, 1)
                front(0, 0)
                step(0, 0)
                step(0, 1)
                with pe.Fori(1, NB // 2 - 2) as q:
                    step(q, 0)
                    step(q, 1)
                for i in range(NB - 4, NB):
                    step(i // 2, i % 2)

            @block.vector
            def _(dve):
                STEPS = 5
                n = [0, 0]

                def chain(ins):
                    n[0] += 1
                    ins.then_inc(s_v, 1)
                    dve.wait_ge(s_v, n[1] + n[0])

                def onehots(j):
                    if later(j):
                        dve.wait_ge(s_hott, j)
                    for u in range(TB):
                        ins = dve.tensor_scalar(hot[:, u, :], iota_f[:, :],
                                                kind_s[:, bass.ds(j * TB + u, 1)], None, ALU.is_equal)
                    ins.then_inc(s_hot, 1)

                def matrices(qj, s):
                    j = qj * 2 + s
                    dve.wait_ge(s_key[s], qj * 16 + 16)
                    if later(j):
                        dve.wait_ge(s_sum, j)
                    for u in range(TB):
                        dve.tensor_scalar(same[:, s, u, :], keys[:, s, u // 2, :], src_f[:, bass.ds(j * TB + u, 1)],
                                          None, ALU.is_equal)
                    for u in range(TB):
                        ins = dve.scalar_tensor_tensor(out=junk[:, u, :], in0=keys[:, s, u // 2, :],
                                                       scalar=src_f[:, bass.ds(j * TB + u, 1)],
                                                       in1=earlier[:, u % 2, :], op0=ALU.is_equal, op1=ALU.mult,
                                                       accum_out=rank[:, u:u + 1])
                    ins.then_inc(s_same, 1)
                    dve.wait_ge(s_same, j + 2)
                    chain(dve.scalar_tensor_tensor(out=rank[:, :], in0=rank[:, :], scalar=1.0, in1=sink[:, :],
                                                   op0=ALU.min, op1=ALU.mult))
                    if later(qj):
                        dve.wait_ge(s_add[s], qj * 64)
                    dve.tensor_tensor(sidx[:, s, :], rank[:, :], src_f[:, bass.ds(j * TB, TB)],
                                      ALU.max).then_inc(s_si, 1)

                def step(q, s):
                    i = q * 2 + s
                    if exists(i + 1):
                        onehots(i + 1)
                    dve.wait_ge(s_gx[s], q * 64 + 64)
                    dve.wait_ge(s_sum, i + 1)
                    dve.tensor_tensor(wgt[:, :], cutw[:, bass.ds(i * TB, TB)], xg[:, s, :, D], ALU.mult)
                    dve.tensor_copy(msg[:, :, D], xg[:, s, :, D])
                    chain(dve.tensor_copy(kind_d[:, :], xg[:, s, :, D + 1].bitcast(I32)))
                    dve.wait_ge(s_lg, i + 1)
                    for u in range(TB):
                        ins = dve.scalar_tensor_tensor(out=junk2[:, u, :], in0=iota_f[:, :],
                                                       scalar=kind_d[:, u:u + 1], in1=logit_p[:, s, u, 0:NEL],
                                                       op0=ALU.is_equal, op1=ALU.mult,
                                                       accum_out=logit[:, u:u + 1])
                    chain(ins)
                    dve.wait_ge(s_gate, i + 1)
                    for u in range(TB):
                        ins = dve.scalar_tensor_tensor(out=gated[:, u, :], in0=gate_p[:, s, u, 0:D],
                                                       scalar=logit[:, u:u + 1], in1=xg[:, s, u, 0:D],
                                                       op0=ALU.add, op1=ALU.mult)
                    chain(ins)
                    for u in range(TB):
                        ins = dve.tensor_scalar(msg[:, u, 0:D], gated[:, u, :], wgt[:, u:u + 1], None, ALU.mult)
                    chain(ins)
                    dve.sem_inc(s_msg, 1)
                    if exists(i + 1):
                        matrices(q + s, 1 - s)

                dve.sem_inc(s_msg, 1)
                dve.memset(hid[:, :], 1.0).then_inc(s_one, 1)
                dve.wait_ge(s_one, 2)
                onehots(0)
                matrices(0, 0)
                step(0, 0)
                step(0, 1)
                first = n[0]
                with dve.Fori(1, NB // 2 - 2) as q:
                    n[:] = [first, (q - 1) * (2 * STEPS)]
                    step(q, 0)
                    step(q, 1)
                    assert n[0] == first + 2 * STEPS
                n[:] = [first, (NB // 2 - 3) * (2 * STEPS)]
                for i in range(NB - 4, NB):
                    step(i // 2, i % 2)
                for s in range(2):
                    dve.wait_ge(s_add[s], NB // 2 * 64)

        indeg_n = sb("indeg_n", [P, NF])
        cj_n = sb("cj_n", [P, NF])
        dinv_n = sb("dinv_n", [P, NF])
        none_n = sb("none_n", [P, NF])

        s_ld = [sem(f"nodes_loaded{s}") for s in range(2)]

        def loaded(dense, i):
            return i * 32 + (dense * (16 * NC) + 32)

        def nodes(tbl, c, width):
            return tbl.rearrange("(p f) d -> p (f d)", p=P)[:, bass.ds(c * (CH * width), CH * width)]

        def stream(sp, loads, stores, s_res, s_st):
            def load(c, s):
                for tbl, width, tile in loads:
                    sp.dma_start(tile[:, s, :, :].rearrange("p f d -> p (f d)"),
                                 nodes(tbl, c, width)).then_inc(s_ld[s], 16)

            def store(c, s):
                sp.wait_ge(s_res, c + 1)
                for tbl, width, tile in stores:
                    sp.dma_start(nodes(tbl, c, width),
                                 tile[:, s, :, :].rearrange("p f d -> p (f d)")).then_inc(s_st[s], 16)

            load(0, 0)
            load(1, 1)
            with sp.Fori(0, NC // 2 - 1) as i:
                for s in range(2):
                    store(i * 2 + s, s)
                    load(i * 2 + s + 2, s)
            for s in range(2):
                store(NC - 2 + s, s)
            for s in range(2):
                sp.wait_ge(s_st[s], 16 * len(stores) * (NC // 2))

        class Norm:
            s_cent = sem("norm_centred")
            s_sq = sem("norm_squared")
            s_var = sem("norm_variance")
            s_root = sem("norm_root")
            done = 0

            def __init__(self, x, sq, stat, per_chunk):
                self.x, self.sq, self.stat, self.per = x, sq, stat, per_chunk
                self.base = Norm.done
                Norm.done += per_chunk * NC

            def count(self, c, k):
                return c * self.per + (self.base + k + 1)

            def centre(self, dve, c, s, did, need, k):
                need(did(dve.tensor_reduce(self.stat[:, s, 0, :], self.x[:, s, :, :], AX.X, ALU.add)))
                need(did(dve.tensor_scalar(self.stat[:, s, 0, :], self.stat[:, s, 0, :], -1.0 / D, None,
                                           ALU.mult)))
                dve.tensor_tensor(self.x[:, s, :, :], self.x[:, s, :, :],
                                  self.stat[:, s, 0, :].unsqueeze(2).to_broadcast([P, CH, D]),
                                  ALU.add).then_inc(self.s_cent, 1)

            def variance(self, dve, c, s, did, need, k):
                dve.wait_ge(self.s_sq, self.count(c, k))
                need(did(dve.tensor_reduce(self.stat[:, s, 1, :], self.sq[:, s, :, :], AX.X, ALU.add)))
                dve.tensor_scalar(self.stat[:, s, 1, :], self.stat[:, s, 1, :], 1.0 / D, EPS, ALU.mult,
                                  ALU.add).then_inc(self.s_var, 1)

            def scale(self, dve, c, s, did, need, k, out):
                dve.wait_ge(self.s_root, self.count(c, k))
                need(did(dve.reciprocal(self.stat[:, s, 2, :], self.stat[:, s, 2, :])))
                return dve.tensor_tensor(out[:, s, :, :], self.x[:, s, :, :],
                                         self.stat[:, s, 2, :].unsqueeze(2).to_broadcast([P, CH, D]), ALU.mult)

            def square(self, act, c, s, k):
                act.wait_ge(self.s_cent, self.count(c, k))
                act.activation(self.sq[:, s, :, :], self.x[:, s, :, :], ACT.Square).then_inc(self.s_sq, 1)

            def root(self, act, c, s, k):
                act.wait_ge(self.s_var, self.count(c, k))
                act.activation(self.stat[:, s, 2, :], self.stat[:, s, 1, :], ACT.Sqrt).then_inc(self.s_root, 1)

        def chunks(eng, step, n=None):
            step(0, 0)
            step(0, 1)
            first = n[0] if n else 0
            with eng.Fori(1, NC // 2 - 1) as q:
                if n:
                    n[1] = (q - 1) * n[2]
                step(q, 0)
                step(q, 1)
            if n:
                assert n[0] == first + n[2], n[0] - first
                n[:2] = [first, (NC // 2 - 2) * n[2]]
            step(NC // 2 - 1, 0)
            step(NC // 2 - 1, 1)

        def chain_of(dve, s_v, n):
            def did(ins):
                n[0] += 1
                ins.then_inc(s_v, 1)
                return n[0]

            def need(k):
                dve.wait_ge(s_v, n[1] + k)
            return did, need

        with ExitStack() as ph, nc.Block() as block:
            def tmp(name, shape, dt=F32):
                return ph.enter_context(nc.sbuf_tensor(name, shape, dt))

            xin = tmp("d0_x", [P, 2, CH, XW])
            agg = tmp("d0_agg", [P, 2, CH, AW])
            x = tmp("d0_sum", [P, 2, CH, D])
            sq = tmp("d0_sq", [P, 2, CH, D])
            stat = tmp("d0_stat", [P, 2, 3, CH])
            stage = tmp("sr_stage", [P, 2, SR], I32)
            ring = tmp("sr_ring", [P, 2, SR, 2])
            ln = Norm(x, sq, stat, 2)
            s_st = [sem(f"d0_stored{s}") for s in range(2)]
            s_res = sem("d0_result")
            s_v = sem("d0_chain")
            s_n = sem("node_degrees")
            s_nr = sem("node_roots")
            s_stage = sem("source_index_staged")
            s_got = [sem(f"source_rows_got{h}") for h in range(2)]
            s_kept = sem("source_rows_kept")

            @block.sync
            def _(sp):
                sp.dma_start(indeg_n[:, :], indeg_t.rearrange("(p f) c -> p (f c)", p=P)).then_inc(s_n, 16)
                stream(sp, [(xz_t.bitcast(F32), XW, xin), (agg0_t, AW, agg)], [(x1_t, D, sq)], s_res, s_st)

            @block.gpsimd
            def _(pool):
                def keep(h, at):
                    pool.nop(nofuse=True)
                    pool.tensor_copy(srows[:, :, :].rearrange("p t c -> p (t c)")[:, at],
                                     ring[:, h, :, :].rearrange("p t c -> p (t c)")).then_inc(s_kept, 1)

                def gather(h, at):
                    pool.nop(nofuse=True)
                    pool.tensor_copy(stage[:, h, :], src_i[:, at]).then_inc(s_stage, 1)

                def fetch(h):
                    pool.nop(nofuse=True)
                    for u in range(SR):
                        pool.indirect_dma_start(
                            out=ring[:, h, u, :], out_offset=None, in_=srow_t,
                            in_offset=bass.IndirectOffsetOnAxis(ap=stage[:, h, u:u + 1], axis=0),
                        ).then_inc(s_got[h], 16)

                for h in range(2):
                    gather(h, slice(h * SR, (h + 1) * SR))
                    pool.wait_ge(s_stage, h + 1)
                    fetch(h)
                with pool.Fori(0, T // (2 * SR) - 1) as i:
                    for h in range(2):
                        pool.wait_ge(s_got[h], i * (16 * SR) + 16 * SR)
                        keep(h, bass.ds((i * 2 + h) * (2 * SR), 2 * SR))
                        gather(h, bass.ds((i * 2 + h + 2) * SR, SR))
                        pool.wait_ge(s_kept, i * 2 + h + 1)
                        pool.wait_ge(s_stage, i * 2 + h + 3)
                        fetch(h)
                for h in range(2):
                    pool.wait_ge(s_got[h], T // 2 * 16)
                    keep(h, slice((T - (2 - h) * SR) * 2, (T - (1 - h) * SR) * 2))

            @block.scalar
            def _(act):
                fill(act, y_t, zeros, s_y)
                fill(act, agg3_t, bias3, s_agg3)
                act.wait_ge(s_nr, 1)
                act.activation(cj_n[:, :], cj_n[:, :], ACT.Sqrt).then_inc(s_nr, 1)

                def step(q, s):
                    c = q * 2 + s
                    ln.square(act, c, s, 0)
                    if later(c):
                        ln.root(act, c - 1, 1 - s, 1)
                    ln.root(act, c, s, 0)
                    ln.square(act, c, s, 1)

                chunks(act, step)
                ln.root(act, NC - 1, 1, 1)

            @block.vector
            def _(dve):
                n = [0, 0, 2 * 16]
                did, need = chain_of(dve, s_v, n)

                def finish(c, s):
                    ln.scale(dve, c, s, did, need, 1, sq).then_inc(s_res, 1)

                def step(q, s):
                    c = q * 2 + s
                    dve.wait_ge(s_ld[s], loaded(0, q))
                    need(did(dve.tensor_scalar(stat[:, s, 0, :], agg[:, s, :, D], 1e-8, None, ALU.max)))
                    need(did(dve.reciprocal(stat[:, s, 1, :], stat[:, s, 0, :])))
                    need(did(dve.tensor_tensor(x[:, s, :, :], agg[:, s, :, 0:D],
                                               stat[:, s, 1, :].unsqueeze(2).to_broadcast([P, CH, D]),
                                               ALU.mult)))
                    need(did(dve.tensor_tensor(x[:, s, :, :], x[:, s, :, :], xin[:, s, :, 0:D], ALU.add)))
                    if later(q):
                        dve.wait_ge(s_st[s], q * 16)
                    ln.centre(dve, c, s, did, need, 0)
                    if later(c):
                        ln.variance(dve, c - 1, 1 - s, did, need, 1)
                    ln.variance(dve, c, s, did, need, 0)
                    if later(c):
                        finish(c - 1, 1 - s)
                    need(did(ln.scale(dve, c, s, did, need, 0, x)))
                    need(did(dve.tensor_tensor(x[:, s, :, :], x[:, s, :, :],
                                               gammab[:, :].unsqueeze(1).to_broadcast([P, CH, D]), ALU.mult)))
                    need(did(dve.tensor_tensor(x[:, s, :, :], x[:, s, :, :],
                                               betab[:, :].unsqueeze(1).to_broadcast([P, CH, D]), ALU.add)))
                    need(did(dve.tensor_tensor(x[:, s, :, :], x[:, s, :, :], xin[:, s, :, 0:D], ALU.add)))
                    ln.centre(dve, c, s, did, need, 1)

                dve.wait_ge(s_n, 16)
                need(did(dve.tensor_scalar(cj_n[:, :], indeg_n[:, :], 1.0, None, ALU.max)))
                dve.reciprocal(cj_n[:, :], cj_n[:, :]).then_inc(s_nr, 1)
                need(did(dve.tensor_scalar(indeg_n[:, :], indeg_n[:, :], 1.0, None, ALU.min)))
                need(did(dve.tensor_scalar(none_n[:, :], indeg_n[:, :], -1.0, 1.0, ALU.mult, ALU.add)))
                dve.wait_ge(s_nr, 2)
                need(did(dve.tensor_tensor(dinv_n[:, :], cj_n[:, :], indeg_n[:, :], ALU.mult)))
                chunks(dve, step, n)
                ln.variance(dve, NC - 1, 1, did, need, 1)
                finish(NC - 1, 1)
                dve.wait_ge(s_kept, T // SR)

        with ExitStack() as ph, nc.Block() as block:
            def tmp(name, shape, dt=F32):
                return ph.enter_context(nc.sbuf_tensor(name, shape, dt))

            def ptmp(name, shape, dt=F32):
                return ph.enter_context(nc.psum_tensor(name, shape, dt))

            TL = T + TB
            TOP = 256
            edge = tmp("edge", [P, T, 4])
            filler = tmp("filler", [1, 4])
            lst = tmp("list", [P, TL, 4])
            prev_dst = tmp("prev_dst", [P, TL])
            own_dst = tmp("own_dst", [P, TL])
            w_k = tmp("w_k", [P, TL])
            zero_in = tmp("zero_in", [P, TL])
            key = tmp("key", [P, T])
            ttop = tmp("ttop", [P, TL])
            best = tmp("best", [P, 8])
            order = tmp("order", [P, T + 8])
            live = tmp("live", [P, T + 8])
            eid_f = tmp("eid_f", [P, T + 8])
            eid = tmp("eid", [P, T + 8], I32)
            ebase = tmp("ebase", [P, 1])
            count = tmp("count", [P, 1])
            sizes_f = tmp("sizes_f", [1, 4])
            sizes = tmp("sizes", [1, 4], I32)
            gi = tmp("gi", [P, TL], I32)
            ri = tmp("ri", [P, TL], I32)
            ci = tmp("ci", [P, TL], I32)
            level = tmp("level", [P, 2 * K])
            off = tmp("off", [P, 2])
            qcur = tmp("qcur", [P, 1])
            gidx = tmp("p_gidx", [P, TB], I32)
            sidx_r = tmp("p_sidx_r", [P, TB], I32)
            sidx_y = tmp("p_sidx_y", [P, TB], I32)
            cidx = tmp("p_cidx", [P, TB], I32)
            lidx = tmp("p_lidx", [P, 2, 2], I32)
            lring = tmp("p_lring", [P, 2, 2, 4])
            fidx = tmp("p_fidx", [P, 2, 2], I32)
            fring = tmp("p_fring", [P, 2, 2, D])
            fjunk = tmp("p_fjunk", [P, 2, 2, D])
            fcount = tmp("p_fcount", [P, 2, 2])
            xg = tmp("p_xg", [P, TB, D])
            xc = tmp("p_xc", [P, TB, D])
            dkey = tmp("p_dkey", [P, TB])
            keys = tmp("p_keys", [P, TB, P])
            same = tmp("p_same", [P, TB, GE])
            junk = tmp("p_junk", [P, TB, GE])
            rank = tmp("p_rank", [P, TB])
            msg = tmp("p_msg", [P, TB, D])
            rows_r = tmp("p_rows_r", [P, TB, D])
            rows_y = tmp("p_rows_y", [P, TB, D])
            keys_p = ptmp("keys_p", [P, TB, P])
            sum_p = ptmp("psum_p", [P, TB, 128])
            cnt_p = ptmp("cnt_p", [P, 512])
            s_lv = sem("p_level_constants")
            s_edge = sem("p_edge_table")
            s_cnt = sem("p_count")
            s_cntt = sem("p_count_turned")
            s_nx = sem("p_list_size")
            s_ei = sem("p_edge_ids")
            s_li = sem("p_list_index")
            s_lg = [sem(f"p_list_rows{h}") for h in range(2)]
            s_lf = sem("p_list_ring_free")
            s_go = sem("p_level_ready")
            s_q = sem("p_coefficient")
            s_gi = sem("p_gather_index")
            s_gx = sem("p_rows_got")
            s_xc = sem("p_rows_copied")
            s_dk = sem("p_target_keys")
            s_kt = sem("p_keys_turned")
            s_kc = sem("p_keys_copied")
            s_si = sem("p_scatter_index")
            s_msg = sem("p_messages")
            s_sum = sem("p_sums")
            s_rows = sem("p_rows_ready")
            s_addr = sem("p_added_powers")
            s_addy = sem("p_added_filter")
            s_ci = sem("p_clear_index")
            s_cl = sem("p_cleared")
            s_fi = sem("p_flag_index")
            s_fg = [sem(f"p_flag_rows{h}") for h in range(2)]
            s_ff = sem("p_flag_ring_free")
            s_v = sem("p_chain")
            s_root = sem("p_first_weights")
            H2 = 2

            class Levels:

                def __init__(self, eng, tag):
                    self.eng = eng
                    self.reg = {x: eng.alloc_register(f"{tag}_{x}") for x in ("n", "c", "m", "b")}
                    eng.wait_ge(s_nx, 1)
                    first = self.size(0)
                    eng.reg_mov(self.reg["n"], first)
                    for x, v in (("c", 0), ("m", 1), ("b", 0)):
                        eng.reg_mov(self.reg[x], v)
                    self.first = first

                def size(self, j):
                    self.eng.nop(nofuse=True)
                    return self.eng.value_load(sizes[0:1, j:j + 1], min_val=1, max_val=NB)

                def here(self):
                    return [self.eng.snap(self.reg[x]) for x in ("n", "c", "m", "b")]

                def next(self, n, c, m, b, new):
                    self.eng.reg_mov(self.reg["b"], b + m)
                    self.eng.reg_mov(self.reg["m"], n)
                    self.eng.reg_mov(self.reg["c"], c + n)
                    self.eng.reg_mov(self.reg["n"], new)

            @block.sync
            def _(sp):
                sp.dma_start(level[:, :], a["level"].partition_broadcast(P)).then_inc(s_lv, 16)
                sp.wait_ge(s_edge, 1)
                sp.dma_start(edge_t[0:EP, :].rearrange("(p t) c -> p (t c)", p=P),
                             edge[:, :, :].rearrange("p t c -> p (t c)")).then_inc(s_edge, 16)
                sp.dma_start(edge_t[EP:EP + 1, :], filler[:, :]).then_inc(s_edge, 16)
                sp.wait_ge(s_edge, 33)

            @block.gpsimd
            def _(pool):
                pool.iota(ebase[:, :], pattern=[[0, 1]], base=TOP - EP, channel_multiplier=T,
                          allow_small_or_imprecise_dtypes=True).then_inc(s_lv, 1)
                pool.iota(edge[:, :, 3:4].rearrange("p t c -> p (t c)"), pattern=[[1, T]], base=0,
                          channel_multiplier=0, allow_small_or_imprecise_dtypes=True).then_inc(s_lv, 1)

                def build(n, c):
                    with pool.Fori(0, n) as i:
                        for h in range(2):
                            pool.wait_ge(s_li, (c + i) * 2 + (h + 1))
                            pool.wait_ge(s_lf, (c + i) * 2 + (h + 1))
                            pool.nop(nofuse=True)
                            for u in range(H2):
                                pool.indirect_dma_start(
                                    out=lring[:, h, u, :], out_offset=None, in_=edge_t,
                                    in_offset=bass.IndirectOffsetOnAxis(ap=lidx[:, h, u:u + 1], axis=0),
                                ).then_inc(s_lg[h], 16)

                def gather(u):
                    pool.indirect_dma_start(
                        out=xg[:, u, :], out_offset=None, in_=pow_t,
                        in_offset=bass.IndirectOffsetOnAxis(ap=gidx[:, u:u + 1], axis=0)).then_inc(s_gx, 16)

                def add(tbl, idx, rows, done, u):
                    pool.indirect_dma_start(
                        out=tbl, out_offset=bass.IndirectOffsetOnAxis(ap=idx[:, u:u + 1], axis=0),
                        in_=rows[:, u, :], in_offset=None, compute_op=ALU.add).then_inc(done, 16)

                lv = Levels(pool, "pool")
                pool.wait_ge(s_edge, 33)
                build(lv.first, 0)
                pool.wait_ge(s_pow, filled(pow_t[NP:, :]))
                pool.wait_ge(s_y, filled(y_t))
                with pool.Fori(0, K) as k:
                    n, c, m, b = lv.here()
                    pool.wait_ge(s_gi, c + k + 1)
                    pool.nop(nofuse=True)
                    for u in range(TB):
                        gather(u)
                    pool.wait_ge(s_cl, b * 64)
                    pool.nop(nofuse=True)
                    with pool.Fori(0, n) as i:
                        pool.wait_ge(s_xc, c + i + 1)
                        pool.wait_ge(s_gi, c + k + i + 2)
                        pool.nop(nofuse=True)
                        gather(0)
                        gather(1)
                        pool.wait_ge(s_rows, c + i + 1)
                        pool.wait_ge(s_si, c + i + 1)
                        pool.wait_ge(s_addr, (c + i) * 64)
                        pool.wait_ge(s_addy, (c + i) * 64)
                        pool.nop(nofuse=True)
                        for g in range(2):
                            if g == 1:
                                gather(2)
                                gather(3)
                                pool.wait_ge(s_addr, (c + i) * 64 + 32)
                                pool.wait_ge(s_addy, (c + i) * 64 + 32)
                                pool.nop(nofuse=True)
                            for u in (2 * g, 2 * g + 1):
                                add(pow_t, sidx_r, rows_r, s_addr, u)
                            for u in (2 * g, 2 * g + 1):
                                add(y_t, sidx_y, rows_y, s_addy, u)
                    pool.wait_ge(s_gx, (c + k + n + 1) * 64)
                    pool.nop(nofuse=True)
                    with pool.Fori(0, m) as i:
                        pool.wait_ge(s_ci, b + i + 1)
                        pool.nop(nofuse=True)
                        for u in range(TB):
                            if u == GE // P:
                                pool.wait_ge(s_cl, (b + i) * 64 + 32)
                                pool.nop(nofuse=True)
                            pool.indirect_dma_start(
                                out=pow_t, out_offset=bass.IndirectOffsetOnAxis(ap=cidx[:, u:u + 1], axis=0),
                                in_=zeros[:, 0:D], in_offset=None).then_inc(s_cl, 16)
                    pool.wait_ge(s_addr, (c + n) * 64)
                    pool.nop(nofuse=True)
                    with pool.Fori(0, n) as i:
                        for h in range(2):
                            pool.wait_ge(s_fi, (c + i) * 2 + (h + 1))
                            pool.wait_ge(s_ff, (c + i) * 2 + (h + 1))
                            pool.nop(nofuse=True)
                            for u in range(H2):
                                pool.indirect_dma_start(
                                    out=fring[:, h, u, :], out_offset=None, in_=pow_t,
                                    in_offset=bass.IndirectOffsetOnAxis(ap=fidx[:, h, u:u + 1], axis=0),
                                ).then_inc(s_fg[h], 16)
                    pool.wait_ge(s_nx, k + 2)
                    new = lv.size(0)
                    build(new, c + n)
                    lv.next(n, c, m, b, new)

            @block.scalar
            def _(act):
                def build(n, c):
                    with act.Fori(0, n) as i:
                        for h in range(2):
                            act.wait_ge(s_lg[h], (c + i) * (16 * H2))
                            act.nop(nofuse=True)
                            act.copy(lidx[:, h, :], eid[:, bass.ds(i * TB + h * H2, H2)]).then_inc(s_li, 1)

                lv = Levels(act, "act")
                act.wait_ge(s_ei, 1)
                build(lv.first, 0)
                act.wait_ge(s_root, 1)
                act.activation(w_k[:, :], w_k[:, :], ACT.Sqrt).then_inc(s_root, 1)
                with act.Fori(0, K) as k:
                    n, c, m, b = lv.here()
                    act.wait_ge(s_go, k + 1)
                    act.nop(nofuse=True)
                    act.copy(qcur[:, :], qk[:, bass.ds(k + 1, 1)]).then_inc(s_q, 1)
                    act.copy(gidx[:, :], gi[:, 0:TB]).then_inc(s_gi, 1)
                    act.wait_ge(s_q, k + 1)
                    with act.Fori(0, n) as i:
                        act.wait_ge(s_gx, (c + k + i) * 64 + 64)
                        act.wait_ge(s_msg, c + i)
                        act.nop(nofuse=True)
                        act.copy(xc[:, :, :], xg[:, :, :]).then_inc(s_xc, 1)
                        act.copy(gidx[:, :], gi[:, bass.ds(i * TB + TB, TB)]).then_inc(s_gi, 1)
                        act.wait_ge(s_kt, c + i + 1)
                        act.wait_ge(s_si, c + i)
                        act.activation(keys[:, :, :], keys_p[:, :, :], ACT.Copy).then_inc(s_kc, 1)
                        act.wait_ge(s_sum, c + i + 1)
                        act.wait_ge(s_addr, (c + i) * 64)
                        act.wait_ge(s_addy, (c + i) * 64)
                        act.activation(rows_r[:, :, :], sum_p[:, :, 0:D], ACT.Copy)
                        act.activation(rows_y[:, :, :], sum_p[:, :, 0:D], ACT.Copy,
                                       scale=qcur[:, 0:1]).then_inc(s_rows, 1)
                    with act.Fori(0, m) as i:
                        act.wait_ge(s_cl, (b + i) * 64)
                        act.nop(nofuse=True)
                        act.copy(cidx[:, :], ci[:, bass.ds(i * TB, TB)]).then_inc(s_ci, 1)
                    with act.Fori(0, n) as i:
                        for h in range(2):
                            act.wait_ge(s_fg[h], (c + i) * (16 * H2))
                            act.nop(nofuse=True)
                            act.copy(fidx[:, h, :], ri[:, bass.ds(i * TB + h * H2, H2)]).then_inc(s_fi, 1)
                    act.wait_ge(s_nx, k + 2)
                    new = lv.size(0)
                    act.wait_ge(s_ei, k + 2)
                    build(new, c + n)
                    lv.next(n, c, m, b, new)

            @block.tensor
            def _(pe):
                pe.wait_ge(s_cnt, 1)
                pe.transpose(cnt_p[0:1, 0:P], count[:, 0:1], ident[:, :]).then_inc(s_cntt, 1)
                lv = Levels(pe, "pe")
                with pe.Fori(0, K) as k:
                    n, c, m, b = lv.here()
                    with pe.Fori(0, n) as i:
                        pe.wait_ge(s_dk, c + i + 1)
                        pe.wait_ge(s_kc, c + i)
                        pe.nop(nofuse=True)
                        for u in range(TB):
                            ins = pe.transpose(keys_p[:, u, :], dkey[:, u:u + 1].to_broadcast([P, P]), ident[:, :])
                        ins.then_inc(s_kt, 1)
                        pe.wait_ge(s_msg, c + i + 1)
                        pe.wait_ge(s_rows, c + i)
                        pe.nop(nofuse=True)
                        group_sums(pe, sum_p, same, msg).then_inc(s_sum, 1)
                    pe.wait_ge(s_cnt, k + 2)
                    pe.nop(nofuse=True)
                    pe.transpose(cnt_p[0:1, 0:P], count[:, 0:1], ident[:, :]).then_inc(s_cntt, 1)
                    pe.wait_ge(s_nx, k + 2)
                    lv.next(n, c, m, b, lv.size(0))

            @block.vector
            def _(dve):
                mark = dve.alloc_register("dve_mark")
                dve.reg_mov(mark, 0)
                here = [dve.snap(mark), 0]

                def chain(ins):
                    here[1] += 1
                    ins.then_inc(s_v, 1)
                    dve.wait_ge(s_v, here[0] + here[1])

                def settle(extra=0):
                    dve.reg_mov(mark, here[0] + (here[1] + extra))

                def resume():
                    here[0], here[1] = dve.snap(mark), 0

                def size_and_sort(k):
                    chain(dve.tensor_scalar(live[:, 0:T], key[:, :], 0.5, None, ALU.is_gt))
                    dve.tensor_reduce(count[:, :], live[:, 0:T], AX.X, ALU.add).then_inc(s_cnt, 1)
                    dve.wait_ge(s_cntt, k + 1)
                    dve.nop(nofuse=True)
                    chain(dve.tensor_reduce(sizes_f[:, 0:1], cnt_p[0:1, 0:P], AX.X, ALU.max))
                    chain(dve.tensor_scalar(sizes_f[:, 0:1], sizes_f[:, 0:1], 3.0, None, ALU.add))
                    chain(dve.tensor_copy(sizes[:, 0:1], sizes_f[:, 0:1]))
                    chain(dve.tensor_scalar(sizes[:, 0:1], sizes[:, 0:1], 2, None, ALU.logical_shift_right))
                    chain(dve.tensor_copy(sizes_f[:, 0:1], sizes[:, 0:1]))
                    chain(dve.tensor_scalar(sizes_f[:, 0:1], sizes_f[:, 0:1], 1.0, None, ALU.max))
                    chain(dve.tensor_scalar(sizes_f[:, 1:2], sizes_f[:, 0:1], 1.0, None, ALU.add))
                    chain(dve.tensor_copy(sizes[:, 0:2], sizes_f[:, 0:2]))
                    chain(dve.tensor_scalar(sizes[:, 1:2], sizes[:, 1:2], 1, None, ALU.logical_shift_right))
                    dve.sem_inc(s_nx, 1)
                    rounds = dve.value_load(sizes[0:1, 1:2], min_val=1, max_val=(NB + 1) // 2)
                    settle()
                    with dve.Fori(0, rounds) as r:
                        resume()
                        chain(dve.max(best[:, :], key[:, :]))
                        dve.tensor_copy(order[:, bass.ds(r * 8, 8)], best[:, :])
                        chain(dve.match_replace(key[:, :], best[:, :], key[:, :], 0.0))
                        settle()
                    resume()
                    chain(dve.tensor_scalar(live[:, :], order[:, :], 1.0, None, ALU.min))
                    chain(dve.tensor_scalar(eid_f[:, :], order[:, :], -1.0, ebase[:, 0:1], ALU.mult, ALU.add))
                    chain(dve.tensor_tensor(eid_f[:, :], eid_f[:, :], live[:, :], ALU.mult))
                    chain(dve.tensor_scalar(eid[:, :], eid_f[:, :], float(EP), None, ALU.add))
                    dve.sem_inc(s_ei, 1)

                def build(n, c):
                    flat = lst[:, :, :].rearrange("p t c -> p (t c)")
                    with dve.Fori(0, n) as i:
                        for h in range(2):
                            dve.wait_ge(s_lg[h], (c + i) * (16 * H2) + 16 * H2)
                            dve.nop(nofuse=True)
                            ins = dve.tensor_copy(flat[:, bass.ds(i * (4 * TB) + h * (4 * H2), 4 * H2)],
                                                  lring[:, h, :, :].rearrange("p t c -> p (t c)"))
                            ins.then_inc(s_lf, 1)
                    dve.wait_ge(s_lf, (c + n) * 2 + 2)
                    dve.nop(nofuse=True)

                dve.wait_ge(s_lv, 18)
                dve.sem_inc(s_lf, 2)
                dve.sem_inc(s_ff, 2)
                dve.tensor_copy(edge[:, :, 0], src_f[:, :])
                dve.tensor_copy(edge[:, :, 1], dst_f[:, :])
                dve.tensor_copy(edge[:, :, 2], srows[:, :, 0])
                dve.memset(order[:, :], 0.0)
                chain(dve.memset(filler[:, :], 0.0))
                dve.memset(filler[:, 0:1], float(SPARE_SRC))
                dve.memset(filler[:, 1:2], float(SPARE_DST))
                dve.memset(filler[:, 2:3], 1.0)
                dve.memset(lst[:, :, :], 1.0)
                dve.memset(prev_dst[:, :], 0.0)
                dve.memset(own_dst[:, :], 0.0)
                chain(dve.tensor_scalar(key[:, :], edge[:, :, 3], -1.0, float(TOP), ALU.mult, ALU.add))
                dve.sem_inc(s_edge, 1)
                dve.tensor_copy(prev_dst[:, 0:TB], sink[:, :])
                chain(dve.tensor_scalar(live[:, 0:T], edge[:, :, 2], 1.0, None, ALU.min))
                chain(dve.tensor_tensor(key[:, :], key[:, :], live[:, 0:T], ALU.mult))
                size_and_sort(0)
                settle()
                lv = Levels(dve, "dve")
                build(lv.first, 0)
                resume()
                dve.reciprocal(w_k[:, :], lst[:, :, 2]).then_inc(s_root, 1)
                dve.wait_ge(s_root, 2)
                with dve.Fori(0, K) as k:
                    n, c, m, b = lv.here()
                    resume()
                    chain(dve.tensor_copy(off[:, :], level[:, bass.ds(k * 2, 2)]))
                    dve.tensor_scalar(gi[:, :], lst[:, :, 0], off[:, 0:1], None, ALU.add)
                    dve.tensor_scalar(ri[:, :], lst[:, :, 0], off[:, 1:2], None, ALU.add)
                    dve.tensor_scalar(ci[:, :], prev_dst[:, :], off[:, 0:1], None, ALU.add)
                    dve.tensor_scalar(ttop[:, :], lst[:, :, 3], -1.0, float(TOP), ALU.mult, ALU.add)
                    dve.memset(zero_in[:, :], float(D))
                    chain(dve.tensor_copy(dkey[:, :], lst[:, 0:TB, 1]))
                    dve.sem_inc(s_go, 1)
                    settle()
                    with dve.Fori(0, n) as i:
                        resume()
                        dve.wait_ge(s_kt, c + i)
                        chain(dve.tensor_copy(dkey[:, :], lst[:, bass.ds(i * TB, TB), 1]))
                        dve.sem_inc(s_dk, 1)
                        dve.wait_ge(s_kc, c + i + 1)
                        dve.wait_ge(s_sum, c + i)
                        for u in range(TB):
                            kg = keys[:, 2 * (u // 2):2 * (u // 2) + 2, :].rearrange("p a b -> p (a b)")
                            dve.tensor_scalar(same[:, u, :], kg, dkey[:, u:u + 1], None, ALU.is_equal)
                        for u in range(TB):
                            kg = keys[:, 2 * (u // 2):2 * (u // 2) + 2, :].rearrange("p a b -> p (a b)")
                            ins = dve.scalar_tensor_tensor(out=junk[:, u, :], in0=kg, scalar=dkey[:, u:u + 1],
                                                           in1=earlier[:, u % 2, :], op0=ALU.is_equal,
                                                           op1=ALU.mult, accum_out=rank[:, u:u + 1])
                        chain(ins)
                        chain(dve.scalar_tensor_tensor(out=rank[:, :], in0=rank[:, :], scalar=1.0, in1=sink[:, :],
                                                   op0=ALU.min, op1=ALU.mult))
                        chain(dve.tensor_tensor(rank[:, :], rank[:, :], dkey[:, :], ALU.max))
                        dve.wait_ge(s_addr, (c + i) * 64)
                        dve.wait_ge(s_addy, (c + i) * 64)
                        dve.tensor_copy(sidx_y[:, :], rank[:, :])
                        dve.tensor_copy(own_dst[:, bass.ds(i * TB, TB)], rank[:, :])
                        dve.tensor_scalar(sidx_r[:, :], rank[:, :], off[:, 1:2], None, ALU.add).then_inc(s_si, 1)
                        dve.wait_ge(s_xc, c + i + 1)
                        for u in range(TB):
                            ins = dve.tensor_scalar(msg[:, u, :], xc[:, u, :],
                                                    w_k[:, bass.ds(i * TB + u, 1)], None, ALU.mult)
                        chain(ins)
                        dve.sem_inc(s_msg, 1)
                        settle()
                    with dve.Fori(0, n) as i:
                        resume()
                        for h in range(2):
                            dve.wait_ge(s_fg[h], (c + i) * (16 * H2) + 16 * H2)
                            for u in range(H2):
                                ins = dve.tensor_scalar(fjunk[:, h, u, :], fring[:, h, u, :], 0.0, 0.0,
                                                        ALU.is_equal, ALU.add, accum_out=fcount[:, h, u:u + 1])
                            chain(ins)
                            dve.sem_inc(s_ff, 1)
                            chain(dve.tensor_copy(zero_in[:, bass.ds(i * TB + h * H2, H2)], fcount[:, h, :]))
                        settle()
                    resume()
                    chain(dve.scalar_tensor_tensor(out=key[:, :], in0=zero_in[:, 0:T], scalar=D - 0.5,
                                                   in1=ttop[:, 0:T], op0=ALU.is_lt, op1=ALU.mult))
                    dve.wait_ge(s_cl, (b + m) * 64)
                    dve.nop(nofuse=True)
                    chain(dve.tensor_copy(prev_dst[:, :], own_dst[:, :]))
                    size_and_sort(k + 1)
                    new = lv.size(0)
                    build(new, c + n)
                    chain(dve.reciprocal(w_k[:, :], lst[:, :, 2]))
                    settle()
                    lv.next(n, c, m, b, new)

        with ExitStack() as ph, nc.Block() as block:
            def tmp(name, shape, dt=F32):
                return ph.enter_context(nc.sbuf_tensor(name, shape, dt))

            xin = tmp("d1_x", [P, 2, CH, D])
            yin = tmp("d1_y", [P, 2, CH, D])
            x = tmp("d1_sum", [P, 2, CH, D])
            own = tmp("d1_own", [P, 2, CH, D])
            sq = tmp("d1_sq", [P, 2, CH, D])
            stat = tmp("d1_stat", [P, 2, 3, CH])
            ln = Norm(x, sq, stat, 1)
            s_st = [sem(f"d1_stored{s}") for s in range(2)]
            s_res = sem("d1_result")
            s_v = sem("d1_chain")

            @block.sync
            def _(sp):
                stream(sp, [(x1_t, D, xin), (y_t, D, yin)], [(x2_t, D, sq), (agg2_t, D, own)], s_res, s_st)

            @block.scalar
            def _(act):
                def step(q, s):
                    c = q * 2 + s
                    if later(c):
                        ln.root(act, c - 1, 1 - s, 0)
                    ln.square(act, c, s, 0)

                chunks(act, step)
                ln.root(act, NC - 1, 1, 0)

            @block.vector
            def _(dve):
                n = [0, 0, 2 * 7]
                did, need = chain_of(dve, s_v, n)

                def finish(q, s):
                    need(did(ln.scale(dve, q * 2 + s, s, did, need, 0, sq)))
                    dve.tensor_tensor(
                        own[:, s, :, :], sq[:, s, :, :],
                        none_n[:, bass.ds((q * 2 + s) * CH, CH)].unsqueeze(2).to_broadcast([P, CH, D]),
                        ALU.mult).then_inc(s_res, 1)

                def step(q, s):
                    c = q * 2 + s
                    dve.wait_ge(s_ld[s], loaded(1, q))
                    need(did(dve.tensor_tensor(
                        yin[:, s, :, :], yin[:, s, :, :],
                        dinv_n[:, bass.ds(c * CH, CH)].unsqueeze(2).to_broadcast([P, CH, D]), ALU.mult)))
                    need(did(dve.scalar_tensor_tensor(
                        out=x[:, s, :, :].rearrange("p f d -> p (f d)"),
                        in0=xin[:, s, :, :].rearrange("p f d -> p (f d)"), scalar=qk[:, K + 1:K + 2],
                        in1=yin[:, s, :, :].rearrange("p f d -> p (f d)"), op0=ALU.mult, op1=ALU.add)))
                    if later(c):
                        ln.variance(dve, c - 1, 1 - s, did, need, 0)
                    if later(q):
                        dve.wait_ge(s_st[s], q * 32)
                    ln.centre(dve, c, s, did, need, 0)
                    if later(c):
                        finish(q - 1 + s, 1 - s)

                chunks(dve, step, n)
                ln.variance(dve, NC - 1, 1, did, need, 0)
                finish(NC // 2 - 1, 1)

        own_rows = sb("own_rows", [P, T], I32)
        with ExitStack() as ph, nc.Block() as block:
            def tmp(name, shape, dt=F32):
                return ph.enter_context(nc.sbuf_tensor(name, shape, dt))

            keys = tmp("e2_keys", [P, 2, TB // 2, GE], I32)
            same = tmp("e2_same", [P, 2, TB, GE])
            junk = tmp("e2_junk", [P, TB, GE])
            rank = tmp("e2_rank", [P, TB])
            sidx = tmp("e2_sidx", [P, 2, TB], I32)
            gidx = tmp("e2_gidx", [P, 2, TB], I32)
            xg = tmp("e2_xg", [P, 2, TB, D])
            msg = tmp("e2_msg", [P, TB, D])
            rows = tmp("e2_rows", [P, 2, TB, D])
            sum_p = ph.enter_context(nc.psum_tensor("e2_sum", [P, TB, 128], F32))
            s_key = [sem(f"e2_keys_loaded{s}") for s in range(2)]
            s_gx = [sem(f"e2_rows_got{s}") for s in range(2)]
            s_gi = sem("e2_gather_index")
            s_same = sem("e2_same")
            s_si = sem("e2_scatter_index")
            s_msg = sem("e2_messages")
            s_sum = sem("e2_sums")
            s_rows = sem("e2_rows_ready")
            s_add = [sem(f"e2_added{s}") for s in range(2)]
            s_v = sem("e2_chain")

            @block.sync
            def _(sp):
                sp.sem_inc(s_same, 1)
                with sp.Fori(0, NB // 2) as q:
                    for s in range(2):
                        i = q * 2 + s
                        sp.wait_ge(s_same, i)
                        sp.dma_start(keys[:, s, :, :].rearrange("p a b -> p (a b)"),
                                     a["dst_rows"][bass.ds(i, 1), :].partition_broadcast(P)).then_inc(s_key[s], 16)

            @block.gpsimd
            def _(pool):
                edge_dmas(pool, x2_t, agg2_t, xg, gidx, rows, sidx, s_gi, s_gx, s_rows, s_si, s_add)

            @block.scalar
            def _(act):
                def step(q, s):
                    i = q * 2 + s
                    if exists(i + 2):
                        act.wait_ge(s_gx[s], q * 64 + 64)
                        act.nop(nofuse=True)
                        act.copy(gidx[:, s, :], src_i[:, bass.ds((i + 2) * TB, TB)]).then_inc(s_gi, 1)
                    act.wait_ge(s_sum, i + 2)
                    if later(q):
                        act.wait_ge(s_add[s], q * 64)
                    act.activation(rows[:, s, :, :], sum_p[:, :, 0:D], ACT.Copy).then_inc(s_rows, 1)

                act.sem_inc(s_rows, 1)
                for s in range(2):
                    act.copy(gidx[:, s, :], src_i[:, s * TB:(s + 1) * TB]).then_inc(s_gi, 1)
                step(0, 0)
                step(0, 1)
                with act.Fori(1, NB // 2 - 2) as q:
                    step(q, 0)
                    step(q, 1)
                for i in range(NB - 4, NB):
                    step(i // 2, i % 2)

            @block.tensor
            def _(pe):
                pe.sem_inc(s_sum, 1)
                with pe.Fori(0, NB // 2) as q:
                    for s in range(2):
                        i = q * 2 + s
                        pe.wait_ge(s_msg, i + 1)
                        pe.wait_ge(s_rows, i + 1)
                        pe.nop(nofuse=True)
                        group_sums(pe, sum_p, same[:, s, :, :], msg).then_inc(s_sum, 1)

            @block.vector
            def _(dve):
                STEPS = 3
                n = [0, 0]

                def chain(ins):
                    n[0] += 1
                    ins.then_inc(s_v, 1)
                    dve.wait_ge(s_v, n[1] + n[0])

                def matrices(qj, s):
                    j = qj * 2 + s
                    dve.wait_ge(s_key[s], qj * 16 + 16)
                    if later(j):
                        dve.wait_ge(s_sum, j)
                    for u in range(TB):
                        dve.tensor_scalar(same[:, s, u, :], keys[:, s, u // 2, :], dst_f[:, bass.ds(j * TB + u, 1)],
                                          None, ALU.is_equal)
                    for u in range(TB):
                        ins = dve.scalar_tensor_tensor(out=junk[:, u, :], in0=keys[:, s, u // 2, :],
                                                       scalar=dst_f[:, bass.ds(j * TB + u, 1)],
                                                       in1=earlier[:, u % 2, :], op0=ALU.is_equal, op1=ALU.mult,
                                                       accum_out=rank[:, u:u + 1])
                    ins.then_inc(s_same, 1)
                    dve.wait_ge(s_same, j + 2)
                    chain(dve.scalar_tensor_tensor(out=rank[:, :], in0=rank[:, :], scalar=1.0, in1=sink[:, :],
                                                   op0=ALU.min, op1=ALU.mult))
                    chain(dve.tensor_tensor(rank[:, :], rank[:, :], dst_f[:, bass.ds(j * TB, TB)], ALU.max))
                    dve.tensor_copy(own_rows[:, bass.ds(j * TB, TB)], rank[:, :])
                    if later(qj):
                        dve.wait_ge(s_add[s], qj * 64)
                    dve.nop(nofuse=True)
                    dve.tensor_copy(sidx[:, s, :], rank[:, :]).then_inc(s_si, 1)

                def step(q, s):
                    i = q * 2 + s
                    dve.wait_ge(s_gx[s], q * 64 + 64)
                    dve.wait_ge(s_sum, i + 1)
                    for u in range(TB):
                        ins = dve.tensor_scalar(
                            msg[:, u, :], xg[:, s, u, :],
                            srows[:, bass.ds(i * TB + u, 1), 1:2].rearrange("p a b -> p (a b)"), None, ALU.mult)
                    chain(ins)
                    dve.sem_inc(s_msg, 1)
                    if exists(i + 1):
                        matrices(q + s, 1 - s)

                matrices(0, 0)
                step(0, 0)
                step(0, 1)
                first = n[0]
                with dve.Fori(1, NB // 2 - 2) as q:
                    n[:] = [first, (q - 1) * (2 * STEPS)]
                    step(q, 0)
                    step(q, 1)
                    assert n[0] == first + 2 * STEPS
                n[:] = [first, (NB // 2 - 3) * (2 * STEPS)]
                for i in range(NB - 4, NB):
                    step(i // 2, i % 2)
                for s in range(2):
                    dve.wait_ge(s_add[s], NB // 2 * 64)

        with ExitStack() as ph, nc.Block() as block:
            def tmp(name, shape, dt=F32):
                return ph.enter_context(nc.sbuf_tensor(name, shape, dt))

            def ptmp(name, shape, dt=F32):
                return ph.enter_context(nc.psum_tensor(name, shape, dt))

            NG = CH // 8
            xin = tmp("d2_x", [P, 2, CH, D])
            agg = tmp("d2_agg", [P, 2, CH, D])
            x = tmp("d2_sum", [P, 2, CH, D])
            sq = tmp("d2_sq", [P, 2, CH, D])
            stat = tmp("d2_stat", [P, 2, 3, CH])
            ht = tmp("d2_turned", [2 * D + 1, 2, 4 * P])
            ht_p = ptmp("d2_turned_p", [P, 512])
            hw_p = ptmp("d2_product", [P, NG, 512])
            ln = Norm(x, sq, stat, 1)
            s_st = [sem(f"d2_stored{s}") for s in range(2)]
            s_res = sem("d2_result")
            s_v = sem("d2_chain")
            s_h = sem("d2_h")
            s_ht = sem("d2_turned")
            s_hc = sem("d2_turned_copied")
            s_hw = sem("d2_product")
            s_hr = sem("d2_product_used")

            @block.sync
            def _(sp):
                stream(sp, [(x2_t, D, xin), (agg2_t, D, agg)], [(x3_t, D, sq)], s_res, s_st)

            @block.tensor
            def _(pe):
                def turn(c, s, g):
                    if g == 0:
                        pe.wait_ge(s_h, c + 2)
                    if g > 0 or later(c):
                        pe.wait_ge(s_hc, c * NG + g)
                    pe.nop(nofuse=True)
                    for j in range(4):
                        pair = agg[:, s, 8 * g + 2 * j:8 * g + 2 * j + 2, :].rearrange("p f d -> p (f d)")
                        ins = pe.transpose(ht_p[0:2 * D, j * P:(j + 1) * P], pair, ident[:, :])
                    ins.then_inc(s_ht, 1)

                def product(c, s, g):
                    pe.wait_ge(s_hc, c * NG + (g + 1))
                    if later(c):
                        pe.wait_ge(s_hr, c * NG + (g + 1 - NG))
                    pe.nop(nofuse=True)
                    for j in range(4):
                        ins = pe.matmul(hw_p[:, g, 2 * D * j:2 * D * (j + 1)], ht[:, (s + g) % 2, j * P:(j + 1) * P],
                                        wl2[:, :], start=True, stop=True)
                    ins.then_inc(s_hw, 1)

                def step(q, s):
                    c = q * 2 + s
                    turn(c, s, 0)
                    for g in range(NG):
                        if g + 1 < NG:
                            pe.wait_ge(s_hc, c * NG + (g + 1))
                            turn(c, s, g + 1)
                        product(c, s, g)

                chunks(pe, step)

            @block.scalar
            def _(act):
                def step(q, s):
                    c = q * 2 + s
                    for g in range(NG):
                        act.wait_ge(s_ht, c * NG + (g + 1))
                        if g > 1 or later(c):
                            act.wait_ge(s_hw, c * NG + (g - 1))
                        act.activation(ht[0:2 * D, (s + g) % 2, :], ht_p[0:2 * D, :], ACT.Copy).then_inc(s_hc, 1)
                        if g == 4 and later(c):
                            ln.square(act, c - 1, 1 - s, 0)
                            ln.root(act, c - 1, 1 - s, 0)

                chunks(act, step)
                ln.square(act, NC - 1, 1, 0)
                ln.root(act, NC - 1, 1, 0)

            @block.vector
            def _(dve):
                n = [0, 0, 2 * 4]
                did, need = chain_of(dve, s_v, n)

                def scaled(q, s):
                    dve.wait_ge(s_ld[s], loaded(2, q))
                    dve.tensor_tensor(
                        agg[:, s, :, :], agg[:, s, :, :],
                        cj_n[:, bass.ds((q * 2 + s) * CH, CH)].unsqueeze(2).to_broadcast([P, CH, D]),
                        ALU.mult).then_inc(s_h, 1)

                def step(q, s):
                    c = q * 2 + s
                    if not isinstance(c, int) or c + 1 < NC:
                        scaled(q + s, 1 - s)
                    for g in range(NG):
                        dve.wait_ge(s_hw, c * NG + (g + 1))
                        grp = slice(8 * g, 8 * g + 8)
                        ins = dve.scalar_tensor_tensor(
                            out=x[:, s, grp, :].rearrange("p f d -> p (f d)"),
                            in0=hw_p[:, g, 0:8 * D], scalar=0.0,
                            in1=xin[:, s, grp, :].rearrange("p f d -> p (f d)"), op0=ALU.max, op1=ALU.add)
                        ins.then_inc(s_hr, 1)
                    dve.wait_ge(s_hr, c * NG + NG)
                    dve.nop(nofuse=True)
                    if later(q):
                        dve.wait_ge(s_st[s], q * 16)
                    ln.centre(dve, c, s, did, need, 0)
                    ln.variance(dve, c, s, did, need, 0)
                    ln.scale(dve, c, s, did, need, 0, sq).then_inc(s_res, 1)

                dve.memset(ht[:, :, :], 1.0).then_inc(s_h, 1)
                scaled(0, 0)
                chunks(dve, step, n)

        with ExitStack() as ph, nc.Block() as block:
            def tmp(name, shape, dt=F32):
                return ph.enter_context(nc.sbuf_tensor(name, shape, dt))

            def ptmp(name, shape, dt=F32):
                return ph.enter_context(nc.psum_tensor(name, shape, dt))

            NJ = NREL * D // P
            keys = tmp("e3_keys", [P, 2, TB // 2, GE], I32)
            rel = tmp("e3_rel", [P, 2, TB * P], I32)
            same = tmp("e3_same", [P, 2, TB, GE])
            sidx = tmp("e3_sidx", [P, 2, TB], I32)
            gidx = tmp("e3_gidx", [P, 2, TB], I32)
            xg = tmp("e3_xg", [P, 2, TB, D])
            xt = tmp("e3_turned", [D, TB * P])
            hr = tmp("e3_hidden", [P, NJ, TB * P])
            hm = tmp("e3_masked", [P, 2, NJ, TB * P])
            msg = tmp("e3_msg", [P, TB, D])
            rows = tmp("e3_rows", [P, 2, TB, D])
            xt_p = ptmp("e3_turned_p", [P, TB, P])
            h_p = ptmp("e3_hidden_p", [P, NJ, TB * P])
            m_p = ptmp("e3_message_p", [P, 2, TB, 128])
            sum_p = ptmp("e3_sum", [P, TB, 128])
            s_key = [sem(f"e3_keys_loaded{s}") for s in range(2)]
            s_rel = [sem(f"e3_kinds_loaded{s}") for s in range(2)]
            s_gx = [sem(f"e3_rows_got{s}") for s in range(2)]
            s_gi = sem("e3_gather_index")
            s_xt = sem("e3_rows_turned")
            s_xtc = sem("e3_turned_copied")
            s_hp = sem("e3_hidden_products")
            s_hr = sem("e3_hidden")
            s_hm = sem("e3_masked")
            s_mp = sem("e3_message_products")
            s_same = sem("e3_same")
            s_msg = sem("e3_messages")
            s_sum = sem("e3_sums")
            s_rows = sem("e3_rows_ready")
            s_si = sem("e3_scatter_index")
            s_add = [sem(f"e3_added{s}") for s in range(2)]

            @block.sync
            def _(sp):
                sp.sem_inc(s_same, 1)
                sp.sem_inc(s_hm, 1)
                with sp.Fori(0, NB // 2) as q:
                    for s in range(2):
                        i = q * 2 + s
                        sp.wait_ge(s_same, i)
                        sp.dma_start(keys[:, s, :, :].rearrange("p a b -> p (a b)"),
                                     a["dst_rows"][bass.ds(i, 1), :].partition_broadcast(P)).then_inc(s_key[s], 16)
                        sp.wait_ge(s_hm, i)
                        sp.dma_start(rel[:, s, :], a["rel_rows"][bass.ds(i, 1), :].partition_broadcast(P)
                                     ).then_inc(s_rel[s], 16)

            @block.gpsimd
            def _(pool):
                pool.wait_ge(s_agg3, filled(agg3_t))
                edge_dmas(pool, x3_t, agg3_t, xg, gidx, rows, sidx, s_gi, s_gx, s_rows, s_si, s_add, lead=3)

            @block.scalar
            def _(act):
                def turned(j):
                    act.wait_ge(s_xt, j + 1)
                    if later(j):
                        act.wait_ge(s_hp, j * NJ)
                    act.activation(xt[:, :], xt_p[0:D, :, :].rearrange("p a b -> p (a b)"),
                                   ACT.Copy).then_inc(s_xtc, 1)

                def hidden(j):
                    for b in range(NJ):
                        act.wait_ge(s_hp, j * NJ + (b + 1))
                        act.wait_ge(s_hm, j + 1)
                        act.activation(hr[:, b, :], h_p[:, b, :], ACT.Relu, bias=br1[:, b:b + 1]).then_inc(s_hr, 1)

                def step(q, s):
                    i = q * 2 + s
                    if exists(i + 3):
                        act.nop(nofuse=True)
                        act.copy(gidx[:, 1 - s, :], src_i[:, bass.ds((i + 3) * TB, TB)]).then_inc(s_gi, 1)
                    if exists(i + 1):
                        hidden(i + 1)
                    act.wait_ge(s_sum, i + 2)
                    if later(q):
                        act.wait_ge(s_add[s], q * 64)
                    act.activation(rows[:, s, :, :], sum_p[:, :, 0:D], ACT.Copy).then_inc(s_rows, 1)
                    if exists(i + 2):
                        turned(i + 2)

                act.sem_inc(s_rows, 1)
                for s in range(2):
                    act.copy(gidx[:, s, :], src_i[:, s * TB:(s + 1) * TB]).then_inc(s_gi, 1)
                turned(0)
                hidden(0)
                turned(1)
                act.copy(gidx[:, 0, :], src_i[:, 2 * TB:3 * TB]).then_inc(s_gi, 1)
                step(0, 0)
                step(0, 1)
                with act.Fori(1, NB // 2 - 2) as q:
                    step(q, 0)
                    step(q, 1)
                for i in range(NB - 4, NB):
                    step(i // 2, i % 2)

            @block.tensor
            def _(pe):
                def turn(q, j, s):
                    pe.wait_ge(s_gx[s], q * 64 + 64)
                    if later(j):
                        pe.wait_ge(s_xtc, j)
                    pe.nop(nofuse=True)
                    for u in range(TB):
                        ins = pe.transpose(xt_p[0:D, u, :], xg[:, s, u, :], ident[:, :])
                    ins.then_inc(s_xt, 1)

                def hidden(j):
                    pe.wait_ge(s_xtc, j + 1)
                    if later(j):
                        pe.wait_ge(s_hr, j * NJ)
                    pe.nop(nofuse=True)
                    for b in range(NJ):
                        pe.matmul(h_p[:, b, :], wr1[:, b * P:(b + 1) * P], xt[:, :], start=True,
                                  stop=True).then_inc(s_hp, 1)

                def step(q, s):
                    i = q * 2 + s
                    pe.wait_ge(s_hm, i + 2)
                    pe.wait_ge(s_msg, i + 1)
                    pe.nop(nofuse=True)
                    for u in range(TB):
                        for b in range(NJ):
                            ins = pe.matmul(m_p[:, s, u, 0:D], hm[:, s, b, u * P:(u + 1) * P],
                                            wr2[:, b * D:(b + 1) * D], start=(b == 0), stop=(b == NJ - 1))
                    ins.then_inc(s_mp, 1)
                    if exists(i + 1):
                        hidden(i + 1)
                    pe.wait_ge(s_msg, i + 2)
                    pe.wait_ge(s_rows, i + 1)
                    pe.nop(nofuse=True)
                    group_sums(pe, sum_p, same[:, s, :, :], msg).then_inc(s_sum, 1)
                    if exists(i + 2):
                        turn(q + 1, i + 2, s)

                pe.sem_inc(s_sum, 1)
                turn(0, 0, 0)
                hidden(0)
                turn(0, 1, 1)
                step(0, 0)
                step(0, 1)
                with pe.Fori(1, NB // 2 - 2) as q:
                    step(q, 0)
                    step(q, 1)
                for i in range(NB - 4, NB):
                    step(i // 2, i % 2)

            @block.vector
            def _(dve):
                def matrices(qj, s):
                    j = qj * 2 + s
                    dve.wait_ge(s_key[s], qj * 16 + 16)
                    if later(j):
                        dve.wait_ge(s_sum, j)
                    for u in range(TB):
                        ins = dve.tensor_scalar(same[:, s, u, :], keys[:, s, u // 2, :],
                                                dst_f[:, bass.ds(j * TB + u, 1)], None, ALU.is_equal)
                    ins.then_inc(s_same, 1)

                def index(qj, s):
                    if later(qj):
                        dve.wait_ge(s_add[s], qj * 64)
                    dve.nop(nofuse=True)
                    dve.tensor_copy(sidx[:, s, :],
                                    own_rows[:, bass.ds((qj * 2 + s) * TB, TB)]).then_inc(s_si, 1)

                def masks(qj, s):
                    j = qj * 2 + s
                    dve.wait_ge(s_rel[s], qj * 16 + 16)
                    if later(j):
                        dve.wait_ge(s_mp, j)
                    for b in range(NJ):
                        dve.wait_ge(s_hr, j * NJ + (b + 1))
                        ins = dve.scalar_tensor_tensor(out=hm[:, s, b, :], in0=rel[:, s, :], scalar=relc[:, b:b + 1],
                                                       in1=hr[:, b, :], op0=ALU.is_equal, op1=ALU.mult)
                    ins.then_inc(s_hm, 1)

                def step(q, s):
                    i = q * 2 + s
                    front = exists(i + 1)
                    if front:
                        matrices(q + s, 1 - s)
                    dve.wait_ge(s_mp, i + 1)
                    dve.wait_ge(s_sum, i + 1)
                    for u in range(TB):
                        ins = dve.tensor_scalar(msg[:, u, :], m_p[:, s, u, 0:D], norm[:, bass.ds(i * TB + u, 1)],
                                                None, ALU.mult)
                    ins.then_inc(s_msg, 1)
                    if front:
                        masks(q + s, 1 - s)
                        index(q + s, 1 - s)

                dve.sem_inc(s_msg, 1)
                matrices(0, 0)
                masks(0, 0)
                index(0, 0)
                step(0, 0)
                step(0, 1)
                with dve.Fori(1, NB // 2 - 2) as q:
                    step(q, 0)
                    step(q, 1)
                for i in range(NB - 4, NB):
                    step(i // 2, i % 2)
                for s in range(2):
                    dve.wait_ge(s_add[s], NB // 2 * 64)

        with ExitStack() as ph, nc.Block() as block:
            def tmp(name, shape, dt=F32):
                return ph.enter_context(nc.sbuf_tensor(name, shape, dt))

            xin = tmp("d3_x", [P, 2, CH, D])
            agg = tmp("d3_agg", [P, 2, CH, D])
            x = tmp("d3_sum", [P, 2, CH, D])
            sq = tmp("d3_sq", [P, 2, CH, D])
            stat = tmp("d3_stat", [P, 2, 3, CH])
            ln = Norm(x, sq, stat, 1)
            s_st = [sem(f"d3_stored{s}") for s in range(2)]
            s_res = sem("d3_result")
            s_v = sem("d3_chain")

            @block.sync
            def _(sp):
                stream(sp, [(x3_t, D, xin), (agg3_t, D, agg)], [(out, D, sq)], s_res, s_st)

            @block.scalar
            def _(act):
                def step(q, s):
                    c = q * 2 + s
                    if later(c):
                        ln.root(act, c - 1, 1 - s, 0)
                    ln.square(act, c, s, 0)

                chunks(act, step)
                ln.root(act, NC - 1, 1, 0)

            @block.vector
            def _(dve):
                n = [0, 0, 2 * 5]
                did, need = chain_of(dve, s_v, n)

                def finish(c, s):
                    ln.scale(dve, c, s, did, need, 0, sq).then_inc(s_res, 1)

                def step(q, s):
                    c = q * 2 + s
                    dve.wait_ge(s_ld[s], loaded(3, q))
                    need(did(dve.scalar_tensor_tensor(
                        out=x[:, s, :, :].rearrange("p f d -> p (f d)"),
                        in0=agg[:, s, :, :].rearrange("p f d -> p (f d)"), scalar=0.0,
                        in1=xin[:, s, :, :].rearrange("p f d -> p (f d)"), op0=ALU.max, op1=ALU.add)))
                    if later(c):
                        ln.variance(dve, c - 1, 1 - s, did, need, 0)
                    if later(q):
                        dve.wait_ge(s_st[s], q * 16)
                    ln.centre(dve, c, s, did, need, 0)
                    if later(c):
                        finish(c - 1, 1 - s)

                chunks(dve, step, n)
                ln.variance(dve, NC - 1, 1, did, need, 0)
                finish(NC - 1, 1)




def arrange(inputs):
    get = {k: np.asarray(v) for k, v in inputs.items()}
    f32, i32 = np.float32, np.int32
    xz = np.zeros((NP, XW), i32)
    xz[:N, 0:D] = get["x"].view(i32)
    xz[:N, D] = get["node_vec"].view(i32)
    xz[:N, D + 1] = get["node_type_119"]
    kind = np.zeros(NP, i32)
    kind[:N] = get["node_type_119"]

    def edges(v, fill=0):
        full = np.zeros((EP,) + v.shape[1:], v.dtype)
        full[:E] = v
        if len(v.shape) == 1 and fill:
            full[E:] = fill
        return full.reshape((P, T) + v.shape[1:])

    def columns(v):
        return np.concatenate([v, np.zeros((P, TB), v.dtype)], 1)

    def by_step(v):
        return np.ascontiguousarray(v.T).reshape(NB, TB * P)

    src = edges(get["src"].astype(i32), SPARE_SRC)
    dst = edges(get["dst"].astype(i32), SPARE_DST)
    ea = edges(get["edge_attr_40"])
    rel = edges(get["edge_type_8"].astype(i32))
    w2 = get["L2_gnn_W"]
    wl2 = np.zeros((2 * D + 1, 2 * D), f32)
    wl2[:D, :D] = w2.T
    wl2[D:2 * D, D:] = w2.T
    wl2[2 * D] = np.tile(get["L2_gnn_b"], 2)
    wr1, wr2, br1 = get["L3_gnn_weight1"], get["L3_gnn_weight2"], get["L3_gnn_bias1"]
    return {
        "xz": xz, "kind": kind[:, None],
        "src": columns(src), "dst": columns(dst), "src_rows": by_step(src), "dst_rows": by_step(dst),
        "rel_rows": by_step(rel),
        "ea": np.ascontiguousarray(ea.transpose(2, 1, 0)).reshape(R, T * P),
        "dist": edges(get["edge_weight"]), "norm": edges(get["edge_weight1"][:, 0]),
        "w1t": np.ascontiguousarray(get["L0_gnn_W1"].T), "b1": get["L0_gnn_b1"][:, None],
        "w2b": np.concatenate([get["L0_gnn_W2"].T, get["L0_gnn_b2"][None]], 0),
        "embt": np.ascontiguousarray(get["L0_gnn_emb"].T), "adwt": np.ascontiguousarray(get["L0_gnn_adaptW"].T),
        "gamma": get["L0_gnn_gamma"][None], "beta": get["L0_gnn_beta"][None],
        "jacobi": np.ascontiguousarray(jacobi_basis().T).reshape(1, -1),
        "lap": get["L1_gnn_lap_coefs"][None], "mf": get["L1_gnn_mf_weights"].reshape(1, -1),
        "wl2": wl2,
        "wr1": np.ascontiguousarray(wr1.transpose(1, 0, 2)).reshape(D, NREL * D),
        "br1": np.ascontiguousarray(np.tile(br1, NREL).reshape(3, P).T),
        "wr2": np.ascontiguousarray(wr2.reshape(3, P, D).transpose(1, 0, 2)).reshape(P, 3 * D),
        "relc": np.ascontiguousarray((np.arange(NREL * D) // D).astype(f32).reshape(3, P).T),
        "level": np.array([[(0 if k == 0 else 1 + (k - 1) % 2, 1 + k % 2) for k in range(K)]],
                          f32).reshape(1, -1) * NP,
        "b3": get["L3_gnn_bias2"][None],
    }


def kernel(**inputs):
    import concourse.bacc as bacc
    from concourse.bass_utils import run_bass_kernel_spmd

    nc = bacc.Bacc("TRN2", target_bir_lowering=False, num_devices=1)
    arrays = {"in_" + k: np.ascontiguousarray(v) for k, v in arrange(inputs).items()}
    a = {k[3:]: nc.dram_tensor(k, v.shape, mybir.dt.from_np(v.dtype), kind="ExternalInput").ap()
         for k, v in arrays.items()}
    out = nc.dram_tensor("out", (NP, D), F32, kind="ExternalOutput").ap()
    program(nc, a, out)
    r = run_bass_kernel_spmd(nc, [arrays], core_ids=[0])
    return r.results[0]["out"][:N]
```

```python
from contextlib import ExitStack

import numpy as np

import concourse.bass as bass
from concourse import mybir
from concourse.alu_op_type import AluOpType as ALU

ACT = mybir.ActivationFunctionType
AX = mybir.AxisListType
F32 = mybir.dt.float32
I32 = mybir.dt.int32
I16 = mybir.dt.int16
BF16 = mybir.dt.bfloat16

P = 128
N = 100000
E = 25000
D = 48
R = 40
NEL = 119
G = 32
NREL = 8
K = 10
CUTOFF = 6.0
EPS = 1e-5

LO = 1024
HI = -(-N // LO)
NP = HI * LO
NF = NP // P
T = 8 * (-(-E // (8 * P)))
EP = T * P
TB = 4
NB = T // TB
GE = 2 * P
SPARE_SRC, SPARE_DST = N, N + 1
SINK = N + 8
XW = D + 2
AW = D + 1
FILL = 49 * D
W0 = NF * AW // 28
W1 = NF * D // (NB // 2 - 1)
CH = 56
NC = NF // CH
W2 = NF * D // (2 * NC)
PI = float(np.pi)
REFINED = 3
assert NP == P * NF and NF % (2 * CH) == 0 and SINK + GE <= NP
assert T % 40 == 0


def jacobi_basis():
    import math
    a = b = 1.0
    rows = np.zeros((K + 1, K + 1))
    rows[0, 0] = 1.0
    rows[1, 0], rows[1, 1] = (a - b) / 2.0, (a + b + 2.0) / 2.0
    for n in range(2, K + 1):
        nab = 2 * n + a + b
        an = nab * (nab - 1) * (nab - 2) / (2 * n * (nab - n) * (nab - 2))
        bn = (nab - 1) * (a * a - b * b) / (2 * n * (nab - n) * (nab - 2))
        cn = -(2 * (n + a - 1) * (n + b - 1) * nab) / (2 * n * (nab - n) * (nab - 2))
        rows[n] = bn * rows[n - 1] + cn * rows[n - 2]
        rows[n, 1:] += an * rows[n - 1, :-1]
    for i in range(K + 1):
        t1 = math.pow(2.0, a + b + 1) / (2 * i + a + b + 1)
        t2 = math.exp(math.lgamma(i + a + 1) - math.lgamma(i + a + b + 1))
        t3 = math.exp(math.lgamma(i + b + 1) - math.lgamma(i + 1))
        rows[i] /= math.sqrt(t1 * t2 * t3)
    return rows.astype(np.float32)


def program(nc, a, out):
    with ExitStack() as ctx:
        def sb(name, shape, dt=F32):
            return ctx.enter_context(nc.sbuf_tensor(name, shape, dt))

        def psum(name, shape, dt=F32):
            return ctx.enter_context(nc.psum_tensor(name, shape, dt))

        def sem(name):
            return ctx.enter_context(nc.semaphore(name))

        def table(name, rows, width):
            return nc.dram_tensor(name, [rows, width], F32, kind="Internal").ap()

        xz_t = a["xz"]
        srow_t = table("srow_t", NP, 2)
        indeg_t = table("indeg_t", NP, 1)
        agg0_t = table("agg0_t", NP, AW)
        pow_t = table("pow_t", 4 * NP, D)
        y_t = table("y_t", NP, D)
        agg2_t = table("agg2_t", NP, D)
        agg3_t = table("agg3_t", NP, D)
        x2_t = table("x2_t", NP, D)
        x3_t = table("x3_t", NP, D)
        edge_t = table("edge_t", EP + 1, 4)
        prime_t = table("prime_t", 32, 4)
        x1_t = pow_t[0:NP, :]

        ident = sb("ident", [P, P])
        iota_lo = sb("iota_lo", [P, LO], I16)
        earlier = sb("earlier", [P, 2, GE])
        zeros = sb("zeros", [P, FILL])
        bias3 = sb("bias3", [P, FILL])
        sink = sb("sink", [P, TB])
        src_i = sb("src_i", [P, T + TB], I32)
        dst_i = sb("dst_i", [P, T + TB], I32)
        src_f = sb("src_f", [P, T])
        dst_f = sb("dst_f", [P, T])
        kind_s = sb("kind_s", [P, T])
        srows = sb("srows", [P, T, 2])
        dist = sb("dist", [P, T])
        cutw = sb("cutw", [P, T])
        norm = sb("norm", [P, T])
        w1t = sb("w1t", [R, D])
        b1c = sb("b1c", [D, 1])
        w2b = sb("w2b", [D + 1, D])
        embt = sb("embt", [G, NEL])
        adwt = sb("adwt", [G, G])
        vmat = sb("vmat", [G, NEL])
        kindm = sb("kindm", [NEL, NEL])
        gammab = sb("gammab", [P, D])
        betab = sb("betab", [P, D])
        halfpi = sb("halfpi", [P, 1])
        jac = sb("jac", [P, (K + 1) * (K + 1)])
        coef = sb("coef", [P, 6, K + 1])
        qk = sb("qk", [P, K + 2])
        wl2 = sb("wl2", [2 * D + 1, 2 * D])
        wr1 = sb("wr1", [D, NREL * D])
        br1 = sb("br1", [P, 3])
        wr2 = sb("wr2", [P, 3 * D])
        relc = sb("relc", [P, 3])
        b3b = sb("b3b", [P, D])

        s_ix = sem("indices_loaded")
        s_w = sem("weights_loaded")
        s_c = sem("constants_made")
        s_z = sem("zeros_made")
        s_agg0 = sem("agg0_cleared")
        s_pow = sem("power_tables_cleared")
        s_y = sem("filter_table_cleared")
        s_agg3 = sem("agg3_cleared")

        def piece(eng, tbl, tile, i, width, done):
            flat = tbl.rearrange("a b -> (a b)").rearrange("(p c) -> p c", p=P)
            eng.dma_start(flat[:, bass.ds(i * width, width)], tile[:, 0:width]).then_inc(done, 16)

        def pieces(tbl, width):
            assert tbl.shape[0] * tbl.shape[1] % (P * width) == 0 and width <= FILL
            return tbl.shape[0] * tbl.shape[1] // (P * width)

        WEIGHTS = [(w1t, "w1t"), (b1c, "b1"), (w2b, "w2b"), (embt, "embt"), (adwt, "adwt"),
                   (gammab, "gamma"), (betab, "beta"), (jac, "jacobi"), (coef[:, 0, :], "lap"),
                   (coef[:, 1, :], "mf"), (wl2, "wl2"), (wr1, "wr1"), (br1, "br1"),
                   (wr2, "wr2"), (relc, "relc"), (b3b, "b3"), (dist, "dist"), (norm, "norm")]
        BROADCAST = ("gamma", "beta", "jacobi", "lap", "mf", "b3")

        SR = 20

        with ExitStack() as ph, nc.Block() as block:
            def tmp(name, shape, dt=F32):
                return ph.enter_context(nc.sbuf_tensor(name, shape, dt))

            digit = tmp("digit", [P, 4, T], I32)
            digit_f = tmp("digit_f", [P, 4, T])
            hot_hi = tmp("hot_hi", [P, TB, 2, HI], BF16)
            hot_lo = tmp("hot_lo", [P, TB, 2, LO], BF16)
            srow = tmp("srow", [HI, LO, 2])
            stage = tmp("kind_stage", [P, 2, SR], I32)
            ring = tmp("kind_ring", [P, 2, SR], I32)
            kinds = tmp("kinds", [P, T], I32)
            indeg = tmp("indeg", [HI, LO])
            outdeg = tmp("outdeg", [HI, LO])
            deg_p = ph.enter_context(nc.psum_tensor("deg_p", [P, 2, LO], F32))
            mat_p = ph.enter_context(nc.psum_tensor("mat_p", [P, 512], F32))
            mat2_p = ph.enter_context(nc.psum_tensor("mat2_p", [P, 512], F32))
            s_dig = sem("digits_chain")
            s_hot = sem("onehots_made")
            s_hotu = sem("onehots_used")
            s_m = sem("kind_matrix")
            s_mc = sem("kind_matrix_copied")
            s_srow = sem("source_rows_made")
            s_sq = sem("outdegree_root")
            s_coef = sem("coefficients")
            s_st = sem("source_rows_stored")
            s_cut = sem("cutoff_weights")
            s_kst = sem("kind_index_staged")
            s_kg = [sem(f"kinds_got{h}") for h in range(2)]
            s_kd = sem("kinds_done")

            @block.sync
            def _(sp):
                sp.dma_start(src_i[:, :], a["src"]).then_inc(s_ix, 16)
                sp.dma_start(dst_i[:, :], a["dst"]).then_inc(s_ix, 16)
                for tile, name in WEIGHTS:
                    src = a[name].partition_broadcast(P) if name in BROADCAST else a[name]
                    dst = tile if isinstance(tile, bass.AP) else tile[:, :]
                    sp.dma_start(dst, src).then_inc(s_w, 16)
                sp.wait_ge(s_z, 1)
                early = [(agg0_t, W0, s_agg0), (pow_t[3 * NP:, :], W1, s_pow), (pow_t[NP:2 * NP, :], W1, s_pow)]
                total = sum(pieces(tbl, width) for tbl, width, _ in early)
                k = 0
                for tbl, width, done in early:
                    for i in range(pieces(tbl, width)):
                        if k * T // total > 0:
                            sp.wait_ge(s_hot, k * T // total)
                        piece(sp, tbl, zeros, i, width, done)
                        k += 1
                sp.wait_ge(s_srow, 2)
                sp.dma_start(srow_t.rearrange("(h l) c -> h (l c)", h=HI),
                             srow[:, :, :].rearrange("h l c -> h (l c)")).then_inc(s_st, 16)
                sp.dma_start(indeg_t.rearrange("(h l) c -> h (l c)", h=HI), indeg[:, :]).then_inc(s_st, 16)
                sp.wait_ge(s_st, 32)

            @block.gpsimd
            def _(pool):
                pool.iota(iota_lo[:, :], pattern=[[1, LO]], base=0, channel_multiplier=0).then_inc(s_c, 1)
                pool.memset(ident[:, :], 0.0).then_inc(s_c, 1)
                pool.memset(earlier[:, :, :], 1.0).then_inc(s_c, 1)
                pool.iota(sink[:, :], pattern=[[0, TB // 2], [P, 2]], base=SINK, channel_multiplier=1,
                          allow_small_or_imprecise_dtypes=True).then_inc(s_c, 1)
                pool.wait_ge(s_c, 4)
                pool.affine_select(out=ident[:, :], in_=ident[:, :], compare_op=ALU.not_equal, fill=1.0,
                                   base=0, pattern=[[-1, P]], channel_multiplier=1).then_inc(s_c, 1)
                for u in range(2):
                    pool.affine_select(out=earlier[:, u, :], in_=earlier[:, u, :], compare_op=ALU.is_gt,
                                       fill=0.0, base=u * P, pattern=[[-1, GE]],
                                       channel_multiplier=1).then_inc(s_c, 1)
                with pool.Fori(0, T // (2 * SR)) as i:
                    for h in range(2):
                        pool.wait_ge(s_kst, i * 2 + h + 1)
                        pool.nop(nofuse=True)
                        for u in range(SR):
                            pool.indirect_dma_start(
                                out=ring[:, h, u:u + 1], out_offset=None, in_=a["kind"],
                                in_offset=bass.IndirectOffsetOnAxis(ap=stage[:, h, u:u + 1], axis=0),
                            ).then_inc(s_kg[h], 16)

            @block.vector
            def _(dve):
                n = [0]

                def link(ins):
                    n[0] += 1
                    ins.then_inc(s_dig, 1)
                    dve.wait_ge(s_dig, n[0])

                dve.memset(zeros[:, :], 0.0).then_inc(s_z, 1)
                dve.memset(halfpi[:, :], PI / 2).then_inc(s_z, 1)
                dve.wait_ge(s_ix, 32)
                for j, ids in ((0, src_i), (2, dst_i)):
                    link(dve.tensor_scalar(digit[:, j, :], ids[:, 0:T], 10, None, ALU.logical_shift_right))
                    link(dve.tensor_scalar(digit[:, j + 1, :], ids[:, 0:T], LO - 1, None, ALU.bitwise_and))
                link(dve.tensor_copy(digit_f[:, :, :], digit[:, :, :]))
                link(dve.tensor_copy(src_f[:, :], src_i[:, 0:T]))
                link(dve.tensor_copy(dst_f[:, :], dst_i[:, 0:T]))
                dve.wait_ge(s_c, 7)
                dve.sem_inc(s_hotu, TB)
                with dve.Fori(0, NB) as i:
                    for u in range(TB):
                        for j in range(2):
                            if j == 0:
                                dve.wait_ge(s_hotu, i * TB + u + 1)
                            dve.tensor_scalar(hot_hi[:, u, j, :], iota_lo[:, 0:HI],
                                              digit_f[:, 2 * j, bass.ds(i * TB + u, 1)], None, ALU.is_equal)
                            ins = dve.tensor_scalar(hot_lo[:, u, j, :], iota_lo[:, :],
                                                    digit_f[:, 2 * j + 1, bass.ds(i * TB + u, 1)], None,
                                                    ALU.is_equal)
                        ins.then_inc(s_hot, 1)
                dve.wait_ge(s_w, 16 * len(WEIGHTS))
                link(dve.tensor_scalar(cutw[:, :], dist[:, :], CUTOFF, None, ALU.min))
                dve.sem_inc(s_cut, 1)
                dve.wait_ge(s_cut, 2)
                link(dve.tensor_scalar(cutw[:, :], cutw[:, :], 1.0, 0.5, ALU.add, ALU.mult))
                link(dve.tensor_scalar(dist[:, :], dist[:, :], CUTOFF, None, ALU.is_lt))
                link(dve.tensor_tensor(cutw[:, :], cutw[:, :], dist[:, :], ALU.mult))
                dve.wait_ge(s_m, 1)
                dve.tensor_copy(vmat[:, :], mat_p[0:G, 0:NEL]).then_inc(s_mc, 1)
                dve.wait_ge(s_m, 2)
                link(dve.tensor_copy(kindm[:, :], mat2_p[0:NEL, 0:NEL]))
                dve.wait_ge(s_coef, 1)
                link(dve.tensor_copy(coef[:, 3, 0:1], coef[:, 2, 0:1]))
                for i in range(1, K):
                    link(dve.tensor_tensor(coef[:, 3, i:i + 1], coef[:, 3, i - 1:i], coef[:, 2, i:i + 1],
                                           ALU.mult))
                link(dve.tensor_copy(coef[:, 4, 0:1], coef[:, 1, 0:1]))
                link(dve.tensor_tensor(coef[:, 4, 1:K + 1], coef[:, 1, 1:K + 1], coef[:, 3, 0:K], ALU.mult))
                jv = jac[:, :].rearrange("p (k i) -> p k i", i=K + 1)
                link(dve.tensor_tensor(jv, jv, coef[:, 4:5, :].to_broadcast([P, K + 1, K + 1]), ALU.mult))
                link(dve.tensor_reduce(qk[:, 0:K + 1], jv, AX.X, ALU.add))
                link(dve.tensor_scalar(qk[:, K + 1:K + 2], qk[:, 0:1], 1.0, None, ALU.add))
                dve.wait_ge(s_hotu, T + TB)
                link(dve.tensor_copy(srow[:, :, 0:1].rearrange("h l c -> h (l c)"), deg_p[0:HI, 1, :]))
                link(dve.tensor_scalar(outdeg[:, :], deg_p[0:HI, 0, :], 1.0, None, ALU.max))
                link(dve.reciprocal(outdeg[:, :], outdeg[:, :]))
                dve.sem_inc(s_sq, 1)
                dve.tensor_copy(indeg[:, :], deg_p[0:HI, 1, :]).then_inc(s_srow, 1)
                link(dve.tensor_copy(bias3[:, :].rearrange("p (n d) -> p n d", d=D),
                                     b3b[:, :].unsqueeze(1).to_broadcast([P, FILL // D, D])))
                dve.wait_ge(s_kd, T // SR)
                link(dve.tensor_copy(kind_s[:, :], kinds[:, :]))
                dve.wait_ge(s_sq, 2)

            @block.scalar
            def _(act):
                act.wait_ge(s_ix, 32)
                for h in range(2):
                    act.copy(stage[:, h, :], src_i[:, h * SR:(h + 1) * SR]).then_inc(s_kst, 1)
                with act.Fori(0, T // (2 * SR) - 1) as i:
                    for h in range(2):
                        act.wait_ge(s_kg[h], i * (16 * SR) + 16 * SR)
                        act.nop(nofuse=True)
                        act.copy(kinds[:, bass.ds((i * 2 + h) * SR, SR)], ring[:, h, :]).then_inc(s_kd, 1)
                        act.wait_ge(s_kd, i * 2 + h + 1)
                        act.nop(nofuse=True)
                        act.copy(stage[:, h, :], src_i[:, bass.ds((i * 2 + h + 2) * SR, SR)]).then_inc(s_kst, 1)
                for h in range(2):
                    act.wait_ge(s_kg[h], T // 2 * 16)
                    act.copy(kinds[:, T - (2 - h) * SR:T - (1 - h) * SR], ring[:, h, :]).then_inc(s_kd, 1)
                act.wait_ge(s_w, 16 * len(WEIGHTS))
                act.wait_ge(s_z, 2)
                act.wait_ge(s_cut, 1)
                act.activation(cutw[:, :], cutw[:, :], ACT.Sin, bias=halfpi[:, 0:1],
                               scale=-PI / CUTOFF).then_inc(s_cut, 1)
                act.activation(coef[:, 2, :], coef[:, 0, :], ACT.Tanh).then_inc(s_coef, 1)
                act.wait_ge(s_sq, 1)
                act.activation(srow[:, :, 1:2].rearrange("h l c -> h (l c)"), outdeg[:, :],
                               ACT.Sqrt).then_inc(s_sq, 1)
                act.wait_ge(s_sq, 2)
                act.sem_inc(s_srow, 1)

            @block.tensor
            def _(pe):
                pe.wait_ge(s_z, 1)
                for j in range(2):
                    for h in range(2):
                        pe.matmul(deg_p[0:HI, j, 512 * h:512 * h + 512], zeros[:, 0:HI],
                                  zeros[:, 0:512], start=True, stop=False, skip_group_check=True)
                with pe.Fori(0, NB) as i:
                    for u in range(TB):
                        pe.wait_ge(s_hot, i * TB + u + 1)
                        pe.nop(nofuse=True)
                        for j in range(2):
                            for h in range(2):
                                ins = pe.matmul(deg_p[0:HI, j, 512 * h:512 * h + 512], hot_hi[:, u, j, :],
                                                hot_lo[:, u, j, 512 * h:512 * h + 512], start=False,
                                                stop=False, skip_group_check=True)
                        ins.then_inc(s_hotu, 1)
                pe.wait_ge(s_w, 16 * len(WEIGHTS))
                pe.matmul(mat_p[0:G, 0:NEL], adwt[:, :], embt[:, :], start=True, stop=True).then_inc(s_m, 1)
                pe.wait_ge(s_mc, 1)
                pe.matmul(mat2_p[0:NEL, 0:NEL], embt[:, :], vmat[:, :], start=True, stop=True).then_inc(s_m, 1)

        def later(i):
            return not isinstance(i, int) or i > 0

        def exists(i):
            return not isinstance(i, int) or i < NB

        def edge_dmas(pool, xt, aggt, xg, gidx, rows, sidx, s_gi, s_gx, s_rows, s_si, s_add, lead=2):
            def gather(s, u):
                pool.indirect_dma_start(
                    out=xg[:, s, u, :], out_offset=None, in_=xt,
                    in_offset=bass.IndirectOffsetOnAxis(ap=gidx[:, s, u:u + 1], axis=0)).then_inc(s_gx[s], 16)

            def add(s, u):
                pool.indirect_dma_start(
                    out=aggt, out_offset=bass.IndirectOffsetOnAxis(ap=sidx[:, s, u:u + 1], axis=0),
                    in_=rows[:, s, u, :], in_offset=None, compute_op=ALU.add).then_inc(s_add[s], 16)

            def step(q, s):
                i = q * 2 + s
                pool.wait_ge(s_si, i + 1)
                pool.wait_ge(s_rows, i + 2)
                if later(i):
                    pool.wait_ge(s_add[1 - s], (q + s) * 64)
                pool.nop(nofuse=True)
                for g in range(2):
                    if g == 1:
                        pool.wait_ge(s_add[s], q * 64 + 32)
                        pool.nop(nofuse=True)
                    add(s, 2 * g)
                    add(s, 2 * g + 1)
                    if exists(i + lead):
                        if g == 0:
                            pool.wait_ge(s_gi, i + (lead + 1))
                            pool.nop(nofuse=True)
                        gather((s + lead) % 2, 2 * g)
                        gather((s + lead) % 2, 2 * g + 1)

            for j in range(lead):
                pool.wait_ge(s_gi, j + 1)
                for u in range(TB):
                    gather(j % 2, u)
            step(0, 0)
            step(0, 1)
            with pool.Fori(1, NB // 2 - 2) as q:
                step(q, 0)
                step(q, 1)
            for i in range(NB - 4, NB):
                step(i // 2, i % 2)

        def group_sums(pe, sum_p, same, msg):
            parts = msg if isinstance(msg, list) else [msg]
            width = parts[0].shape[2]
            for g in range(TB // 2):
                for c in range(2):
                    for r in range(2):
                        for part in parts:
                            ins = pe.matmul(sum_p[:, 2 * g + c, 0:width],
                                            same[:, 2 * g + r, c * P:(c + 1) * P], part[:, 2 * g + r, :],
                                            start=(r == 0 and part is parts[0]),
                                            stop=(r == 1 and part is parts[-1]))
            return ins

        with ExitStack() as ph, nc.Block() as block:
            def tmp(name, shape, dt=F32):
                return ph.enter_context(nc.sbuf_tensor(name, shape, dt))

            def ptmp(name, shape, dt=F32):
                return ph.enter_context(nc.psum_tensor(name, shape, dt))

            iota_f = tmp("iota_f", [P, NEL])
            keys = tmp("keys", [P, 2, TB // 2, GE], I32)
            same = tmp("same", [P, 2, TB, GE], BF16)
            junk = tmp("junk", [P, TB, GE])
            junk2 = tmp("junk2", [P, TB, NEL])
            rank = tmp("rank", [P, TB])
            sidx = tmp("sidx", [P, 2, TB], I32)
            gidx = tmp("gidx", [P, 2, TB], I32)
            xg = tmp("xg", [P, 2, TB, XW])
            kind_d = tmp("kind_d", [P, TB])
            hot = tmp("hot", [P, TB, NEL])
            hot_t = tmp("hot_t", [NEL, TB, P])
            logit = tmp("logit", [P, TB])
            wgt = tmp("wgt", [P, TB])
            gated = tmp("gated", [P, TB, D])
            msg = tmp("msg", [P, TB, AW])
            rest = tmp("rest", [P, TB, AW])
            parts = tmp("parts", [P, TB, 3, AW], BF16)
            rows = tmp("rows", [P, 2, TB, AW])
            ea = tmp("ea", [R, 2, TB * P])
            hid = tmp("hid", [D + 1, TB * P])
            hid_p = ptmp("hid_p", [P, 512])
            gate_p = ptmp("gate_p", [P, 2, TB, 128])
            hott_p = ptmp("hott_p", [P, TB, P])
            logit_p = ptmp("logit_p", [P, 2, TB, 128])
            sum_p = ptmp("sum_p", [P, TB, 128])
            s_ea = [sem(f"l0_edge_features{s}") for s in range(2)]
            s_key = [sem(f"l0_keys{s}") for s in range(2)]
            s_gx = [sem(f"l0_target_rows_got{s}") for s in range(2)]
            s_gi = sem("l0_gather_index")
            s_hp = sem("l0_hidden_product")
            s_hid = sem("l0_hidden")
            s_gate = sem("l0_gate")
            s_hot = sem("l0_onehots")
            s_hott = sem("l0_onehots_turned")
            s_hotc = sem("l0_turned_copied")
            s_lg = sem("l0_logit_rows")
            s_same = sem("l0_same")
            s_si = sem("l0_scatter_index")
            s_msg = sem("l0_messages")
            s_sum = sem("l0_sums")
            s_rows = sem("l0_rows")
            s_add = [sem(f"l0_added{s}") for s in range(2)]
            s_v = sem("l0_vector_chain")
            s_one = sem("l0_ones")

            @block.sync
            def _(sp):
                sp.sem_inc(s_hp, 1)
                sp.sem_inc(s_same, 1)
                def turn(q):
                    for s in range(2):
                        i = q * 2 + s
                        if later(i):
                            sp.wait_ge(s_hp, i)
                        sp.dma_start(ea[:, s, :], a["ea"][:, bass.ds(i * (TB * P), TB * P)]).then_inc(s_ea[s], 16)
                        if later(i):
                            sp.wait_ge(s_same, i)
                        sp.dma_start(keys[:, s, :, :].rearrange("p a b -> p (a b)"),
                                     a["src_rows"][bass.ds(i, 1), :].partition_broadcast(P)).then_inc(s_key[s], 16)

                turn(0)
                with sp.Fori(1, NB // 2) as q:
                    turn(q)
                    piece(sp, pow_t[2 * NP:3 * NP, :], zeros, q - 1, W1, s_pow)

            @block.gpsimd
            def _(pool):
                pool.iota(iota_f[:, :], pattern=[[1, NEL]], base=0, channel_multiplier=0,
                          allow_small_or_imprecise_dtypes=True).then_inc(s_one, 1)
                pool.wait_ge(s_agg0, 16 * pieces(agg0_t, W0))
                edge_dmas(pool, xz_t.bitcast(F32), agg0_t, xg, gidx, rows, sidx, s_gi, s_gx, s_rows, s_si, s_add)

            @block.scalar
            def _(act):
                def front(j):
                    act.wait_ge(s_hp, j + 2)
                    if later(j):
                        act.wait_ge(s_gate, j)
                    act.activation(hid[0:D, :], hid_p[0:D, :], ACT.Silu, bias=b1c[:, 0:1]).then_inc(s_hid, 1)
                    act.wait_ge(s_hott, j + 1)
                    if later(j):
                        act.wait_ge(s_lg, j)
                    act.activation(hot_t[:, :, :], hott_p[0:NEL, :, :], ACT.Copy).then_inc(s_hotc, 1)

                def step(q, s):
                    i = q * 2 + s
                    if exists(i + 1):
                        front(i + 1)
                    if exists(i + 2):
                        act.wait_ge(s_gx[s], q * 64 + 64)
                        act.nop(nofuse=True)
                        act.copy(gidx[:, s, :], dst_i[:, bass.ds((i + 2) * TB, TB)]).then_inc(s_gi, 1)
                    act.wait_ge(s_sum, i + 2)
                    if later(q):
                        act.wait_ge(s_add[s], q * 64)
                    act.activation(rows[:, s, :, :], sum_p[:, :, 0:AW], ACT.Copy).then_inc(s_rows, 1)

                act.sem_inc(s_rows, 1)
                for s in range(2):
                    act.copy(gidx[:, s, :], dst_i[:, s * TB:(s + 1) * TB]).then_inc(s_gi, 1)
                act.wait_ge(s_one, 2)
                front(0)
                step(0, 0)
                step(0, 1)
                with act.Fori(1, NB // 2 - 2) as q:
                    step(q, 0)
                    step(q, 1)
                for i in range(NB - 4, NB):
                    step(i // 2, i % 2)

            @block.tensor
            def _(pe):
                def front(qj, s):
                    j = qj * 2 + s
                    pe.wait_ge(s_ea[s], qj * 16 + 16)
                    if later(j):
                        pe.wait_ge(s_hid, j)
                        pe.wait_ge(s_hotc, j)
                    pe.nop(nofuse=True)
                    pe.matmul(hid_p[0:D, :], w1t[:, :], ea[:, s, :], start=True, stop=True).then_inc(s_hp, 1)
                    pe.wait_ge(s_hot, j + 1)
                    pe.nop(nofuse=True)
                    for u in range(TB):
                        ins = pe.transpose(hott_p[0:NEL, u, :], hot[:, u, :], ident[:, :])
                    ins.then_inc(s_hott, 1)
                    pe.wait_ge(s_hid, j + 1)
                    if later(j):
                        pe.wait_ge(s_msg, j)
                    pe.nop(nofuse=True)
                    for u in range(TB):
                        ins = pe.matmul(gate_p[:, s, u, 0:D], hid[:, u * P:(u + 1) * P], w2b[:, :],
                                        start=True, stop=True)
                    ins.then_inc(s_gate, 1)
                    pe.wait_ge(s_hotc, j + 1)
                    pe.nop(nofuse=True)
                    for u in range(TB):
                        ins = pe.matmul(logit_p[:, s, u, 0:NEL], hot_t[:, u, :], kindm[:, :], start=True, stop=True)
                    ins.then_inc(s_lg, 1)

                def step(q, s):
                    i = q * 2 + s
                    if exists(i + 1):
                        front(q + s, 1 - s)
                    pe.wait_ge(s_msg, i + 2)
                    pe.wait_ge(s_rows, i + 1)
                    pe.nop(nofuse=True)
                    group_sums(pe, sum_p, same[:, s, :, :], [parts[:, :, k, :] for k in range(3)]).then_inc(s_sum, 1)

                pe.sem_inc(s_sum, 1)
                front(0, 0)
                step(0, 0)
                step(0, 1)
                with pe.Fori(1, NB // 2 - 2) as q:
                    step(q, 0)
                    step(q, 1)
                for i in range(NB - 4, NB):
                    step(i // 2, i % 2)

            @block.vector
            def _(dve):
                STEPS = 8
                n = [0, 0]

                def chain(ins):
                    n[0] += 1
                    ins.then_inc(s_v, 1)
                    dve.wait_ge(s_v, n[1] + n[0])

                def onehots(j):
                    if later(j):
                        dve.wait_ge(s_hott, j)
                    for u in range(TB):
                        ins = dve.tensor_scalar(hot[:, u, :], iota_f[:, :],
                                                kind_s[:, bass.ds(j * TB + u, 1)], None, ALU.is_equal)
                    ins.then_inc(s_hot, 1)

                def matrices(qj, s):
                    j = qj * 2 + s
                    dve.wait_ge(s_key[s], qj * 16 + 16)
                    if later(j):
                        dve.wait_ge(s_sum, j)
                    for u in range(TB):
                        dve.tensor_scalar(same[:, s, u, :], keys[:, s, u // 2, :], src_f[:, bass.ds(j * TB + u, 1)],
                                          None, ALU.is_equal)
                    for u in range(TB):
                        ins = dve.scalar_tensor_tensor(out=junk[:, u, :], in0=keys[:, s, u // 2, :],
                                                       scalar=src_f[:, bass.ds(j * TB + u, 1)],
                                                       in1=earlier[:, u % 2, :], op0=ALU.is_equal, op1=ALU.mult,
                                                       accum_out=rank[:, u:u + 1])
                    ins.then_inc(s_same, 1)
                    dve.wait_ge(s_same, j + 2)
                    chain(dve.scalar_tensor_tensor(out=rank[:, :], in0=rank[:, :], scalar=1.0, in1=sink[:, :],
                                                   op0=ALU.min, op1=ALU.mult))
                    if later(qj):
                        dve.wait_ge(s_add[s], qj * 64)
                    dve.tensor_tensor(sidx[:, s, :], rank[:, :], src_f[:, bass.ds(j * TB, TB)],
                                      ALU.max).then_inc(s_si, 1)

                def step(q, s):
                    i = q * 2 + s
                    if exists(i + 1):
                        onehots(i + 1)
                    dve.wait_ge(s_gx[s], q * 64 + 64)
                    dve.wait_ge(s_sum, i + 1)
                    dve.tensor_tensor(wgt[:, :], cutw[:, bass.ds(i * TB, TB)], xg[:, s, :, D], ALU.mult)
                    dve.tensor_copy(msg[:, :, D], xg[:, s, :, D])
                    chain(dve.tensor_copy(kind_d[:, :], xg[:, s, :, D + 1].bitcast(I32)))
                    dve.wait_ge(s_lg, i + 1)
                    for u in range(TB):
                        ins = dve.scalar_tensor_tensor(out=junk2[:, u, :], in0=iota_f[:, :],
                                                       scalar=kind_d[:, u:u + 1], in1=logit_p[:, s, u, 0:NEL],
                                                       op0=ALU.is_equal, op1=ALU.mult,
                                                       accum_out=logit[:, u:u + 1])
                    chain(ins)
                    dve.wait_ge(s_gate, i + 1)
                    for u in range(TB):
                        ins = dve.scalar_tensor_tensor(out=gated[:, u, :], in0=gate_p[:, s, u, 0:D],
                                                       scalar=logit[:, u:u + 1], in1=xg[:, s, u, 0:D],
                                                       op0=ALU.add, op1=ALU.mult)
                    chain(ins)
                    for u in range(TB):
                        ins = dve.tensor_scalar(msg[:, u, 0:D], gated[:, u, :], wgt[:, u:u + 1], None, ALU.mult)
                    chain(ins)
                    chain(dve.tensor_copy(parts[:, :, 0, :], msg[:, :, :]))
                    chain(dve.tensor_tensor(rest[:, :, :], msg[:, :, :], parts[:, :, 0, :], ALU.subtract))
                    chain(dve.tensor_copy(parts[:, :, 1, :], rest[:, :, :]))
                    dve.tensor_tensor(parts[:, :, 2, :], rest[:, :, :], parts[:, :, 1, :],
                                      ALU.subtract).then_inc(s_msg, 1)
                    if exists(i + 1):
                        matrices(q + s, 1 - s)

                dve.sem_inc(s_msg, 1)
                dve.memset(hid[:, :], 1.0).then_inc(s_one, 1)
                dve.wait_ge(s_one, 2)
                onehots(0)
                matrices(0, 0)
                step(0, 0)
                step(0, 1)
                first = n[0]
                with dve.Fori(1, NB // 2 - 2) as q:
                    n[:] = [first, (q - 1) * (2 * STEPS)]
                    step(q, 0)
                    step(q, 1)
                    assert n[0] == first + 2 * STEPS
                n[:] = [first, (NB // 2 - 3) * (2 * STEPS)]
                for i in range(NB - 4, NB):
                    step(i // 2, i % 2)
                for s in range(2):
                    dve.wait_ge(s_add[s], NB // 2 * 64)

        indeg_n = sb("indeg_n", [P, NF])
        cj_n = sb("cj_n", [P, NF])
        dinv_n = sb("dinv_n", [P, NF])
        none_n = sb("none_n", [P, NF])

        s_ld = [sem(f"nodes_loaded{s}") for s in range(2)]

        def loaded(dense, i):
            return i * 32 + (dense * (16 * NC) + 32)

        def nodes(tbl, c, width):
            return tbl.rearrange("(p f) d -> p (f d)", p=P)[:, bass.ds(c * (CH * width), CH * width)]

        def stream(sp, loads, stores, s_res, s_st, beside=None):
            def load(c, s, tbl, width, tile):
                sp.dma_start(tile[:, s, :, :].rearrange("p f d -> p (f d)"),
                             nodes(tbl, c, width)).then_inc(s_ld[s], 16)

            def store(c, s):
                sp.wait_ge(s_res, c + 1)
                for tbl, width, tile in stores:
                    sp.dma_start(nodes(tbl, c, width),
                                 tile[:, s, :, :].rearrange("p f d -> p (f d)")).then_inc(s_st[s], 16)

            def step(q, s):
                c = q * 2 + s
                for tbl, width, tile, s_used, late in loads:
                    if late and not later(c) or isinstance(c, int) and c + 2 - late >= NC:
                        continue
                    sp.wait_ge(s_used, c + (1 - late))
                    load(c + (2 - late), (s + late) % 2, tbl, width, tile)
                if later(c):
                    store(c - 1, 1 - s)
                if beside:
                    beside(c)

            for c in range(2):
                for tbl, width, tile, _, _ in loads:
                    load(c, c, tbl, width, tile)
            chunks(sp, step)
            store(NC - 1, 1)
            for s in range(2):
                sp.wait_ge(s_st[s], 16 * len(stores) * (NC // 2))

        class Norm:
            s_cent = sem("norm_centred")
            s_sq = sem("norm_squared")
            s_var = sem("norm_variance")
            s_root = sem("norm_root")
            done = 0

            def __init__(self, x, sq, stat, per_chunk):
                self.x, self.sq, self.stat, self.per = x, sq, stat, per_chunk
                self.base = Norm.done
                Norm.done += per_chunk * NC

            def count(self, c, k):
                if self.per == 1:
                    return c + (self.base + 1)
                if k == 0:
                    return c * 2 + self.base if later(c) else self.base + 1
                return c * 2 + (self.base + (2 if isinstance(c, int) and c == NC - 1 else 3))

            def centre(self, dve, c, s, did, need, k):
                need(did(dve.tensor_reduce(self.stat[:, s, 0, :], self.x[:, s, :, :], AX.X, ALU.add)))
                need(did(dve.tensor_scalar(self.stat[:, s, 0, :], self.stat[:, s, 0, :], -1.0 / D, None,
                                           ALU.mult)))
                dve.tensor_tensor(self.x[:, s, :, :], self.x[:, s, :, :],
                                  self.stat[:, s, 0, :].unsqueeze(2).to_broadcast([P, CH, D]),
                                  ALU.add).then_inc(self.s_cent, 1)

            def variance(self, dve, c, s, did, need, k):
                dve.wait_ge(self.s_sq, self.count(c, k))
                need(did(dve.tensor_reduce(self.stat[:, s, 1, :], self.sq[:, s, :, :], AX.X, ALU.add)))
                dve.tensor_scalar(self.stat[:, s, 1, :], self.stat[:, s, 1, :], 1.0 / D, EPS, ALU.mult,
                                  ALU.add).then_inc(self.s_var, 1)

            def scale(self, dve, c, s, did, need, k, out):
                dve.wait_ge(self.s_root, self.count(c, k))
                need(did(dve.reciprocal(self.stat[:, s, 2, :], self.stat[:, s, 2, :])))
                return dve.tensor_tensor(out[:, s, :, :], self.x[:, s, :, :],
                                         self.stat[:, s, 2, :].unsqueeze(2).to_broadcast([P, CH, D]), ALU.mult)

            def square(self, act, c, s, k):
                act.wait_ge(self.s_cent, self.count(c, k))
                act.activation(self.sq[:, s, :, :], self.x[:, s, :, :], ACT.Square).then_inc(self.s_sq, 1)

            def root(self, act, c, s, k):
                act.wait_ge(self.s_var, self.count(c, k))
                act.activation(self.stat[:, s, 2, :], self.stat[:, s, 1, :], ACT.Sqrt).then_inc(self.s_root, 1)

        def chunks(eng, step, n=None, pause=None):
            tail = 4 if pause else 2
            step(0, 0)
            step(0, 1)
            first = n[0] if n else 0
            with eng.Fori(1, (NC - tail) // 2) as q:
                if n:
                    n[1] = (q - 1) * n[2]
                step(q, 0)
                step(q, 1)
            if n:
                assert n[0] == first + n[2], n[0] - first
                n[:2] = [first, ((NC - tail) // 2 - 1) * n[2]]
            if pause:
                pause()
            for c in range(NC - tail, NC):
                step(c // 2, c % 2)

        def chain_of(dve, s_v, n):
            def did(ins):
                n[0] += 1
                ins.then_inc(s_v, 1)
                return n[0]

            def need(k):
                dve.wait_ge(s_v, n[1] + k)
            return did, need

        TL = T + TB
        TOP = 256
        edge = sb("edge", [P, T, 4])
        filler = sb("filler", [1, 4])
        lst = sb("list", [P, TL, 4])
        key = sb("key", [P, T])
        best = sb("best", [P, 8])
        order = sb("order", [P, T + 8])
        live = sb("live", [P, T + 8])
        eid_f = sb("eid_f", [P, T + 8])
        eid = sb("eid", [P, T + 8], I32)
        ebase = sb("ebase", [P, 1])
        count = sb("count", [P, 1])
        sizes_f = sb("sizes_f", [1, 4])
        sizes = sb("sizes", [1, 4], I32)
        lidx = sb("p_lidx", [P, 2, 2], I32)
        lring = sb("p_lring", [P, 2, 2, 4])
        s_lv = sem("p_level_constants")
        s_edge = sem("p_edge_rows")
        s_edst = sem("p_edge_table")
        s_cnt = sem("p_count")
        s_cntt = sem("p_count_turned")
        s_nx = sem("p_list_sizes")
        s_ei = sem("p_edge_ids")
        s_li = sem("p_list_index")
        s_lg = [sem(f"p_list_rows{h}") for h in range(2)]
        s_lf = sem("p_list_ring_free")
        s_gx = sem("p_rows_got")
        s_addr = sem("p_added_powers")
        s_addy = sem("p_added_filter")
        s_cl = sem("p_cleared")
        s_fg = [sem(f"p_flag_rows{h}") for h in range(2)]
        s_chain = sem("p_chain")
        H2 = 2

        mark = []

        def list_chain(dve, register):
            here = [dve.snap(register), 0]

            def chain(ins):
                here[1] += 1
                ins.then_inc(s_chain, 1)
                dve.wait_ge(s_chain, here[0] + here[1])

            def settle():
                dve.reg_mov(register, here[0] + here[1])

            def resume():
                here[0], here[1] = dve.snap(register), 0
            return chain, settle, resume

        def size_and_sort(dve, k, cnt_p, chain, settle, resume):
            chain(dve.tensor_scalar(live[:, 0:T], key[:, :], 0.5, None, ALU.is_gt))
            dve.tensor_reduce(count[:, :], live[:, 0:T], AX.X, ALU.add).then_inc(s_cnt, 1)
            dve.wait_ge(s_cntt, k + 1)
            dve.nop(nofuse=True)
            chain(dve.tensor_reduce(sizes_f[:, 0:1], cnt_p[0:1, 0:P], AX.X, ALU.max))
            chain(dve.tensor_scalar(sizes_f[:, 0:1], sizes_f[:, 0:1], 3.0, None, ALU.add))
            chain(dve.tensor_copy(sizes[:, 0:1], sizes_f[:, 0:1]))
            chain(dve.tensor_scalar(sizes[:, 0:1], sizes[:, 0:1], 2, None, ALU.logical_shift_right))
            chain(dve.tensor_copy(sizes_f[:, 0:1], sizes[:, 0:1]))
            chain(dve.tensor_scalar(sizes_f[:, 0:1], sizes_f[:, 0:1], 1.0, None, ALU.max))
            chain(dve.tensor_scalar(sizes_f[:, 1:2], sizes_f[:, 0:1], 1.0, None, ALU.add))
            chain(dve.tensor_copy(sizes[:, :], sizes_f[:, :]))
            chain(dve.tensor_scalar(sizes[:, 1:2], sizes[:, 1:2], 1, None, ALU.logical_shift_right))
            dve.sem_inc(s_nx, 1)
            rounds = dve.value_load(sizes[0:1, 1:2], min_val=1, max_val=(NB + 1) // 2)
            settle()
            with dve.Fori(0, rounds) as r:
                resume()
                chain(dve.max(best[:, :], key[:, :]))
                dve.tensor_copy(order[:, bass.ds(r * 8, 8)], best[:, :])
                chain(dve.match_replace(key[:, :], best[:, :], key[:, :], 0.0))
                settle()
            resume()
            chain(dve.tensor_scalar(live[:, :], order[:, :], 1.0, None, ALU.min))
            chain(dve.tensor_scalar(eid_f[:, :], order[:, :], -1.0, ebase[:, 0:1], ALU.mult, ALU.add))
            chain(dve.tensor_tensor(eid_f[:, :], eid_f[:, :], live[:, :], ALU.mult))
            chain(dve.tensor_scalar(eid[:, :], eid_f[:, :], float(EP), None, ALU.add))
            dve.sem_inc(s_ei, 1)

        with ExitStack() as ph, nc.Block() as block:
            def tmp(name, shape, dt=F32):
                return ph.enter_context(nc.sbuf_tensor(name, shape, dt))

            xin = tmp("d0_x", [P, 2, CH, XW])
            agg = tmp("d0_agg", [P, 2, CH, AW])
            x = tmp("d0_sum", [P, 2, CH, D])
            sq = tmp("d0_sq", [P, 2, CH, D])
            stat = tmp("d0_stat", [P, 2, 3, CH])
            stage = tmp("sr_stage", [P, 2, SR], I32)
            ring = tmp("sr_ring", [P, 2, SR, 2])
            cnt_p = ph.enter_context(nc.psum_tensor("d0_count_p", [P, 512], F32))
            ln = Norm(x, sq, stat, 2)
            s_st = [sem(f"d0_stored{s}") for s in range(2)]
            s_used = sem("d0_features_used")
            s_aggu = sem("d0_sums_used")
            s_sc = sem("d0_scaled")
            s_aff = sem("d0_gamma_beta")
            s_res = sem("d0_result")
            s_v = sem("d0_chain")
            s_n = sem("node_degrees")
            s_nr = sem("node_roots")
            s_stage = sem("source_index_staged")
            s_got = [sem(f"source_rows_got{h}") for h in range(2)]
            s_kept = sem("source_rows_kept")

            @block.sync
            def _(sp):
                sp.dma_start(indeg_n[:, :], indeg_t.rearrange("(p f) c -> p (f c)", p=P)).then_inc(s_n, 16)

                def clear_filter(c):
                    for u in range(2):
                        piece(sp, y_t, zeros, c * 2 + u, W2, s_y)

                stream(sp, [(agg0_t, AW, agg, s_aggu, 0), (xz_t.bitcast(F32), XW, xin, s_used, 1)],
                       [(x1_t, D, sq)], s_res, s_st, clear_filter)

            @block.tensor
            def _(pe):
                pe.wait_ge(s_cnt, 1)
                pe.transpose(cnt_p[0:1, 0:P], count[:, 0:1], ident[:, :]).then_inc(s_cntt, 1)

            @block.gpsimd
            def _(pool):
                pool.iota(ebase[:, :], pattern=[[0, 1]], base=TOP - EP, channel_multiplier=T,
                          allow_small_or_imprecise_dtypes=True).then_inc(s_lv, 1)
                pool.iota(edge[:, :, 3:4].rearrange("p t c -> p (t c)"), pattern=[[1, T]], base=0,
                          channel_multiplier=0, allow_small_or_imprecise_dtypes=True).then_inc(s_lv, 1)

                def keep(h, at):
                    pool.nop(nofuse=True)
                    pool.tensor_copy(srows[:, :, :].rearrange("p t c -> p (t c)")[:, at],
                                     ring[:, h, :, :].rearrange("p t c -> p (t c)")).then_inc(s_kept, 1)

                def gather(h, at):
                    pool.nop(nofuse=True)
                    pool.tensor_copy(stage[:, h, :], src_i[:, at]).then_inc(s_stage, 1)

                def fetch(h):
                    pool.nop(nofuse=True)
                    for u in range(SR):
                        pool.indirect_dma_start(
                            out=ring[:, h, u, :], out_offset=None, in_=srow_t,
                            in_offset=bass.IndirectOffsetOnAxis(ap=stage[:, h, u:u + 1], axis=0),
                        ).then_inc(s_got[h], 16)

                for h in range(2):
                    gather(h, slice(h * SR, (h + 1) * SR))
                    pool.wait_ge(s_stage, h + 1)
                    fetch(h)
                with pool.Fori(0, T // (2 * SR) - 1) as i:
                    for h in range(2):
                        pool.wait_ge(s_got[h], i * (16 * SR) + 16 * SR)
                        keep(h, bass.ds((i * 2 + h) * (2 * SR), 2 * SR))
                        gather(h, bass.ds((i * 2 + h + 2) * SR, SR))
                        pool.wait_ge(s_kept, i * 2 + h + 1)
                        pool.wait_ge(s_stage, i * 2 + h + 3)
                        fetch(h)
                for h in range(2):
                    pool.wait_ge(s_got[h], T // 2 * 16)
                    keep(h, slice((T - (2 - h) * SR) * 2, (T - (1 - h) * SR) * 2))

                primed = [s_gx, s_addr, s_addy, s_cl] * TB + (s_lg + s_fg) * H2
                for j, done in enumerate(primed):
                    pool.dma_start(prime_t[j:j + 1, :], zeros[0:1, 0:4]).then_inc(done, 16)

                pool.sem_inc(s_li, 2)
                pool.sem_inc(s_lf, 4)
                pool.wait_ge(s_edge, 1)
                pool.dma_start(edge_t[0:EP, :].rearrange("(p t) c -> p (t c)", p=P),
                               edge[:, :, :].rearrange("p t c -> p (t c)")).then_inc(s_edst, 16)
                pool.dma_start(edge_t[EP:EP + 1, :], filler[:, :]).then_inc(s_edst, 16)
                pool.wait_ge(s_nx, 1)
                pool.nop(nofuse=True)
                steps = pool.value_load(sizes[0:1, 0:1], min_val=1, max_val=NB)
                pool.wait_ge(s_ei, 1)
                pool.wait_ge(s_edst, 32)
                pool.nop(nofuse=True)
                flat = lst[:, :, :].rearrange("p t c -> p (t c)")
                with pool.Fori(0, steps) as i:
                    for h in range(2):
                        pool.tensor_copy(lidx[:, h, :], eid[:, bass.ds(i * TB + h * H2, H2)]).then_inc(s_li, 1)
                    for h in range(2):
                        pool.wait_ge(s_li, i * 2 + (h + 3))
                        pool.wait_ge(s_lf, i * 2 + (h + 3))
                        pool.nop(nofuse=True)
                        for u in range(H2):
                            pool.indirect_dma_start(
                                out=lring[:, h, u, :], out_offset=None, in_=edge_t,
                                in_offset=bass.IndirectOffsetOnAxis(ap=lidx[:, h, u:u + 1], axis=0),
                            ).then_inc(s_lg[h], 16)
                    for h in range(2):
                        pool.wait_ge(s_lg[h], i * (16 * H2) + 32 * H2)
                        pool.nop(nofuse=True)
                        pool.tensor_copy(flat[:, bass.ds(i * (4 * TB) + h * (4 * H2), 4 * H2)],
                                         lring[:, h, :, :].rearrange("p t c -> p (t c)")).then_inc(s_lf, 1)
                pool.wait_ge(s_lf, steps * 2 + 4)
                for done in (s_gx, s_addr, s_addy, s_cl):
                    pool.wait_ge(done, 16 * TB)
                for done in s_fg:
                    pool.wait_ge(done, 16 * H2)

            @block.scalar
            def _(act):
                act.wait_ge(s_nr, 1)
                act.activation(cj_n[:, :], cj_n[:, :], ACT.Sqrt).then_inc(s_nr, 1)

                def step(q, s):
                    c = q * 2 + s
                    ln.square(act, c, s, 0)
                    if later(c):
                        ln.square(act, c - 1, 1 - s, 1)
                    ln.root(act, c, s, 0)
                    if later(c):
                        ln.root(act, c - 1, 1 - s, 1)
                    act.wait_ge(s_sc, c + 1)
                    for d in range(D):
                        ins = act.activation(x[:, s, :, d], x[:, s, :, d], ACT.Identity,
                                             bias=betab[:, d:d + 1], scale=gammab[:, d:d + 1])
                    ins.then_inc(s_aff, 1)

                chunks(act, step)
                ln.square(act, NC - 1, 1, 1)
                ln.root(act, NC - 1, 1, 1)

            @block.vector
            def _(dve):
                n = [0, 0, 2 * 13]
                did, need = chain_of(dve, s_v, n)

                def again(c, s):
                    dve.wait_ge(s_aff, c + 1)
                    need(did(dve.tensor_tensor(x[:, s, :, :], x[:, s, :, :], xin[:, s, :, 0:D], ALU.add)))
                    dve.sem_inc(s_used, 1)
                    ln.centre(dve, c, s, did, need, 1)

                def finish(c, s):
                    ln.scale(dve, c, s, did, need, 1, sq).then_inc(s_res, 1)

                def step(q, s):
                    c = q * 2 + s
                    if later(q):
                        dve.wait_ge(s_res, c - 1)
                    dve.wait_ge(s_ld[s], loaded(0, q))
                    need(did(dve.tensor_scalar(stat[:, s, 0, :], agg[:, s, :, D], 1e-8, None, ALU.max)))
                    need(did(dve.reciprocal(stat[:, s, 1, :], stat[:, s, 0, :])))
                    need(did(dve.tensor_tensor(x[:, s, :, :], agg[:, s, :, 0:D],
                                               stat[:, s, 1, :].unsqueeze(2).to_broadcast([P, CH, D]),
                                               ALU.mult)))
                    dve.sem_inc(s_aggu, 1)
                    need(did(dve.tensor_tensor(x[:, s, :, :], x[:, s, :, :], xin[:, s, :, 0:D], ALU.add)))
                    if later(q):
                        dve.wait_ge(s_st[s], q * 16)
                    ln.centre(dve, c, s, did, need, 0)
                    if later(c):
                        again(c - 1, 1 - s)
                    ln.variance(dve, c, s, did, need, 0)
                    if later(c):
                        ln.variance(dve, c - 1, 1 - s, did, need, 1)
                    ln.scale(dve, c, s, did, need, 0, x).then_inc(s_sc, 1)
                    if later(c):
                        finish(c - 1, 1 - s)

                dve.wait_ge(s_n, 16)
                need(did(dve.tensor_scalar(cj_n[:, :], indeg_n[:, :], 1.0, None, ALU.max)))
                dve.reciprocal(cj_n[:, :], cj_n[:, :]).then_inc(s_nr, 1)
                need(did(dve.tensor_scalar(indeg_n[:, :], indeg_n[:, :], 1.0, None, ALU.min)))
                need(did(dve.tensor_scalar(none_n[:, :], indeg_n[:, :], -1.0, 1.0, ALU.mult, ALU.add)))
                dve.wait_ge(s_nr, 2)
                need(did(dve.tensor_tensor(dinv_n[:, :], cj_n[:, :], indeg_n[:, :], ALU.mult)))
                mark.append(dve.alloc_register("dve_mark"))
                dve.reg_mov(mark[0], 0)

                def list_edges():
                    chain, settle, resume = list_chain(dve, mark[0])
                    dve.wait_ge(s_lv, 2)
                    dve.wait_ge(s_kept, T // SR)
                    dve.tensor_copy(edge[:, :, 0], src_f[:, :])
                    dve.tensor_copy(edge[:, :, 1], dst_f[:, :])
                    dve.tensor_copy(edge[:, :, 2], srows[:, :, 0])
                    dve.memset(order[:, :], 0.0)
                    chain(dve.memset(filler[:, :], 0.0))
                    dve.memset(sizes_f[:, :], 1.0)
                    dve.memset(filler[:, 0:1], float(SPARE_SRC))
                    dve.memset(filler[:, 1:2], float(SPARE_DST))
                    dve.memset(filler[:, 2:3], 1.0)
                    dve.memset(lst[:, :, :], 1.0)
                    chain(dve.tensor_scalar(key[:, :], edge[:, :, 3], -1.0, float(TOP), ALU.mult, ALU.add))
                    dve.sem_inc(s_edge, 1)
                    chain(dve.tensor_scalar(live[:, 0:T], edge[:, :, 2], 1.0, None, ALU.min))
                    chain(dve.tensor_tensor(key[:, :], key[:, :], live[:, 0:T], ALU.mult))
                    size_and_sort(dve, 0, cnt_p, chain, settle, resume)
                    dve.nop(nofuse=True)
                    settle()

                chunks(dve, step, n, list_edges)
                again(NC - 1, 1)
                ln.variance(dve, NC - 1, 1, did, need, 1)
                finish(NC - 1, 1)

        with ExitStack() as ph, nc.Block() as block:
            def tmp(name, shape, dt=F32):
                return ph.enter_context(nc.sbuf_tensor(name, shape, dt))

            def ptmp(name, shape, dt=F32):
                return ph.enter_context(nc.psum_tensor(name, shape, dt))

            own_dst = tmp("own_dst", [P, TL])
            w_k = tmp("w_k", [P, TL])
            zero_in = tmp("zero_in", [P, TL])
            ttop = tmp("ttop", [P, TL])
            gi = tmp("gi", [P, TL], I32)
            ri = tmp("ri", [P, TL], I32)
            ci = tmp("ci", [P, TL], I32)
            level = tmp("level", [P, 3 * K])
            off = tmp("off", [P, 2])
            qcur = tmp("qcur", [P, 1])
            gidx = tmp("p_gidx", [P, TB], I32)
            sidx_r = tmp("p_sidx_r", [P, TB], I32)
            sidx_y = tmp("p_sidx_y", [P, TB], I32)
            cidx = tmp("p_cidx", [P, TB], I32)
            fidx = tmp("p_fidx", [P, 2, 2], I32)
            fring = tmp("p_fring", [P, 2, 2, D])
            fjunk = tmp("p_fjunk", [P, 2, 2, D])
            fcount = tmp("p_fcount", [P, 2, 2])
            xg = tmp("p_xg", [P, TB, D])
            xc = tmp("p_xc", [P, TB, D])
            dkey = tmp("p_dkey", [P, TB])
            keys = tmp("p_keys", [P, TB, P])
            same = tmp("p_same", [P, TB, GE])
            junk = tmp("p_junk", [P, TB, GE])
            rank = tmp("p_rank", [P, TB])
            msg = tmp("p_msg", [P, TB, D])
            rows_r = tmp("p_rows_r", [P, TB, D])
            rows_y = tmp("p_rows_y", [P, TB, D])
            keys_p = ptmp("keys_p", [P, TB, P])
            sum_p = ptmp("psum_p", [P, TB, 128])
            cnt_p = ptmp("cnt_p", [P, 512])
            s_go = sem("p_level_ready")
            s_q = sem("p_coefficient")
            s_gi = sem("p_gather_index")
            s_xc = sem("p_rows_copied")
            s_dk = sem("p_target_keys")
            s_kt = sem("p_keys_turned")
            s_kc = sem("p_keys_copied")
            s_sir = sem("p_power_index")
            s_siy = sem("p_filter_index")
            s_msg = sem("p_messages")
            s_sum = sem("p_sums")
            s_rr = sem("p_power_rows_ready")
            s_ry = sem("p_filter_rows_ready")
            s_ci = sem("p_clear_index")
            s_fi = sem("p_flag_index")
            s_ff = sem("p_flag_ring_free")
            s_root = sem("p_first_weights")

            class Levels:

                def __init__(self, eng, tag):
                    self.eng = eng
                    self.reg = {x: eng.alloc_register(f"{tag}_{x}") for x in ("n", "c", "m", "b")}
                    eng.wait_ge(s_nx, 1)
                    for x in ("c", "b"):
                        eng.reg_mov(self.reg[x], 1)
                    self.first = self.sizes()

                def sizes(self):
                    self.eng.nop(nofuse=True)
                    n, m = (self.eng.value_load(sizes[0:1, j:j + 1], min_val=1, max_val=NB) for j in (0, 2))
                    self.eng.reg_mov(self.reg["n"], n)
                    self.eng.reg_mov(self.reg["m"], m)
                    return n

                def here(self):
                    return [self.eng.snap(self.reg[x]) for x in ("n", "c", "m", "b")]

                def passed(self, n, c, m, b):
                    self.eng.reg_mov(self.reg["b"], b + m)
                    self.eng.reg_mov(self.reg["m"], n)
                    self.eng.reg_mov(self.reg["c"], c + n)

            @block.sync
            def _(sp):
                sp.dma_start(level[:, :], a["level"].partition_broadcast(P)).then_inc(s_lv, 16)

            @block.gpsimd
            def _(pool):
                def build(n, c):
                    with pool.Fori(0, n) as i:
                        for h in range(2):
                            pool.wait_ge(s_li, (c + i) * 2 + (h + 1))
                            pool.wait_ge(s_lf, (c + i) * 2 + (h + 1))
                            pool.nop(nofuse=True)
                            for u in range(H2):
                                pool.indirect_dma_start(
                                    out=lring[:, h, u, :], out_offset=None, in_=edge_t,
                                    in_offset=bass.IndirectOffsetOnAxis(ap=lidx[:, h, u:u + 1], axis=0),
                                ).then_inc(s_lg[h], 16)

                def gather(u):
                    pool.indirect_dma_start(
                        out=xg[:, u, :], out_offset=None, in_=pow_t,
                        in_offset=bass.IndirectOffsetOnAxis(ap=gidx[:, u:u + 1], axis=0)).then_inc(s_gx, 16)

                def add(tbl, idx, rows, done, u):
                    pool.indirect_dma_start(
                        out=tbl, out_offset=bass.IndirectOffsetOnAxis(ap=idx[:, u:u + 1], axis=0),
                        in_=rows[:, u, :], in_offset=None, compute_op=ALU.add).then_inc(done, 16)

                lv = Levels(pool, "pool")
                pool.wait_ge(s_pow, 48 * pieces(y_t, W1))
                pool.wait_ge(s_y, 16 * pieces(y_t, W2))
                def power(k, refine):
                    n, c, m, b = lv.here()
                    pool.wait_ge(s_gi, c + k + 1)
                    pool.nop(nofuse=True)
                    for u in range(TB):
                        gather(u)
                    pool.wait_ge(s_cl, b * 64)
                    pool.nop(nofuse=True)
                    with pool.Fori(0, n) as i:
                        pool.wait_ge(s_xc, c + i + 1)
                        pool.wait_ge(s_gi, c + k + i + 2)
                        pool.nop(nofuse=True)
                        gather(0)
                        gather(1)
                        for g in range(2):
                            if g == 1:
                                gather(2)
                                gather(3)
                            for tbl, idx, rows, done, ready, sent in (
                                    (pow_t, sidx_r, rows_r, s_addr, s_rr, s_sir),
                                    (y_t, sidx_y, rows_y, s_addy, s_ry, s_siy)):
                                if g == 0:
                                    pool.wait_ge(ready, c + i + 1)
                                    pool.wait_ge(sent, c + i + 1)
                                pool.wait_ge(done, (c + i) * 64 + 32 * g)
                                pool.nop(nofuse=True)
                                for u in (2 * g, 2 * g + 1):
                                    add(tbl, idx, rows, done, u)
                    pool.wait_ge(s_gx, (c + k + n + 1) * 64)
                    pool.nop(nofuse=True)
                    with pool.Fori(0, m) as i:
                        pool.wait_ge(s_ci, b + i + 1)
                        pool.nop(nofuse=True)
                        for u in range(TB):
                            if u == GE // P:
                                pool.wait_ge(s_cl, (b + i) * 64 + 32)
                                pool.nop(nofuse=True)
                            pool.indirect_dma_start(
                                out=pow_t, out_offset=bass.IndirectOffsetOnAxis(ap=cidx[:, u:u + 1], axis=0),
                                in_=zeros[:, 0:D], in_offset=None).then_inc(s_cl, 16)
                    lv.passed(n, c, m, b)
                    pool.wait_ge(s_addr, (c + n) * 64)
                    pool.nop(nofuse=True)
                    if refine:
                        with pool.Fori(0, n) as i:
                            for h in range(2):
                                pool.wait_ge(s_fi, (c + i) * 2 + (h + 1))
                                pool.wait_ge(s_ff, (c + i) * 2 + (h + 1))
                                pool.nop(nofuse=True)
                                for u in range(H2):
                                    pool.indirect_dma_start(
                                        out=fring[:, h, u, :], out_offset=None, in_=pow_t,
                                        in_offset=bass.IndirectOffsetOnAxis(ap=fidx[:, h, u:u + 1], axis=0),
                                    ).then_inc(s_fg[h], 16)
                        pool.wait_ge(s_nx, k + 2)
                        build(lv.sizes(), c + n)

                with pool.Fori(0, REFINED) as k:
                    power(k, True)
                with pool.Fori(REFINED, K) as k:
                    power(k, False)

            @block.scalar
            def _(act):
                def build(n, c):
                    with act.Fori(0, n) as i:
                        for h in range(2):
                            act.wait_ge(s_lg[h], (c + i) * (16 * H2))
                            act.nop(nofuse=True)
                            act.copy(lidx[:, h, :], eid[:, bass.ds(i * TB + h * H2, H2)]).then_inc(s_li, 1)

                for done, v in ((s_gi, 1), (s_xc, 1), (s_kc, 1), (s_rr, 1), (s_ry, 1), (s_ci, 1), (s_fi, 2)):
                    act.sem_inc(done, v)
                lv = Levels(act, "act")
                act.wait_ge(s_root, 1)
                act.activation(w_k[:, :], w_k[:, :], ACT.Sqrt).then_inc(s_root, 1)
                def power(k, refine):
                    n, c, m, b = lv.here()
                    act.wait_ge(s_go, k * 2 + 1)
                    act.wait_ge(s_gx, (c + k) * 64)
                    act.nop(nofuse=True)
                    act.copy(qcur[:, :], qk[:, bass.ds(k + 1, 1)]).then_inc(s_q, 1)
                    act.copy(gidx[:, :], gi[:, 0:TB]).then_inc(s_gi, 1)
                    act.wait_ge(s_q, k + 1)
                    with act.Fori(0, n) as i:
                        act.wait_ge(s_kt, c + i + 1)
                        act.wait_ge(s_siy, c + i)
                        act.activation(keys[:, :, :], keys_p[:, :, :], ACT.Copy).then_inc(s_kc, 1)
                        act.wait_ge(s_gx, (c + k + i) * 64 + 64)
                        act.wait_ge(s_msg, c + i)
                        act.nop(nofuse=True)
                        act.copy(xc[:, :, :], xg[:, :, :]).then_inc(s_xc, 1)
                        act.copy(gidx[:, :], gi[:, bass.ds(i * TB + TB, TB)]).then_inc(s_gi, 1)
                        act.wait_ge(s_sum, c + i + 1)
                        act.wait_ge(s_addr, (c + i) * 64)
                        act.activation(rows_r[:, :, :], sum_p[:, :, 0:D], ACT.Copy).then_inc(s_rr, 1)
                        act.wait_ge(s_addy, (c + i) * 64)
                        act.activation(rows_y[:, :, :], sum_p[:, :, 0:D], ACT.Copy,
                                       scale=qcur[:, 0:1]).then_inc(s_ry, 1)
                    act.wait_ge(s_go, k * 2 + 2)
                    with act.Fori(0, m) as i:
                        act.wait_ge(s_cl, (b + i) * 64)
                        act.nop(nofuse=True)
                        act.copy(cidx[:, :], ci[:, bass.ds(i * TB, TB)]).then_inc(s_ci, 1)
                    lv.passed(n, c, m, b)
                    if refine:
                        with act.Fori(0, n) as i:
                            for h in range(2):
                                act.wait_ge(s_fg[h], (c + i) * (16 * H2))
                                act.nop(nofuse=True)
                                act.copy(fidx[:, h, :], ri[:, bass.ds(i * TB + h * H2, H2)]).then_inc(s_fi, 1)
                        act.wait_ge(s_nx, k + 2)
                        new = lv.sizes()
                        act.wait_ge(s_ei, k + 2)
                        build(new, c + n)

                with act.Fori(0, REFINED) as k:
                    power(k, True)
                with act.Fori(REFINED, K) as k:
                    power(k, False)

            @block.tensor
            def _(pe):
                for done in (s_kt, s_sum):
                    pe.sem_inc(done, 1)
                lv = Levels(pe, "pe")
                def power(k, refine):
                    n, c, m, b = lv.here()
                    with pe.Fori(0, n) as i:
                        pe.wait_ge(s_dk, c + i + 1)
                        pe.wait_ge(s_kc, c + i)
                        pe.nop(nofuse=True)
                        for u in range(TB):
                            ins = pe.transpose(keys_p[:, u, :], dkey[:, u:u + 1].to_broadcast([P, P]), ident[:, :])
                        ins.then_inc(s_kt, 1)
                        pe.wait_ge(s_msg, c + i + 1)
                        pe.wait_ge(s_ry, c + i)
                        pe.nop(nofuse=True)
                        group_sums(pe, sum_p, same, msg).then_inc(s_sum, 1)
                    lv.passed(n, c, m, b)
                    if refine:
                        pe.wait_ge(s_cnt, k + 2)
                        pe.nop(nofuse=True)
                        pe.transpose(cnt_p[0:1, 0:P], count[:, 0:1], ident[:, :]).then_inc(s_cntt, 1)
                        pe.wait_ge(s_nx, k + 2)
                        lv.sizes()

                with pe.Fori(0, REFINED) as k:
                    power(k, True)
                with pe.Fori(REFINED, K) as k:
                    power(k, False)

            @block.vector
            def _(dve):
                chain, settle, resume = list_chain(dve, mark[0])

                def build(n, c):
                    flat = lst[:, :, :].rearrange("p t c -> p (t c)")
                    with dve.Fori(0, n) as i:
                        for h in range(2):
                            dve.wait_ge(s_lg[h], (c + i) * (16 * H2) + 16 * H2)
                            dve.nop(nofuse=True)
                            ins = dve.tensor_copy(flat[:, bass.ds(i * (4 * TB) + h * (4 * H2), 4 * H2)],
                                                  lring[:, h, :, :].rearrange("p t c -> p (t c)"))
                            ins.then_inc(s_lf, 1)
                    dve.wait_ge(s_lf, (c + n) * 2 + 2)
                    dve.nop(nofuse=True)

                dve.wait_ge(s_lv, 18)
                for done, v in ((s_dk, 1), (s_msg, 1), (s_sir, 1), (s_siy, 1), (s_ff, 4)):
                    dve.sem_inc(done, v)
                chain(dve.memset(own_dst[:, :], 0.0))
                chain(dve.tensor_copy(own_dst[:, 0:TB], sink[:, :]))
                dve.nop(nofuse=True)
                settle()
                lv = Levels(dve, "dve")
                dve.reciprocal(w_k[:, :], lst[:, :, 2]).then_inc(s_root, 1)
                dve.wait_ge(s_root, 2)
                def power(k, refine):
                    n, c, m, b = lv.here()
                    resume()
                    dve.wait_ge(s_siy, c)
                    dve.wait_ge(s_kt, c)
                    dve.nop(nofuse=True)
                    chain(dve.tensor_copy(off[:, :], level[:, bass.ds(k * 2, 2)]))
                    dve.wait_ge(s_gi, c + k)
                    dve.nop(nofuse=True)
                    dve.tensor_scalar(gi[:, :], lst[:, :, 0], off[:, 0:1], None, ALU.add).then_inc(s_go, 1)
                    dve.tensor_copy(dkey[:, :], lst[:, 0:TB, 1])
                    dve.wait_ge(s_ci, b)
                    dve.nop(nofuse=True)
                    chain(dve.tensor_scalar(ci[:, :], own_dst[:, :], off[:, 0:1], None, ALU.add))
                    if refine:
                        dve.tensor_scalar(ri[:, :], lst[:, :, 0], off[:, 1:2], None, ALU.add)
                        dve.tensor_scalar(ttop[:, :], lst[:, :, 3], -1.0, float(TOP), ALU.mult, ALU.add)
                        chain(dve.memset(zero_in[:, :], float(D)))
                    dve.sem_inc(s_go, 1)
                    settle()
                    with dve.Fori(0, n) as i:
                        resume()
                        dve.wait_ge(s_kt, c + i)
                        chain(dve.tensor_copy(dkey[:, :], lst[:, bass.ds(i * TB, TB), 1]))
                        dve.sem_inc(s_dk, 1)
                        dve.wait_ge(s_kc, c + i + 1)
                        dve.wait_ge(s_sum, c + i)
                        for u in range(TB):
                            kg = keys[:, 2 * (u // 2):2 * (u // 2) + 2, :].rearrange("p a b -> p (a b)")
                            dve.tensor_scalar(same[:, u, :], kg, dkey[:, u:u + 1], None, ALU.is_equal)
                        for u in range(TB):
                            kg = keys[:, 2 * (u // 2):2 * (u // 2) + 2, :].rearrange("p a b -> p (a b)")
                            ins = dve.scalar_tensor_tensor(out=junk[:, u, :], in0=kg, scalar=dkey[:, u:u + 1],
                                                           in1=earlier[:, u % 2, :], op0=ALU.is_equal,
                                                           op1=ALU.mult, accum_out=rank[:, u:u + 1])
                        chain(ins)
                        chain(dve.scalar_tensor_tensor(out=rank[:, :], in0=rank[:, :], scalar=1.0, in1=sink[:, :],
                                                   op0=ALU.min, op1=ALU.mult))
                        chain(dve.tensor_tensor(rank[:, :], rank[:, :], dkey[:, :], ALU.max))
                        dve.nop(nofuse=True)
                        chain(dve.tensor_copy(own_dst[:, bass.ds(i * TB, TB)], rank[:, :]))
                        dve.wait_ge(s_xc, c + i + 1)
                        dve.nop(nofuse=True)
                        ins = dve.tensor_tensor(msg[:, :, :], xc[:, :, :],
                                                w_k[:, bass.ds(i * TB, TB)].unsqueeze(2).to_broadcast([P, TB, D]),
                                                ALU.mult)
                        chain(ins)
                        dve.sem_inc(s_msg, 1)
                        dve.wait_ge(s_addr, (c + i) * 64)
                        dve.nop(nofuse=True)
                        dve.tensor_scalar(sidx_r[:, :], rank[:, :], off[:, 1:2], None, ALU.add).then_inc(s_sir, 1)
                        dve.wait_ge(s_addy, (c + i) * 64)
                        dve.nop(nofuse=True)
                        dve.tensor_copy(sidx_y[:, :], rank[:, :]).then_inc(s_siy, 1)
                        settle()
                    lv.passed(n, c, m, b)
                    if refine:
                        with dve.Fori(0, n) as i:
                            resume()
                            for h in range(2):
                                dve.wait_ge(s_fg[h], (c + i) * (16 * H2) + 16 * H2)
                                for u in range(H2):
                                    ins = dve.tensor_scalar(fjunk[:, h, u, :], fring[:, h, u, :], 0.0, 0.0,
                                                            ALU.is_equal, ALU.add, accum_out=fcount[:, h, u:u + 1])
                                chain(ins)
                                dve.sem_inc(s_ff, 1)
                                chain(dve.tensor_copy(zero_in[:, bass.ds(i * TB + h * H2, H2)], fcount[:, h, :]))
                            settle()
                        resume()
                        chain(dve.scalar_tensor_tensor(out=key[:, :], in0=zero_in[:, 0:T], scalar=D - 0.5,
                                                       in1=ttop[:, 0:T], op0=ALU.is_lt, op1=ALU.mult))
                        dve.nop(nofuse=True)
                        chain(dve.tensor_scalar(sizes_f[:, 2:3], sizes_f[:, 0:1],
                                                level[0:1, bass.ds(k + 2 * K, 1)], 1.0, ALU.mult, ALU.max))
                        size_and_sort(dve, k + 1, cnt_p, chain, settle, resume)
                        build(lv.sizes(), c + n)
                        chain(dve.reciprocal(w_k[:, :], lst[:, :, 2]))
                        settle()

                with dve.Fori(0, REFINED) as k:
                    power(k, True)
                with dve.Fori(REFINED, K) as k:
                    power(k, False)

        with ExitStack() as ph, nc.Block() as block:
            def tmp(name, shape, dt=F32):
                return ph.enter_context(nc.sbuf_tensor(name, shape, dt))

            xin = tmp("d1_x", [P, 2, CH, D])
            yin = tmp("d1_y", [P, 2, CH, D])
            x = tmp("d1_sum", [P, 2, CH, D])
            own = tmp("d1_own", [P, 2, CH, D])
            sq = tmp("d1_sq", [P, 2, CH, D])
            stat = tmp("d1_stat", [P, 2, 3, CH])
            ln = Norm(x, sq, stat, 1)
            s_st = [sem(f"d1_stored{s}") for s in range(2)]
            s_used = sem("d1_inputs_used")
            s_res = sem("d1_result")
            s_v = sem("d1_chain")

            @block.sync
            def _(sp):
                stream(sp, [(x1_t, D, xin, s_used, 0), (y_t, D, yin, s_used, 0)], [(x2_t, D, sq), (agg2_t, D, own)],
                       s_res, s_st)

            @block.scalar
            def _(act):
                def step(q, s):
                    c = q * 2 + s
                    if later(c):
                        ln.root(act, c - 1, 1 - s, 0)
                    ln.square(act, c, s, 0)

                chunks(act, step)
                ln.root(act, NC - 1, 1, 0)

            @block.vector
            def _(dve):
                n = [0, 0, 2 * 7]
                did, need = chain_of(dve, s_v, n)

                def finish(q, s):
                    need(did(ln.scale(dve, q * 2 + s, s, did, need, 0, sq)))
                    dve.tensor_tensor(
                        own[:, s, :, :], sq[:, s, :, :],
                        none_n[:, bass.ds((q * 2 + s) * CH, CH)].unsqueeze(2).to_broadcast([P, CH, D]),
                        ALU.mult).then_inc(s_res, 1)

                def step(q, s):
                    c = q * 2 + s
                    if later(q):
                        dve.wait_ge(s_res, c - 1)
                    dve.wait_ge(s_ld[s], loaded(1, q))
                    need(did(dve.tensor_tensor(
                        yin[:, s, :, :], yin[:, s, :, :],
                        dinv_n[:, bass.ds(c * CH, CH)].unsqueeze(2).to_broadcast([P, CH, D]), ALU.mult)))
                    need(did(dve.scalar_tensor_tensor(
                        out=x[:, s, :, :].rearrange("p f d -> p (f d)"),
                        in0=xin[:, s, :, :].rearrange("p f d -> p (f d)"), scalar=qk[:, K + 1:K + 2],
                        in1=yin[:, s, :, :].rearrange("p f d -> p (f d)"), op0=ALU.mult, op1=ALU.add)))
                    dve.sem_inc(s_used, 1)
                    if later(c):
                        ln.variance(dve, c - 1, 1 - s, did, need, 0)
                    if later(q):
                        dve.wait_ge(s_st[s], q * 32)
                    ln.centre(dve, c, s, did, need, 0)
                    if later(c):
                        finish(q - 1 + s, 1 - s)

                chunks(dve, step, n)
                ln.variance(dve, NC - 1, 1, did, need, 0)
                finish(NC // 2 - 1, 1)

        own_rows = sb("own_rows", [P, T], I32)
        with ExitStack() as ph, nc.Block() as block:
            def tmp(name, shape, dt=F32):
                return ph.enter_context(nc.sbuf_tensor(name, shape, dt))

            keys = tmp("e2_keys", [P, 2, TB // 2, GE], I32)
            same = tmp("e2_same", [P, 2, TB, GE])
            junk = tmp("e2_junk", [P, TB, GE])
            rank = tmp("e2_rank", [P, TB])
            sidx = tmp("e2_sidx", [P, 2, TB], I32)
            gidx = tmp("e2_gidx", [P, 2, TB], I32)
            xg = tmp("e2_xg", [P, 2, TB, D])
            msg = tmp("e2_msg", [P, TB, D])
            rows = tmp("e2_rows", [P, 2, TB, D])
            sum_p = ph.enter_context(nc.psum_tensor("e2_sum", [P, TB, 128], F32))
            s_key = [sem(f"e2_keys_loaded{s}") for s in range(2)]
            s_gx = [sem(f"e2_rows_got{s}") for s in range(2)]
            s_gi = sem("e2_gather_index")
            s_same = sem("e2_same")
            s_si = sem("e2_scatter_index")
            s_msg = sem("e2_messages")
            s_sum = sem("e2_sums")
            s_rows = sem("e2_rows_ready")
            s_add = [sem(f"e2_added{s}") for s in range(2)]
            s_v = sem("e2_chain")

            @block.sync
            def _(sp):
                sp.sem_inc(s_same, 1)
                def turn(q):
                    for s in range(2):
                        i = q * 2 + s
                        if later(i):
                            sp.wait_ge(s_same, i)
                        sp.dma_start(keys[:, s, :, :].rearrange("p a b -> p (a b)"),
                                     a["dst_rows"][bass.ds(i, 1), :].partition_broadcast(P)).then_inc(s_key[s], 16)

                turn(0)
                with sp.Fori(1, pieces(agg3_t, FILL) + 1) as q:
                    turn(q)
                    piece(sp, agg3_t, bias3, q - 1, FILL, s_agg3)
                with sp.Fori(pieces(agg3_t, FILL) + 1, NB // 2) as q:
                    turn(q)

            @block.gpsimd
            def _(pool):
                edge_dmas(pool, x2_t, agg2_t, xg, gidx, rows, sidx, s_gi, s_gx, s_rows, s_si, s_add)

            @block.scalar
            def _(act):
                def step(q, s):
                    i = q * 2 + s
                    if exists(i + 2):
                        act.wait_ge(s_gx[s], q * 64 + 64)
                        act.nop(nofuse=True)
                        act.copy(gidx[:, s, :], src_i[:, bass.ds((i + 2) * TB, TB)]).then_inc(s_gi, 1)
                    act.wait_ge(s_sum, i + 2)
                    if later(q):
                        act.wait_ge(s_add[s], q * 64)
                    act.activation(rows[:, s, :, :], sum_p[:, :, 0:D], ACT.Copy).then_inc(s_rows, 1)

                act.sem_inc(s_rows, 1)
                for s in range(2):
                    act.copy(gidx[:, s, :], src_i[:, s * TB:(s + 1) * TB]).then_inc(s_gi, 1)
                step(0, 0)
                step(0, 1)
                with act.Fori(1, NB // 2 - 2) as q:
                    step(q, 0)
                    step(q, 1)
                for i in range(NB - 4, NB):
                    step(i // 2, i % 2)

            @block.tensor
            def _(pe):
                pe.sem_inc(s_sum, 1)
                with pe.Fori(0, NB // 2) as q:
                    for s in range(2):
                        i = q * 2 + s
                        pe.wait_ge(s_msg, i + 1)
                        pe.wait_ge(s_rows, i + 1)
                        pe.nop(nofuse=True)
                        group_sums(pe, sum_p, same[:, s, :, :], msg).then_inc(s_sum, 1)

            @block.vector
            def _(dve):
                STEPS = 3
                n = [0, 0]

                def chain(ins):
                    n[0] += 1
                    ins.then_inc(s_v, 1)
                    dve.wait_ge(s_v, n[1] + n[0])

                def matrices(qj, s):
                    j = qj * 2 + s
                    dve.wait_ge(s_key[s], qj * 16 + 16)
                    if later(j):
                        dve.wait_ge(s_sum, j)
                    for u in range(TB):
                        dve.tensor_scalar(same[:, s, u, :], keys[:, s, u // 2, :], dst_f[:, bass.ds(j * TB + u, 1)],
                                          None, ALU.is_equal)
                    for u in range(TB):
                        ins = dve.scalar_tensor_tensor(out=junk[:, u, :], in0=keys[:, s, u // 2, :],
                                                       scalar=dst_f[:, bass.ds(j * TB + u, 1)],
                                                       in1=earlier[:, u % 2, :], op0=ALU.is_equal, op1=ALU.mult,
                                                       accum_out=rank[:, u:u + 1])
                    ins.then_inc(s_same, 1)
                    dve.wait_ge(s_same, j + 2)
                    chain(dve.scalar_tensor_tensor(out=rank[:, :], in0=rank[:, :], scalar=1.0, in1=sink[:, :],
                                                   op0=ALU.min, op1=ALU.mult))
                    chain(dve.tensor_tensor(rank[:, :], rank[:, :], dst_f[:, bass.ds(j * TB, TB)], ALU.max))
                    dve.tensor_copy(own_rows[:, bass.ds(j * TB, TB)], rank[:, :])
                    if later(qj):
                        dve.wait_ge(s_add[s], qj * 64)
                    dve.nop(nofuse=True)
                    dve.tensor_copy(sidx[:, s, :], rank[:, :]).then_inc(s_si, 1)

                def step(q, s):
                    i = q * 2 + s
                    dve.wait_ge(s_gx[s], q * 64 + 64)
                    dve.wait_ge(s_sum, i + 1)
                    for u in range(TB):
                        ins = dve.tensor_scalar(
                            msg[:, u, :], xg[:, s, u, :],
                            srows[:, bass.ds(i * TB + u, 1), 1:2].rearrange("p a b -> p (a b)"), None, ALU.mult)
                    chain(ins)
                    dve.sem_inc(s_msg, 1)
                    if exists(i + 1):
                        matrices(q + s, 1 - s)

                matrices(0, 0)
                step(0, 0)
                step(0, 1)
                first = n[0]
                with dve.Fori(1, NB // 2 - 2) as q:
                    n[:] = [first, (q - 1) * (2 * STEPS)]
                    step(q, 0)
                    step(q, 1)
                    assert n[0] == first + 2 * STEPS
                n[:] = [first, (NB // 2 - 3) * (2 * STEPS)]
                for i in range(NB - 4, NB):
                    step(i // 2, i % 2)
                for s in range(2):
                    dve.wait_ge(s_add[s], NB // 2 * 64)

        with ExitStack() as ph, nc.Block() as block:
            def tmp(name, shape, dt=F32):
                return ph.enter_context(nc.sbuf_tensor(name, shape, dt))

            def ptmp(name, shape, dt=F32):
                return ph.enter_context(nc.psum_tensor(name, shape, dt))

            NG = CH // 8
            xin = tmp("d2_x", [P, 2, CH, D])
            agg = tmp("d2_agg", [P, 2, CH, D])
            x = tmp("d2_sum", [P, 2, CH, D])
            sq = tmp("d2_sq", [P, 2, CH, D])
            stat = tmp("d2_stat", [P, 2, 3, CH])
            ht = tmp("d2_turned", [2 * D + 1, 2, 4 * P])
            ht_p = ptmp("d2_turned_p", [P, 512])
            hw_p = ptmp("d2_product", [P, NG, 512])
            ln = Norm(x, sq, stat, 1)
            s_st = [sem(f"d2_stored{s}") for s in range(2)]
            s_used = sem("d2_inputs_used")
            s_res = sem("d2_result")
            s_v = sem("d2_chain")
            s_h = sem("d2_h")
            s_ht = sem("d2_turned")
            s_hc = sem("d2_turned_copied")
            s_hw = sem("d2_product")
            s_hr = sem("d2_product_used")

            @block.sync
            def _(sp):
                stream(sp, [(x2_t, D, xin, s_used, 0), (agg2_t, D, agg, s_used, 0)], [(x3_t, D, sq)], s_res, s_st)

            @block.tensor
            def _(pe):
                def turn(c, s, g):
                    if g == 0:
                        pe.wait_ge(s_h, c + 2)
                    if g > 0 or later(c):
                        pe.wait_ge(s_hc, c * NG + g)
                    pe.nop(nofuse=True)
                    for j in range(4):
                        pair = agg[:, s, 8 * g + 2 * j:8 * g + 2 * j + 2, :].rearrange("p f d -> p (f d)")
                        ins = pe.transpose(ht_p[0:2 * D, j * P:(j + 1) * P], pair, ident[:, :])
                    ins.then_inc(s_ht, 1)

                def product(c, s, g):
                    pe.wait_ge(s_hc, c * NG + (g + 1))
                    if later(c):
                        pe.wait_ge(s_hr, c * NG + (g + 1 - NG))
                    pe.nop(nofuse=True)
                    for j in range(4):
                        ins = pe.matmul(hw_p[:, g, 2 * D * j:2 * D * (j + 1)], ht[:, (s + g) % 2, j * P:(j + 1) * P],
                                        wl2[:, :], start=True, stop=True)
                    ins.then_inc(s_hw, 1)

                def step(q, s):
                    c = q * 2 + s
                    turn(c, s, 0)
                    for g in range(NG):
                        if g + 1 < NG:
                            pe.wait_ge(s_hc, c * NG + (g + 1))
                            turn(c, s, g + 1)
                        product(c, s, g)

                chunks(pe, step)

            @block.scalar
            def _(act):
                def step(q, s):
                    c = q * 2 + s
                    for g in range(NG):
                        act.wait_ge(s_ht, c * NG + (g + 1))
                        if g > 1 or later(c):
                            act.wait_ge(s_hw, c * NG + (g - 1))
                        act.activation(ht[0:2 * D, (s + g) % 2, :], ht_p[0:2 * D, :], ACT.Copy).then_inc(s_hc, 1)
                        if g == 4 and later(c):
                            ln.square(act, c - 1, 1 - s, 0)
                            ln.root(act, c - 1, 1 - s, 0)

                chunks(act, step)
                ln.square(act, NC - 1, 1, 0)
                ln.root(act, NC - 1, 1, 0)

            @block.vector
            def _(dve):
                n = [0, 0, 2 * 4]
                did, need = chain_of(dve, s_v, n)

                def scaled(q, s):
                    dve.wait_ge(s_ld[s], loaded(2, q))
                    dve.tensor_tensor(
                        agg[:, s, :, :], agg[:, s, :, :],
                        cj_n[:, bass.ds((q * 2 + s) * CH, CH)].unsqueeze(2).to_broadcast([P, CH, D]),
                        ALU.mult).then_inc(s_h, 1)

                def step(q, s):
                    c = q * 2 + s
                    if not isinstance(c, int) or c + 1 < NC:
                        scaled(q + s, 1 - s)
                    if later(q):
                        dve.wait_ge(s_res, c - 1)
                    for g in range(NG):
                        dve.wait_ge(s_hw, c * NG + (g + 1))
                        grp = slice(8 * g, 8 * g + 8)
                        ins = dve.scalar_tensor_tensor(
                            out=x[:, s, grp, :].rearrange("p f d -> p (f d)"),
                            in0=hw_p[:, g, 0:8 * D], scalar=0.0,
                            in1=xin[:, s, grp, :].rearrange("p f d -> p (f d)"), op0=ALU.max, op1=ALU.add)
                        ins.then_inc(s_hr, 1)
                    dve.wait_ge(s_hr, c * NG + NG)
                    dve.nop(nofuse=True)
                    dve.sem_inc(s_used, 1)
                    if later(q):
                        dve.wait_ge(s_st[s], q * 16)
                    ln.centre(dve, c, s, did, need, 0)
                    ln.variance(dve, c, s, did, need, 0)
                    ln.scale(dve, c, s, did, need, 0, sq).then_inc(s_res, 1)

                dve.memset(ht[:, :, :], 1.0).then_inc(s_h, 1)
                scaled(0, 0)
                chunks(dve, step, n)

        with ExitStack() as ph, nc.Block() as block:
            def tmp(name, shape, dt=F32):
                return ph.enter_context(nc.sbuf_tensor(name, shape, dt))

            def ptmp(name, shape, dt=F32):
                return ph.enter_context(nc.psum_tensor(name, shape, dt))

            NJ = NREL * D // P
            keys = tmp("e3_keys", [P, 2, TB // 2, GE], I32)
            rel = tmp("e3_rel", [P, 2, TB * P], I32)
            same = tmp("e3_same", [P, 2, TB, GE], BF16)
            sidx = tmp("e3_sidx", [P, 2, TB], I32)
            gidx = tmp("e3_gidx", [P, 2, TB], I32)
            xg = tmp("e3_xg", [P, 2, TB, D])
            xt = tmp("e3_turned", [D, TB * P])
            hr = tmp("e3_hidden", [P, NJ, TB * P])
            hm = tmp("e3_masked", [P, 2, NJ, TB * P])
            msg = tmp("e3_msg", [P, TB, D])
            rest = tmp("e3_rest", [P, TB, D])
            parts = tmp("e3_parts", [P, TB, 3, D], BF16)
            rows = tmp("e3_rows", [P, 2, TB, D])
            xt_p = ptmp("e3_turned_p", [P, TB, P])
            h_p = ptmp("e3_hidden_p", [P, NJ, TB * P])
            m_p = ptmp("e3_message_p", [P, 2, TB, 128])
            sum_p = ptmp("e3_sum", [P, TB, 128])
            s_key = [sem(f"e3_keys_loaded{s}") for s in range(2)]
            s_rel = [sem(f"e3_kinds_loaded{s}") for s in range(2)]
            s_gx = [sem(f"e3_rows_got{s}") for s in range(2)]
            s_gi = sem("e3_gather_index")
            s_xt = sem("e3_rows_turned")
            s_xtc = sem("e3_turned_copied")
            s_hp = sem("e3_hidden_products")
            s_hr = sem("e3_hidden")
            s_hm = sem("e3_masked")
            s_mp = sem("e3_message_products")
            s_same = sem("e3_same")
            s_msg = sem("e3_messages")
            s_sum = sem("e3_sums")
            s_rows = sem("e3_rows_ready")
            s_si = sem("e3_scatter_index")
            s_v = sem("e3_chain")
            s_add = [sem(f"e3_added{s}") for s in range(2)]

            @block.sync
            def _(sp):
                sp.sem_inc(s_same, 1)
                sp.sem_inc(s_hm, 1)
                def turn(q):
                    for s in range(2):
                        i = q * 2 + s
                        if later(i):
                            sp.wait_ge(s_same, i)
                        sp.dma_start(keys[:, s, :, :].rearrange("p a b -> p (a b)"),
                                     a["dst_rows"][bass.ds(i, 1), :].partition_broadcast(P)).then_inc(s_key[s], 16)
                        if later(i):
                            sp.wait_ge(s_hm, i)
                        sp.dma_start(rel[:, s, :], a["rel_rows"][bass.ds(i, 1), :].partition_broadcast(P)
                                     ).then_inc(s_rel[s], 16)

                turn(0)
                with sp.Fori(1, NB // 2) as q:
                    turn(q)

            @block.gpsimd
            def _(pool):
                pool.wait_ge(s_agg3, 16 * pieces(agg3_t, FILL))
                edge_dmas(pool, x3_t, agg3_t, xg, gidx, rows, sidx, s_gi, s_gx, s_rows, s_si, s_add, lead=3)

            @block.scalar
            def _(act):
                def turned(j):
                    act.wait_ge(s_xt, j + 1)
                    if later(j):
                        act.wait_ge(s_hp, j * NJ)
                    act.activation(xt[:, :], xt_p[0:D, :, :].rearrange("p a b -> p (a b)"),
                                   ACT.Copy).then_inc(s_xtc, 1)

                def hidden(j):
                    for b in range(NJ):
                        act.wait_ge(s_hp, j * NJ + (b + 1))
                        act.wait_ge(s_hm, j + 1)
                        act.activation(hr[:, b, :], h_p[:, b, :], ACT.Relu, bias=br1[:, b:b + 1]).then_inc(s_hr, 1)

                def step(q, s):
                    i = q * 2 + s
                    if exists(i + 3):
                        act.nop(nofuse=True)
                        act.copy(gidx[:, 1 - s, :], src_i[:, bass.ds((i + 3) * TB, TB)]).then_inc(s_gi, 1)
                    if exists(i + 1):
                        hidden(i + 1)
                    act.wait_ge(s_sum, i + 2)
                    if later(q):
                        act.wait_ge(s_add[s], q * 64)
                    act.activation(rows[:, s, :, :], sum_p[:, :, 0:D], ACT.Copy).then_inc(s_rows, 1)
                    if exists(i + 2):
                        turned(i + 2)

                act.sem_inc(s_rows, 1)
                for s in range(2):
                    act.copy(gidx[:, s, :], src_i[:, s * TB:(s + 1) * TB]).then_inc(s_gi, 1)
                turned(0)
                hidden(0)
                turned(1)
                act.copy(gidx[:, 0, :], src_i[:, 2 * TB:3 * TB]).then_inc(s_gi, 1)
                step(0, 0)
                step(0, 1)
                with act.Fori(1, NB // 2 - 2) as q:
                    step(q, 0)
                    step(q, 1)
                for i in range(NB - 4, NB):
                    step(i // 2, i % 2)

            @block.tensor
            def _(pe):
                def turn(q, j, s):
                    pe.wait_ge(s_gx[s], q * 64 + 64)
                    if later(j):
                        pe.wait_ge(s_xtc, j)
                    pe.nop(nofuse=True)
                    for u in range(TB):
                        ins = pe.transpose(xt_p[0:D, u, :], xg[:, s, u, :], ident[:, :])
                    ins.then_inc(s_xt, 1)

                def hidden(j):
                    pe.wait_ge(s_xtc, j + 1)
                    if later(j):
                        pe.wait_ge(s_hr, j * NJ)
                    pe.nop(nofuse=True)
                    for b in range(NJ):
                        pe.matmul(h_p[:, b, :], wr1[:, b * P:(b + 1) * P], xt[:, :], start=True,
                                  stop=True).then_inc(s_hp, 1)

                def step(q, s):
                    i = q * 2 + s
                    pe.wait_ge(s_hm, i + 2)
                    pe.wait_ge(s_msg, i + 1)
                    pe.nop(nofuse=True)
                    for u in range(TB):
                        for b in range(NJ):
                            ins = pe.matmul(m_p[:, s, u, 0:D], hm[:, s, b, u * P:(u + 1) * P],
                                            wr2[:, b * D:(b + 1) * D], start=(b == 0), stop=(b == NJ - 1))
                    ins.then_inc(s_mp, 1)
                    if exists(i + 1):
                        hidden(i + 1)
                    pe.wait_ge(s_msg, i + 2)
                    pe.wait_ge(s_rows, i + 1)
                    pe.nop(nofuse=True)
                    group_sums(pe, sum_p, same[:, s, :, :], [parts[:, :, k, :] for k in range(3)]).then_inc(s_sum, 1)
                    if exists(i + 2):
                        turn(q + 1, i + 2, s)

                pe.sem_inc(s_sum, 1)
                turn(0, 0, 0)
                hidden(0)
                turn(0, 1, 1)
                step(0, 0)
                step(0, 1)
                with pe.Fori(1, NB // 2 - 2) as q:
                    step(q, 0)
                    step(q, 1)
                for i in range(NB - 4, NB):
                    step(i // 2, i % 2)

            @block.vector
            def _(dve):
                STEPS = 4
                n = [0, 0]

                def chain(ins):
                    n[0] += 1
                    ins.then_inc(s_v, 1)
                    dve.wait_ge(s_v, n[1] + n[0])

                def matrices(qj, s):
                    j = qj * 2 + s
                    dve.wait_ge(s_key[s], qj * 16 + 16)
                    if later(j):
                        dve.wait_ge(s_sum, j)
                    for u in range(TB):
                        ins = dve.tensor_scalar(same[:, s, u, :], keys[:, s, u // 2, :],
                                                dst_f[:, bass.ds(j * TB + u, 1)], None, ALU.is_equal)
                    ins.then_inc(s_same, 1)

                def index(qj, s):
                    if later(qj):
                        dve.wait_ge(s_add[s], qj * 64)
                    dve.nop(nofuse=True)
                    dve.tensor_copy(sidx[:, s, :],
                                    own_rows[:, bass.ds((qj * 2 + s) * TB, TB)]).then_inc(s_si, 1)

                def masks(qj, s):
                    j = qj * 2 + s
                    dve.wait_ge(s_rel[s], qj * 16 + 16)
                    if later(j):
                        dve.wait_ge(s_mp, j)
                    for b in range(NJ):
                        dve.wait_ge(s_hr, j * NJ + (b + 1))
                        ins = dve.scalar_tensor_tensor(out=hm[:, s, b, :], in0=rel[:, s, :], scalar=relc[:, b:b + 1],
                                                       in1=hr[:, b, :], op0=ALU.is_equal, op1=ALU.mult)
                    ins.then_inc(s_hm, 1)

                def step(q, s):
                    i = q * 2 + s
                    front = exists(i + 1)
                    if front:
                        matrices(q + s, 1 - s)
                    dve.wait_ge(s_mp, i + 1)
                    dve.wait_ge(s_sum, i + 1)
                    for u in range(TB):
                        ins = dve.tensor_scalar(msg[:, u, :], m_p[:, s, u, 0:D], norm[:, bass.ds(i * TB + u, 1)],
                                                None, ALU.mult)
                    chain(ins)
                    chain(dve.tensor_copy(parts[:, :, 0, :], msg[:, :, :]))
                    chain(dve.tensor_tensor(rest[:, :, :], msg[:, :, :], parts[:, :, 0, :], ALU.subtract))
                    chain(dve.tensor_copy(parts[:, :, 1, :], rest[:, :, :]))
                    dve.tensor_tensor(parts[:, :, 2, :], rest[:, :, :], parts[:, :, 1, :],
                                      ALU.subtract).then_inc(s_msg, 1)
                    if front:
                        masks(q + s, 1 - s)
                        index(q + s, 1 - s)

                dve.sem_inc(s_msg, 1)
                matrices(0, 0)
                masks(0, 0)
                index(0, 0)
                step(0, 0)
                step(0, 1)
                first = n[0]
                with dve.Fori(1, NB // 2 - 2) as q:
                    n[:] = [first, (q - 1) * (2 * STEPS)]
                    step(q, 0)
                    step(q, 1)
                    assert n[0] == first + 2 * STEPS
                n[:] = [first, (NB // 2 - 3) * (2 * STEPS)]
                for i in range(NB - 4, NB):
                    step(i // 2, i % 2)
                for s in range(2):
                    dve.wait_ge(s_add[s], NB // 2 * 64)

        with ExitStack() as ph, nc.Block() as block:
            def tmp(name, shape, dt=F32):
                return ph.enter_context(nc.sbuf_tensor(name, shape, dt))

            xin = tmp("d3_x", [P, 2, CH, D])
            agg = tmp("d3_agg", [P, 2, CH, D])
            x = tmp("d3_sum", [P, 2, CH, D])
            sq = tmp("d3_sq", [P, 2, CH, D])
            stat = tmp("d3_stat", [P, 2, 3, CH])
            ln = Norm(x, sq, stat, 1)
            s_st = [sem(f"d3_stored{s}") for s in range(2)]
            s_used = sem("d3_inputs_used")
            s_res = sem("d3_result")
            s_v = sem("d3_chain")

            @block.sync
            def _(sp):
                stream(sp, [(x3_t, D, xin, s_used, 0), (agg3_t, D, agg, s_used, 0)], [(out, D, sq)], s_res, s_st)

            @block.scalar
            def _(act):
                def step(q, s):
                    c = q * 2 + s
                    if later(c):
                        ln.root(act, c - 1, 1 - s, 0)
                    ln.square(act, c, s, 0)

                chunks(act, step)
                ln.root(act, NC - 1, 1, 0)

            @block.vector
            def _(dve):
                n = [0, 0, 2 * 5]
                did, need = chain_of(dve, s_v, n)

                def finish(c, s):
                    ln.scale(dve, c, s, did, need, 0, sq).then_inc(s_res, 1)

                def step(q, s):
                    c = q * 2 + s
                    if later(q):
                        dve.wait_ge(s_res, c - 1)
                    dve.wait_ge(s_ld[s], loaded(3, q))
                    need(did(dve.scalar_tensor_tensor(
                        out=x[:, s, :, :].rearrange("p f d -> p (f d)"),
                        in0=agg[:, s, :, :].rearrange("p f d -> p (f d)"), scalar=0.0,
                        in1=xin[:, s, :, :].rearrange("p f d -> p (f d)"), op0=ALU.max, op1=ALU.add)))
                    dve.sem_inc(s_used, 1)
                    if later(c):
                        ln.variance(dve, c - 1, 1 - s, did, need, 0)
                    if later(q):
                        dve.wait_ge(s_st[s], q * 16)
                    ln.centre(dve, c, s, did, need, 0)
                    if later(c):
                        finish(c - 1, 1 - s)

                chunks(dve, step, n)
                ln.variance(dve, NC - 1, 1, did, need, 0)
                finish(NC - 1, 1)




def power_table(k):
    return 0 if k == 0 else 3 if k == 1 else 1 + k % 2


def arrange(inputs):
    get = {k: np.asarray(v) for k, v in inputs.items()}
    f32, i32 = np.float32, np.int32
    xz = np.zeros((NP, XW), i32)
    xz[:N, 0:D] = get["x"].view(i32)
    xz[:N, D] = get["node_vec"].view(i32)
    xz[:N, D + 1] = get["node_type_119"]
    kind = np.zeros(NP, i32)
    kind[:N] = get["node_type_119"]

    def edges(v, fill=0):
        full = np.zeros((EP,) + v.shape[1:], v.dtype)
        full[:E] = v
        if len(v.shape) == 1 and fill:
            full[E:] = fill
        return full.reshape((P, T) + v.shape[1:])

    def columns(v):
        return np.concatenate([v, np.zeros((P, TB), v.dtype)], 1)

    def by_step(v):
        return np.ascontiguousarray(v.T).reshape(NB, TB * P)

    src = edges(get["src"].astype(i32), SPARE_SRC)
    dst = edges(get["dst"].astype(i32), SPARE_DST)
    ea = edges(get["edge_attr_40"])
    rel = edges(get["edge_type_8"].astype(i32))
    w2 = get["L2_gnn_W"]
    wl2 = np.zeros((2 * D + 1, 2 * D), f32)
    wl2[:D, :D] = w2.T
    wl2[D:2 * D, D:] = w2.T
    wl2[2 * D] = np.tile(get["L2_gnn_b"], 2)
    wr1, wr2, br1 = get["L3_gnn_weight1"], get["L3_gnn_weight2"], get["L3_gnn_bias1"]
    return {
        "xz": xz, "kind": kind[:, None],
        "src": columns(src), "dst": columns(dst), "src_rows": by_step(src), "dst_rows": by_step(dst),
        "rel_rows": by_step(rel),
        "ea": np.ascontiguousarray(ea.transpose(2, 1, 0)).reshape(R, T * P),
        "dist": edges(get["edge_weight"]), "norm": edges(get["edge_weight1"][:, 0]),
        "w1t": np.ascontiguousarray(get["L0_gnn_W1"].T), "b1": get["L0_gnn_b1"][:, None],
        "w2b": np.concatenate([get["L0_gnn_W2"].T, get["L0_gnn_b2"][None]], 0),
        "embt": np.ascontiguousarray(get["L0_gnn_emb"].T), "adwt": np.ascontiguousarray(get["L0_gnn_adaptW"].T),
        "gamma": get["L0_gnn_gamma"][None], "beta": get["L0_gnn_beta"][None],
        "jacobi": np.ascontiguousarray(jacobi_basis().T).reshape(1, -1),
        "lap": get["L1_gnn_lap_coefs"][None], "mf": get["L1_gnn_mf_weights"].reshape(1, -1),
        "wl2": wl2,
        "wr1": np.ascontiguousarray(wr1.transpose(1, 0, 2)).reshape(D, NREL * D),
        "br1": np.ascontiguousarray(np.tile(br1, NREL).reshape(3, P).T),
        "wr2": np.ascontiguousarray(wr2.reshape(3, P, D).transpose(1, 0, 2)).reshape(P, 3 * D),
        "relc": np.ascontiguousarray((np.arange(NREL * D) // D).astype(f32).reshape(3, P).T),
        "level": np.array([[v * NP for k in range(K) for v in (power_table(k), power_table(k + 1))]
                           + [float(k > 0) for k in range(K)]], f32),
        "b3": get["L3_gnn_bias2"][None],
    }


def kernel(**inputs):
    import concourse.bacc as bacc
    from concourse.bass_utils import run_bass_kernel_spmd

    nc = bacc.Bacc("TRN2", target_bir_lowering=False, num_devices=1)
    arrays = {"in_" + k: np.ascontiguousarray(v) for k, v in arrange(inputs).items()}
    a = {k[3:]: nc.dram_tensor(k, v.shape, mybir.dt.from_np(v.dtype), kind="ExternalInput").ap()
         for k, v in arrays.items()}
    out = nc.dram_tensor("out", (NP, D), F32, kind="ExternalOutput").ap()
    program(nc, a, out)
    r = run_bass_kernel_spmd(nc, [arrays], core_ids=[0])
    return r.results[0]["out"][:N]
```
